# Optimizing a Trainium2 kernel written in Bass

```python
import numpy as np
import jax
import jax.numpy as jnp

def _softmax(x, axis=-1):
    return jax.nn.softmax(x, axis=axis)

def _gelu(x):
    return jax.nn.gelu(x, approximate=True)

def _silu(x):
    return jax.nn.silu(x)

def _sigmoid(x):
    return jax.nn.sigmoid(x)

def _layernorm(x, axis=-1, eps=1e-05):
    m = jnp.mean(x, axis=axis, keepdims=True)
    v = jnp.var(x, axis=axis, keepdims=True)
    return (x - m) / jnp.sqrt(v + eps)

def _scatter_add(tgt, idx, src, axis=0):
    return tgt.at[idx].add(src)

def _segment_sum(src, seg, n):
    return jax.ops.segment_sum(src, seg, n)
kernel_name = 'mk_xattn_seq_d4_seqx_r8_6cdaa5'

def setup_inputs(seed: int=0):
    np.random.seed(seed)
    _w = jnp.asarray

    def _rec_inputs():
        import jax
        import jax.numpy as jnp
        _rk = jax.random.key(seed)
        x = -0.0002928 + 1 * jax.random.normal(jax.random.fold_in(_rk, 1), (64, 64, 256), jnp.float32)
        _lenS = 64 - jax.random.randint(jax.random.fold_in(_rk, 7), (64,), 0, max(1, 64 // 4) + 1, jnp.int32)
        _lenS2 = 64 - jax.random.randint(jax.random.fold_in(_rk, 8), (64,), 0, max(1, 64 // 4) + 1, jnp.int32)
        _ctx_2048P = jax.random.normal(jax.random.fold_in(_rk, 11), (64, 16, 256), jnp.float32)
        _ctx_2048c = jax.random.dirichlet(jax.random.fold_in(_rk, 511), 0.3 * jnp.ones((16,), jnp.float32), (64, 64))
        _ctx_2048t = jnp.einsum('bsk,bkd->bsd', _ctx_2048c, _ctx_2048P)
        _ctx_2048t = _ctx_2048t * jax.lax.rsqrt(jnp.mean(jnp.square(_ctx_2048t)) + 1e-12) * 0.953939
        ctx_2048 = -1.39393e-06 + 0.999914 * (_ctx_2048t + 0.3 * jax.random.normal(jax.random.fold_in(_rk, 611), (64, 64, 256), jnp.float32))
        _validS = jnp.arange(64)[None, :] < _lenS[:, None]
        _validS2 = jnp.arange(64)[None, :] < _lenS2[:, None]
        _causal = jnp.tril(jnp.ones((64, 64), dtype=bool))
        mask_1x1xSxS2_fc1 = jnp.where(jnp.broadcast_to(_validS2[0:1, None, None, :], (1, 1, 64, 64)), 1.0, 0.0).astype(jnp.float32)
        mask_Bx1xSxS2_ff1 = jnp.where(jnp.ones((64, 1, 64, 64), dtype=bool), 1.0, 0.0).astype(jnp.float32)
        return (x, ctx_2048, mask_1x1xSxS2_fc1, mask_Bx1xSxS2_ff1)
    x, ctx_2048, mask_1x1xSxS2_fc1, mask_Bx1xSxS2_ff1 = _rec_inputs()

    def _L0_xattn_setup():
        import jax, jax.numpy as jnp
        import numpy as np
        N, C, S, S2, H, CTX = (4, 64, 256, 256, 8, 64)
        EPS = 1e-05
        key = jax.random.key(seed)
        ks = jax.random.split(key, 6)
        sd = lambda fan: 1.0 / np.sqrt(fan)
        return {'input': jax.random.normal(ks[0], (N, C, S), jnp.float32), 'context': jax.random.normal(ks[1], (N, CTX, S2), jnp.float32), 'gamma': jnp.ones((C,), jnp.float32), 'beta': jnp.zeros((C,), jnp.float32), 'Wq': jax.random.normal(ks[2], (C * H, C), jnp.float32) * sd(C), 'bq': jnp.zeros((C * H,), jnp.float32), 'Wkv': jax.random.normal(ks[3], (C * H * 2, CTX), jnp.float32) * sd(CTX), 'bkv': jnp.zeros((C * H * 2,), jnp.float32), 'Wo': jax.random.normal(ks[4], (C, C * H), jnp.float32) * sd(C * H), 'bo': jnp.zeros((C,), jnp.float32)}
    _L0_xattn_all = _L0_xattn_setup()
    _L0_xattn_in = {k: v for k, v in _L0_xattn_all.items() if k in ('gamma', 'beta', 'Wq', 'bq', 'Wkv', 'bkv', 'Wo', 'bo')}
    del _L0_xattn_all

    def _L1_xattn_setup():
        import jax, jax.numpy as jnp
        import numpy as np
        N_HEAD = 32
        EPS = 1e-05

        def _ln(x, w, b):
            m = jnp.mean(x, axis=-1, keepdims=True)
            v = jnp.mean((x - m) ** 2, axis=-1, keepdims=True)
            return (x - m) * jax.lax.rsqrt(v + EPS) * w + b

        def _forward(x, state, i, ln1_w, ln1_b, ln2_w, ln2_b, maa_x, maa_w, maa_k, maa_v, maa_r, maa_g, maa_w1, maa_w2, time_decay, decay_w1, decay_w2, faaaa, Wr, Wk, Wv, Wg, Wo, gn_w, gn_b, fmaa_k, fmaa_r, fWk, fWr, fWv):
            B, L, C = x.shape
            H = N_HEAD
            S = C // H
            i0 = (2 + S) * i
            xa = _ln(x, ln1_w, ln1_b)
            sx = jnp.concatenate([state[:, i0 + 1][:, None], xa[:, :-1]], axis=1) - xa
            xxx = xa + sx * maa_x
            t = jnp.tanh(xxx @ maa_w1).reshape(B, L, 5, -1)
            m = jnp.einsum('blfd,fdc->blfc', t, maa_w2)
            mw, mk, mv, mr, mg = (m[:, :, j] for j in range(5))
            xw = xa + sx * (maa_w + mw)
            xk = xa + sx * (maa_k + mk)
            xv = xa + sx * (maa_v + mv)
            xr = xa + sx * (maa_r + mr)
            xg = xa + sx * (maa_g + mg)
            w = time_decay + jnp.tanh(xw @ decay_w1) @ decay_w2
            w = jnp.exp(-jnp.exp(w)).reshape(B, L, H, S)
            r = (xr @ Wr.T).reshape(B, L, H, S)
            k = (xk @ Wk.T).reshape(B, L, H, S)
            v = (xv @ Wv.T).reshape(B, L, H, S)
            g = jax.nn.silu(xg @ Wg.T)
            s0 = state[:, i0 + 2:i0 + 2 + S].reshape(B, H, S, S)

            def step(s, inp):
                k_l, v_l, w_l, r_l = inp
                a = k_l[..., :, None] * v_l[..., None, :]
                out = jnp.einsum('bhs,bhst->bht', r_l, faaaa * a + s)
                s_new = a + w_l[..., None] * s
                return (s_new, out)
            seq = tuple((z.transpose(1, 0, 2, 3) for z in (k, v, w, r)))
            _, outs = jax.lax.scan(step, s0, seq)
            y = outs.transpose(1, 0, 2, 3)
            gm = jnp.mean(y, axis=-1, keepdims=True)
            gv = jnp.mean((y - gm) ** 2, axis=-1, keepdims=True)
            y = ((y - gm) * jax.lax.rsqrt(gv + EPS)).reshape(B, L, C) * gn_w + gn_b
            x = x + y * g @ Wo.T
            xc = _ln(x, ln2_w, ln2_b)
            sxc = jnp.concatenate([state[:, i0][:, None], xc[:, :-1]], axis=1) - xc
            xk2 = xc + sxc * fmaa_k
            xr2 = xc + sxc * fmaa_r
            rr = jax.nn.sigmoid(xr2 @ fWr.T)
            kk = jnp.square(jax.nn.relu(xk2 @ fWk.T))
            x = x + rr * (kk @ fWv.T)
            return x
        key = jax.random.key(seed)
        B, L, C, H = (8, 64, 256, N_HEAD)
        S = C // H
        DM, DD = (32, 64)
        ks = jax.random.split(key, 32)
        n = lambda k, shp, s=1.0: jax.random.normal(k, shp, dtype=jnp.float32) * s
        u = lambda k, shp: jax.random.uniform(k, shp, dtype=jnp.float32)
        inp = {'x': n(ks[0], (B, L, C)), 'state': n(ks[1], (B, 2 + S, C), 0.1), 'i': 0, 'ln1_w': jnp.ones((C,), jnp.float32), 'ln1_b': jnp.zeros((C,), jnp.float32), 'ln2_w': jnp.ones((C,), jnp.float32), 'ln2_b': jnp.zeros((C,), jnp.float32), 'maa_x': u(ks[2], (C,)), 'maa_w': u(ks[3], (C,)), 'maa_k': u(ks[4], (C,)), 'maa_v': u(ks[5], (C,)), 'maa_r': u(ks[6], (C,)), 'maa_g': u(ks[7], (C,)), 'maa_w1': n(ks[8], (C, 5 * DM), 0.02), 'maa_w2': n(ks[9], (5, DM, C), 0.02), 'time_decay': n(ks[10], (C,), 0.5), 'decay_w1': n(ks[11], (C, DD), 0.02), 'decay_w2': n(ks[12], (DD, C), 0.02), 'faaaa': n(ks[13], (H, S, 1), 0.1), 'Wr': n(ks[14], (C, C), 0.02), 'Wk': n(ks[15], (C, C), 0.02), 'Wv': n(ks[16], (C, C), 0.02), 'Wg': n(ks[17], (C, C), 0.02), 'Wo': n(ks[18], (C, C), 0.02), 'gn_w': jnp.ones((C,), jnp.float32), 'gn_b': jnp.zeros((C,), jnp.float32), 'fmaa_k': u(ks[19], (C,)), 'fmaa_r': u(ks[20], (C,)), 'fWk': n(ks[21], (C, C), 0.02), 'fWr': n(ks[22], (C, C), 0.02), 'fWv': n(ks[23], (C, C), 0.02)}
        return inp
    _L1_xattn_all = _L1_xattn_setup()
    _L1_xattn_in = {k: v for k, v in _L1_xattn_all.items() if k in ('ln1_w', 'ln1_b', 'ln2_w', 'ln2_b', 'maa_x', 'maa_w', 'maa_k', 'maa_v', 'maa_r', 'maa_g', 'maa_w1', 'maa_w2', 'time_decay', 'decay_w1', 'decay_w2', 'faaaa', 'Wr', 'Wk', 'Wv', 'Wg', 'Wo', 'gn_w', 'gn_b', 'fmaa_k', 'fmaa_r', 'fWk', 'fWr', 'fWv')}
    del _L1_xattn_all

    def _L2_xattn_setup():
        import jax, jax.numpy as jnp
        import numpy as np
        H = 256
        NH = 16
        HD = H // NH
        EPS = 1e-05

        def gelu(x):
            return 0.5 * x * (1.0 + jnp.tanh(0.7978845608028654 * x * (1.0 + 0.044715 * x * x)))

        def layernorm(x, scale, bias):
            m = jnp.mean(x, axis=-1, keepdims=True)
            v = jnp.mean(jnp.square(x - m), axis=-1, keepdims=True)
            return (x - m) * jax.lax.rsqrt(v + EPS) * scale + bias

        def split_heads(x):
            b, s, _ = x.shape
            return x.reshape(b, s, NH, HD).transpose(0, 2, 1, 3)

        def merge_heads(x):
            b, nh, s, hd = x.shape
            return x.transpose(0, 2, 1, 3).reshape(b, s, nh * hd)

        def attention(q, k, v, mask):
            scores = jnp.einsum('bhqd,bhkd->bhqk', q, k) / jnp.sqrt(jnp.float32(HD))
            scores = scores * mask - 10000.0 * (1.0 - mask)
            probs = jax.nn.softmax(scores, axis=-1)
            return jnp.einsum('bhqk,bhkd->bhqd', probs, v)
        key = jax.random.key(seed)
        ks = jax.random.split(key, 16)
        b, s, t = (2, 128, 128)
        w = lambda k, i, o: jax.random.normal(k, (i, o), jnp.float32) * 0.02
        inp = {'hidden_states': jax.random.normal(ks[0], (b, s, H), jnp.float32), 'encoder_states': jax.random.normal(ks[1], (b, t, H), jnp.float32), 'ltor_mask': jnp.tril(jnp.ones((1, 1, s, s), jnp.float32)), 'cross_mask': jnp.ones((b, 1, s, t), jnp.float32), 'ln1_s': jnp.ones((H,), jnp.float32), 'ln1_b': jnp.zeros((H,), jnp.float32), 'w_qkv': w(ks[2], H, 3 * H), 'b_qkv': jnp.zeros((3 * H,), jnp.float32), 'w_ao': w(ks[3], H, H), 'b_ao': jnp.zeros((H,), jnp.float32), 'ln2_s': jnp.ones((H,), jnp.float32), 'ln2_b': jnp.zeros((H,), jnp.float32), 'w_q': w(ks[4], H, H), 'b_q': jnp.zeros((H,), jnp.float32), 'w_kv': w(ks[5], H, 2 * H), 'b_kv': jnp.zeros((2 * H,), jnp.float32), 'w_co': w(ks[6], H, H), 'b_co': jnp.zeros((H,), jnp.float32), 'ln3_s': jnp.ones((H,), jnp.float32), 'ln3_b': jnp.zeros((H,), jnp.float32), 'w1': w(ks[7], H, 4 * H), 'b1': jnp.zeros((4 * H,), jnp.float32), 'w2': w(ks[8], 4 * H, H), 'b2': jnp.zeros((H,), jnp.float32)}
        return inp
    _L2_xattn_all = _L2_xattn_setup()
    _L2_xattn_in = {k: v for k, v in _L2_xattn_all.items() if k in ('ln1_s', 'ln1_b', 'w_qkv', 'b_qkv', 'w_ao', 'b_ao', 'ln2_s', 'ln2_b', 'w_q', 'b_q', 'w_kv', 'b_kv', 'w_co', 'b_co', 'ln3_s', 'ln3_b', 'w1', 'b1', 'w2', 'b2')}
    del _L2_xattn_all

    def _L3_xattn_setup():
        import jax, jax.numpy as jnp
        import numpy as np
        H = 256
        B, L, S = (4, 512, 10)
        key = jax.random.key(seed)
        k1, k2, k3, k4, k5, k6 = jax.random.split(key, 6)
        scale = 1.0 / np.sqrt(H)
        return {'h_english': jax.random.normal(k1, (B, L, H), dtype=jnp.float32), 'h_lojban': jax.random.normal(k2, (B, S, H), dtype=jnp.float32), 'w_q': jax.random.normal(k3, (H, H), dtype=jnp.float32) * scale, 'w_k': jax.random.normal(k4, (H, H), dtype=jnp.float32) * scale, 'w_v': jax.random.normal(k5, (H, H), dtype=jnp.float32) * scale, 'w_o': jax.random.normal(k6, (H, H), dtype=jnp.float32) * scale, 'alpha': jnp.float32(0.1)}
    _L3_xattn_all = _L3_xattn_setup()
    _L3_xattn_in = {k: v for k, v in _L3_xattn_all.items() if k in ('w_q', 'w_k', 'w_v', 'w_o', 'alpha')}
    del _L3_xattn_all
    return {'x': x, 'ctx_2048': ctx_2048, 'mask_1x1xSxS2_fc1': mask_1x1xSxS2_fc1, 'mask_Bx1xSxS2_ff1': mask_Bx1xSxS2_ff1, 'L0_xattn_gamma': _L0_xattn_in['gamma'], 'L0_xattn_beta': _L0_xattn_in['beta'], 'L0_xattn_Wq': _L0_xattn_in['Wq'], 'L0_xattn_bq': _L0_xattn_in['bq'], 'L0_xattn_Wkv': _L0_xattn_in['Wkv'], 'L0_xattn_bkv': _L0_xattn_in['bkv'], 'L0_xattn_Wo': _L0_xattn_in['Wo'], 'L0_xattn_bo': _L0_xattn_in['bo'], 'L1_xattn_ln1_w': _L1_xattn_in['ln1_w'], 'L1_xattn_ln1_b': _L1_xattn_in['ln1_b'], 'L1_xattn_ln2_w': _L1_xattn_in['ln2_w'], 'L1_xattn_ln2_b': _L1_xattn_in['ln2_b'], 'L1_xattn_maa_x': _L1_xattn_in['maa_x'], 'L1_xattn_maa_w': _L1_xattn_in['maa_w'], 'L1_xattn_maa_k': _L1_xattn_in['maa_k'], 'L1_xattn_maa_v': _L1_xattn_in['maa_v'], 'L1_xattn_maa_r': _L1_xattn_in['maa_r'], 'L1_xattn_maa_g': _L1_xattn_in['maa_g'], 'L1_xattn_maa_w1': _L1_xattn_in['maa_w1'], 'L1_xattn_maa_w2': _L1_xattn_in['maa_w2'], 'L1_xattn_time_decay': _L1_xattn_in['time_decay'], 'L1_xattn_decay_w1': _L1_xattn_in['decay_w1'], 'L1_xattn_decay_w2': _L1_xattn_in['decay_w2'], 'L1_xattn_faaaa': _L1_xattn_in['faaaa'], 'L1_xattn_Wr': _L1_xattn_in['Wr'], 'L1_xattn_Wk': _L1_xattn_in['Wk'], 'L1_xattn_Wv': _L1_xattn_in['Wv'], 'L1_xattn_Wg': _L1_xattn_in['Wg'], 'L1_xattn_Wo': _L1_xattn_in['Wo'], 'L1_xattn_gn_w': _L1_xattn_in['gn_w'], 'L1_xattn_gn_b': _L1_xattn_in['gn_b'], 'L1_xattn_fmaa_k': _L1_xattn_in['fmaa_k'], 'L1_xattn_fmaa_r': _L1_xattn_in['fmaa_r'], 'L1_xattn_fWk': _L1_xattn_in['fWk'], 'L1_xattn_fWr': _L1_xattn_in['fWr'], 'L1_xattn_fWv': _L1_xattn_in['fWv'], 'L2_xattn_ln1_s': _L2_xattn_in['ln1_s'], 'L2_xattn_ln1_b': _L2_xattn_in['ln1_b'], 'L2_xattn_w_qkv': _L2_xattn_in['w_qkv'], 'L2_xattn_b_qkv': _L2_xattn_in['b_qkv'], 'L2_xattn_w_ao': _L2_xattn_in['w_ao'], 'L2_xattn_b_ao': _L2_xattn_in['b_ao'], 'L2_xattn_ln2_s': _L2_xattn_in['ln2_s'], 'L2_xattn_ln2_b': _L2_xattn_in['ln2_b'], 'L2_xattn_w_q': _L2_xattn_in['w_q'], 'L2_xattn_b_q': _L2_xattn_in['b_q'], 'L2_xattn_w_kv': _L2_xattn_in['w_kv'], 'L2_xattn_b_kv': _L2_xattn_in['b_kv'], 'L2_xattn_w_co': _L2_xattn_in['w_co'], 'L2_xattn_b_co': _L2_xattn_in['b_co'], 'L2_xattn_ln3_s': _L2_xattn_in['ln3_s'], 'L2_xattn_ln3_b': _L2_xattn_in['ln3_b'], 'L2_xattn_w1': _L2_xattn_in['w1'], 'L2_xattn_b1': _L2_xattn_in['b1'], 'L2_xattn_w2': _L2_xattn_in['w2'], 'L2_xattn_b2': _L2_xattn_in['b2'], 'L3_xattn_w_q': _L3_xattn_in['w_q'], 'L3_xattn_w_k': _L3_xattn_in['w_k'], 'L3_xattn_w_v': _L3_xattn_in['w_v'], 'L3_xattn_w_o': _L3_xattn_in['w_o'], 'L3_xattn_alpha': _L3_xattn_in['alpha']}

def reference(x, ctx_2048, mask_1x1xSxS2_fc1, mask_Bx1xSxS2_ff1, L0_xattn_gamma, L0_xattn_beta, L0_xattn_Wq, L0_xattn_bq, L0_xattn_Wkv, L0_xattn_bkv, L0_xattn_Wo, L0_xattn_bo, L1_xattn_ln1_w, L1_xattn_ln1_b, L1_xattn_ln2_w, L1_xattn_ln2_b, L1_xattn_maa_x, L1_xattn_maa_w, L1_xattn_maa_k, L1_xattn_maa_v, L1_xattn_maa_r, L1_xattn_maa_g, L1_xattn_maa_w1, L1_xattn_maa_w2, L1_xattn_time_decay, L1_xattn_decay_w1, L1_xattn_decay_w2, L1_xattn_faaaa, L1_xattn_Wr, L1_xattn_Wk, L1_xattn_Wv, L1_xattn_Wg, L1_xattn_Wo, L1_xattn_gn_w, L1_xattn_gn_b, L1_xattn_fmaa_k, L1_xattn_fmaa_r, L1_xattn_fWk, L1_xattn_fWr, L1_xattn_fWv, L2_xattn_ln1_s, L2_xattn_ln1_b, L2_xattn_w_qkv, L2_xattn_b_qkv, L2_xattn_w_ao, L2_xattn_b_ao, L2_xattn_ln2_s, L2_xattn_ln2_b, L2_xattn_w_q, L2_xattn_b_q, L2_xattn_w_kv, L2_xattn_b_kv, L2_xattn_w_co, L2_xattn_b_co, L2_xattn_ln3_s, L2_xattn_ln3_b, L2_xattn_w1, L2_xattn_b1, L2_xattn_w2, L2_xattn_b2, L3_xattn_w_q, L3_xattn_w_k, L3_xattn_w_v, L3_xattn_w_o, L3_xattn_alpha):
    import jax
    import jax.numpy as jnp

    def _L0_xattn_ref(input, context, gamma, beta, Wq, bq, Wkv, bkv, Wo, bo):
        import jax, jax.numpy as jnp
        import numpy as np
        N, C, S, S2, H, CTX = (4, 64, 256, 256, 8, 64)
        EPS = 1e-05
        n, c, s = input.shape
        h = H
        mu = jnp.mean(input, axis=(1, 2), keepdims=True)
        var = jnp.var(input, axis=(1, 2), keepdims=True)
        xn = (input - mu) * jax.lax.rsqrt(var + EPS)
        xn = xn * gamma[None, :, None] + beta[None, :, None]
        q = jnp.einsum('oc,ncs->nos', Wq, xn) + bq[None, :, None]
        kv = jnp.einsum('od,nds->nos', Wkv, context) + bkv[None, :, None]
        q = q.reshape(n, h, c, s).transpose(0, 1, 3, 2)
        kv = kv.reshape(n, 2 * h, c, -1).transpose(0, 1, 3, 2)
        k, v = (kv[:, :h], kv[:, h:])
        scale = c ** (-0.25)
        att = jax.nn.softmax(jnp.einsum('nhqc,nhkc->nhqk', q * scale, k * scale), axis=-1)
        y = jnp.einsum('nhqk,nhkc->nhqc', att, v)
        y = y.transpose(0, 1, 3, 2).reshape(n, h * c, s)
        out = jnp.einsum('co,nos->ncs', Wo, y) + bo[None, :, None]
        return input + out

    def _L1_xattn_ref(x, state, i, ln1_w, ln1_b, ln2_w, ln2_b, maa_x, maa_w, maa_k, maa_v, maa_r, maa_g, maa_w1, maa_w2, time_decay, decay_w1, decay_w2, faaaa, Wr, Wk, Wv, Wg, Wo, gn_w, gn_b, fmaa_k, fmaa_r, fWk, fWr, fWv):
        import jax, jax.numpy as jnp
        import numpy as np
        N_HEAD = 32
        EPS = 1e-05

        def _ln(x, w, b):
            m = jnp.mean(x, axis=-1, keepdims=True)
            v = jnp.mean((x - m) ** 2, axis=-1, keepdims=True)
            return (x - m) * jax.lax.rsqrt(v + EPS) * w + b

        def _forward(x, state, i, ln1_w, ln1_b, ln2_w, ln2_b, maa_x, maa_w, maa_k, maa_v, maa_r, maa_g, maa_w1, maa_w2, time_decay, decay_w1, decay_w2, faaaa, Wr, Wk, Wv, Wg, Wo, gn_w, gn_b, fmaa_k, fmaa_r, fWk, fWr, fWv):
            B, L, C = x.shape
            H = N_HEAD
            S = C // H
            i0 = (2 + S) * i
            xa = _ln(x, ln1_w, ln1_b)
            sx = jnp.concatenate([state[:, i0 + 1][:, None], xa[:, :-1]], axis=1) - xa
            xxx = xa + sx * maa_x
            t = jnp.tanh(xxx @ maa_w1).reshape(B, L, 5, -1)
            m = jnp.einsum('blfd,fdc->blfc', t, maa_w2)
            mw, mk, mv, mr, mg = (m[:, :, j] for j in range(5))
            xw = xa + sx * (maa_w + mw)
            xk = xa + sx * (maa_k + mk)
            xv = xa + sx * (maa_v + mv)
            xr = xa + sx * (maa_r + mr)
            xg = xa + sx * (maa_g + mg)
            w = time_decay + jnp.tanh(xw @ decay_w1) @ decay_w2
            w = jnp.exp(-jnp.exp(w)).reshape(B, L, H, S)
            r = (xr @ Wr.T).reshape(B, L, H, S)
            k = (xk @ Wk.T).reshape(B, L, H, S)
            v = (xv @ Wv.T).reshape(B, L, H, S)
            g = jax.nn.silu(xg @ Wg.T)
            s0 = state[:, i0 + 2:i0 + 2 + S].reshape(B, H, S, S)

            def step(s, inp):
                k_l, v_l, w_l, r_l = inp
                a = k_l[..., :, None] * v_l[..., None, :]
                out = jnp.einsum('bhs,bhst->bht', r_l, faaaa * a + s)
                s_new = a + w_l[..., None] * s
                return (s_new, out)
            seq = tuple((z.transpose(1, 0, 2, 3) for z in (k, v, w, r)))
            _, outs = jax.lax.scan(step, s0, seq)
            y = outs.transpose(1, 0, 2, 3)
            gm = jnp.mean(y, axis=-1, keepdims=True)
            gv = jnp.mean((y - gm) ** 2, axis=-1, keepdims=True)
            y = ((y - gm) * jax.lax.rsqrt(gv + EPS)).reshape(B, L, C) * gn_w + gn_b
            x = x + y * g @ Wo.T
            xc = _ln(x, ln2_w, ln2_b)
            sxc = jnp.concatenate([state[:, i0][:, None], xc[:, :-1]], axis=1) - xc
            xk2 = xc + sxc * fmaa_k
            xr2 = xc + sxc * fmaa_r
            rr = jax.nn.sigmoid(xr2 @ fWr.T)
            kk = jnp.square(jax.nn.relu(xk2 @ fWk.T))
            x = x + rr * (kk @ fWv.T)
            return x
        return _forward(x, state, i, ln1_w, ln1_b, ln2_w, ln2_b, maa_x, maa_w, maa_k, maa_v, maa_r, maa_g, maa_w1, maa_w2, time_decay, decay_w1, decay_w2, faaaa, Wr, Wk, Wv, Wg, Wo, gn_w, gn_b, fmaa_k, fmaa_r, fWk, fWr, fWv)

    def _L2_xattn_ref(hidden_states, encoder_states, ltor_mask, cross_mask, ln1_s, ln1_b, w_qkv, b_qkv, w_ao, b_ao, ln2_s, ln2_b, w_q, b_q, w_kv, b_kv, w_co, b_co, ln3_s, ln3_b, w1, b1, w2, b2):
        import jax, jax.numpy as jnp
        import numpy as np
        H = 256
        NH = 16
        HD = H // NH
        EPS = 1e-05

        def gelu(x):
            return 0.5 * x * (1.0 + jnp.tanh(0.7978845608028654 * x * (1.0 + 0.044715 * x * x)))

        def layernorm(x, scale, bias):
            m = jnp.mean(x, axis=-1, keepdims=True)
            v = jnp.mean(jnp.square(x - m), axis=-1, keepdims=True)
            return (x - m) * jax.lax.rsqrt(v + EPS) * scale + bias

        def split_heads(x):
            b, s, _ = x.shape
            return x.reshape(b, s, NH, HD).transpose(0, 2, 1, 3)

        def merge_heads(x):
            b, nh, s, hd = x.shape
            return x.transpose(0, 2, 1, 3).reshape(b, s, nh * hd)

        def attention(q, k, v, mask):
            scores = jnp.einsum('bhqd,bhkd->bhqk', q, k) / jnp.sqrt(jnp.float32(HD))
            scores = scores * mask - 10000.0 * (1.0 - mask)
            probs = jax.nn.softmax(scores, axis=-1)
            return jnp.einsum('bhqk,bhkd->bhqd', probs, v)
        ln_out = layernorm(hidden_states, ln1_s, ln1_b)
        qkv = ln_out @ w_qkv + b_qkv
        q, k, v = jnp.split(qkv, 3, axis=-1)
        ctx = merge_heads(attention(split_heads(q), split_heads(k), split_heads(v), ltor_mask))
        attn_out = ctx @ w_ao + b_ao
        x = hidden_states + attn_out
        ln_out = layernorm(x, ln2_s, ln2_b)
        q = ln_out @ w_q + b_q
        kv = encoder_states @ w_kv + b_kv
        k, v = jnp.split(kv, 2, axis=-1)
        ctx = merge_heads(attention(split_heads(q), split_heads(k), split_heads(v), cross_mask))
        cross_out = ctx @ w_co + b_co
        x = x + cross_out
        ln_out = layernorm(x, ln3_s, ln3_b)
        mlp_out = gelu(ln_out @ w1 + b1) @ w2 + b2
        return x + mlp_out

    def _L3_xattn_ref(h_english, h_lojban, w_q, w_k, w_v, w_o, alpha):
        import jax, jax.numpy as jnp
        import numpy as np
        H = 256
        B, L, S = (4, 512, 10)
        h = h_english.shape[-1]
        q = jnp.einsum('blh,oh->blo', h_english, w_q)
        k = jnp.einsum('bsh,oh->bso', h_lojban, w_k)
        v = jnp.einsum('bsh,oh->bso', h_lojban, w_v)
        scores = jnp.einsum('blh,bsh->bls', q, k) / jnp.sqrt(jnp.float32(h))
        probs = jax.nn.softmax(scores, axis=-1)
        context = jnp.einsum('bls,bsh->blh', probs, v)
        delta = jnp.einsum('blh,oh->blo', context, w_o)
        return h_english + alpha * delta
    x = _L0_xattn_ref(x, ctx_2048, L0_xattn_gamma, L0_xattn_beta, L0_xattn_Wq, L0_xattn_bq, L0_xattn_Wkv, L0_xattn_bkv, L0_xattn_Wo, L0_xattn_bo)
    x = _L1_xattn_ref(x, ctx_2048, 0, L1_xattn_ln1_w, L1_xattn_ln1_b, L1_xattn_ln2_w, L1_xattn_ln2_b, L1_xattn_maa_x, L1_xattn_maa_w, L1_xattn_maa_k, L1_xattn_maa_v, L1_xattn_maa_r, L1_xattn_maa_g, L1_xattn_maa_w1, L1_xattn_maa_w2, L1_xattn_time_decay, L1_xattn_decay_w1, L1_xattn_decay_w2, L1_xattn_faaaa, L1_xattn_Wr, L1_xattn_Wk, L1_xattn_Wv, L1_xattn_Wg, L1_xattn_Wo, L1_xattn_gn_w, L1_xattn_gn_b, L1_xattn_fmaa_k, L1_xattn_fmaa_r, L1_xattn_fWk, L1_xattn_fWr, L1_xattn_fWv)
    x = _L2_xattn_ref(x, ctx_2048, mask_1x1xSxS2_fc1, mask_Bx1xSxS2_ff1, L2_xattn_ln1_s, L2_xattn_ln1_b, L2_xattn_w_qkv, L2_xattn_b_qkv, L2_xattn_w_ao, L2_xattn_b_ao, L2_xattn_ln2_s, L2_xattn_ln2_b, L2_xattn_w_q, L2_xattn_b_q, L2_xattn_w_kv, L2_xattn_b_kv, L2_xattn_w_co, L2_xattn_b_co, L2_xattn_ln3_s, L2_xattn_ln3_b, L2_xattn_w1, L2_xattn_b1, L2_xattn_w2, L2_xattn_b2)
    x = _L3_xattn_ref(x, ctx_2048, L3_xattn_w_q, L3_xattn_w_k, L3_xattn_w_v, L3_xattn_w_o, L3_xattn_alpha)
    return x

_drawn_inputs = setup_inputs


def setup_inputs(seed=0):
    import zlib

    import numpy as np

    out = dict(_drawn_inputs(seed))
    spreads = {'L0_xattn_gamma': (1.0, 0.2),
     'L0_xattn_beta': (0.0, 0.1),
     'L0_xattn_bq': (0.0, 0.1),
     'L0_xattn_bkv': (0.0, 2.0),
     'L0_xattn_bo': (0.0, 2.0),
     'L1_xattn_ln1_w': (1.0, 0.6),
     'L1_xattn_ln1_b': (0.0, 0.615),
     'L1_xattn_ln2_w': (1.0, 0.6),
     'L1_xattn_ln2_b': (0.0, 0.8),
     'L1_xattn_gn_w': (1.0, 0.6),
     'L1_xattn_gn_b': (0.0, 0.8),
     'L2_xattn_ln1_s': (1.0, 0.6),
     'L2_xattn_ln1_b': (0.0, 2.0),
     'L2_xattn_b_qkv': (0.0, 2.0),
     'L2_xattn_b_ao': (0.0, 2.0),
     'L2_xattn_ln2_s': (1.0, 0.6),
     'L2_xattn_ln2_b': (0.0, 2.0),
     'L2_xattn_b_q': (0.0, 2.0),
     'L2_xattn_b_kv': (0.0, 2.0),
     'L2_xattn_b_co': (0.0, 2.0),
     'L2_xattn_ln3_s': (1.0, 0.6),
     'L2_xattn_ln3_b': (0.0, 2.0),
     'L2_xattn_b1': (0.0, 2.0),
     'L2_xattn_b2': (0.0, 2.0)}
    factors = {'L1_xattn_maa_x': 8.0,
     'L1_xattn_maa_w': 8.0,
     'L1_xattn_maa_v': 2.802,
     'L1_xattn_maa_g': 2.689,
     'L1_xattn_maa_w1': 8.0,
     'L1_xattn_maa_w2': 8.0,
     'L1_xattn_time_decay': 3.783,
     'L1_xattn_decay_w1': 8.0,
     'L1_xattn_decay_w2': 8.0,
     'L1_xattn_faaaa': 8.0,
     'L1_xattn_fmaa_k': 7.838,
     'L1_xattn_fmaa_r': 8.0,
     'L1_xattn_fWk': 4.53,
     'L1_xattn_fWr': 8.0,
     'L1_xattn_fWv': 4.102,
     'L2_xattn_w_qkv': 26.512,
     'L2_xattn_w_q': 64.0,
     'L2_xattn_w_ao': 8.0,
     'L2_xattn_w_kv': 8.0,
     'L2_xattn_w_co': 8.0,
     'L2_xattn_w1': 8.0,
     'L2_xattn_w2': 8.0,
     'L3_xattn_w_q': 8.0,
     'L3_xattn_w_k': 8.0,
     'L3_xattn_w_v': 8.0,
     'L3_xattn_w_o': 8.0}
    for name, (base, spread) in spreads.items():
        noise = np.random.default_rng([zlib.crc32(name.encode()), seed]).standard_normal(out[name].shape)
        drawn = base * np.exp(spread * noise) if base else spread * noise
        out[name] = jnp.asarray(drawn.astype(out[name].dtype))
    for name, factor in factors.items():
        out[name] = (out[name] * factor).astype(out[name].dtype)
    return out
```

```python
from contextlib import ExitStack

import concourse.bass as bass
from concourse import mybir

F32 = mybir.dt.float32
ALU = mybir.AluOpType
ACT = mybir.ActivationFunctionType
AX = mybir.AxisListType.X

P = 128
B, L, C = 64, 64, 256
CT = C // P
G = 4
NG = B // G
PAIRS = G // 2
TOK = G * L
EPS = 1e-5
H0, D0 = 8, 64
H1, S1 = 32, 8
H2, D2 = 16, 16
KV = D2 + 1
DM, DD = 32, 64
FF = 4 * C

COLS = {}
for _name, _n in (("l0_gamma", 1), ("l0_beta", 1), ("l0_bq", 4), ("l0_bk", 4), ("l0_bo", 1),
                  ("ln1_w", 2), ("ln1_b", 2), ("ln2_w", 2), ("ln2_b", 2), ("maa_x", 2),
                  ("maa_w", 2), ("maa_k", 2), ("maa_v", 2), ("maa_r", 2), ("maa_g", 2),
                  ("time_decay", 2), ("faaaa", 2), ("gn_w", 2), ("gn_b", 2), ("fmaa_k", 2), ("fmaa_r", 2),
                  ("sa_s", 2), ("sa_b", 2), ("ca_s", 2), ("ca_b", 2), ("ml_s", 2), ("ml_b", 2),
                  ("sa_bq", 2), ("sa_bk", 2), ("ca_bq", 2), ("ca_bk", 2), ("b1", 8), ("alpha", 1),
                  ("even_head", 1), ("odd_head", 1)):
    COLS[_name] = (sum(n for _, n in COLS.values()), _n)
N_COLS = sum(n for _, n in COLS.values())
ROWS = {}
for _name, _n in (("l0_bv", H0 * D0), ("sa_bv", C), ("sa_bo", C), ("ca_bv", C), ("ca_bo", C), ("b2", C)):
    ROWS[_name] = (sum(n for _, n in ROWS.values()), _n)
N_ROWS = sum(n for _, n in ROWS.values())
WTS = {}
for _name, _t, _n in (("l0_q", 1, 512), ("l0_k", 1, 512), ("l0_v", 1, 512), ("l0_o", 4, 64),
                      ("ident", 1, 128), ("mean64", 1, 128), ("sum8", 1, 128), ("mean8", 1, 128),
                      ("spread", 8, 128), ("gather", 8, 128),
                      ("maa_w1", 2, 160), ("maa_w2", 1, 256), ("maa_w2g", 1, 256), ("dec_w1", 2, 64), ("dec_w2", 1, 256),
                      ("Wk", 2, 256), ("Wv", 2, 256), ("Wr", 2, 256), ("Wg", 2, 256), ("Wo", 2, 256),
                      ("fWk", 2, 256), ("fWr", 2, 256), ("fWv", 2, 256),
                      ("sa_q", 2, 256), ("sa_k", 2, 256), ("sa_v", 2, 256), ("sa_o", 2, 256),
                      ("ca_q", 2, 256), ("ca_k", 2, 256), ("ca_v", 2, 256), ("ca_o", 2, 256),
                      ("w1", 2, 1024), ("w2", 8, 256),
                      ("x_q", 2, 256), ("x_k", 2, 256), ("x_v", 2, 256), ("x_o", 2, 256)):
    WTS[_name] = (sum(t * n for _, t, n in WTS.values()), _t, _n)
N_WTS = sum(t * n for _, t, n in WTS.values())

PER = dict(
    l0_stat=4, l0_mean=4, l0_var=2, l0_rstd=2, l0_xn=2, l0_proj=24, l0_S=32, l0_nm=32, l0_T=32, l0_pt=32,
    l0_AV=32, l0_y=8, l0_yT=8, l0_out=4, l0_x1=4, ring0=32, ring1=32,
    ctx_tr=1, ctxT=1,
    ln_var=5, ln_rstd=5, ln_xh=5, ln_T=6, ln_out=6, xr_free=1,
    xxx=1, maa_p=1, maa_t=1, mix_p=5, mix_tmp=5, mix_x=5,
    dech_p=1, dech=1, decw_p=1, decw=1, rkv_p=4, rkv=3, eg=1, silu=1,
    ruk=1, ruk_p=1, bonus=1, spread_p=8, wkv_a=8, wkv_s=16, wkv_p=8, wkv_yp=2, wkv_y=2,
    gm_p=1, gd=1, gsq=1, gv_p=1, gve=1, grs=1, yg=1, wo_p=1, x2=1,
    ffn_in=1, fk_p=1, frelu=1, fkk=1, fr_p=1, fe=1, fv_p=1, x3=1,
    qkv_p=6, q_T=2, k_bd=2, v_sb=2, v_bd=2, s_p=8, mskd=8, mbias=8, sub=8, pexp=8, pt_p=8, pt_a=4, pt_v=4,
    av_p=4, cx=4, cxT_p=2, cxT=2, ao_p=2, ao=2, cmask=1,
    h1_p=4, u=4, usq=4, ut=4, utu=4, uth=4, ug=4, w2_p=1, x5=1,
    x3qk_p=3, x3q=1, x3k=1, x3v=1, s3_p=1, nm3=1, e3=1, pn3=1, pt3_p=1, pt3=1, c3_p=1, c3=1, d3_p=1, xo=1,
)
CHAIN = dict(vec_l0=20, vec=38, act=1)


def program(nc, x, ctx, mask_self, mask_cross, cols_d, rows_d, wts_d, out):
    with ExitStack() as es:
        def sb(name, *shape):
            return es.enter_context(nc.sbuf_tensor(name, [P, *shape], F32))

        sem = {n: es.enter_context(nc.semaphore(n)) for n in PER}
        vec_l0_step = es.enter_context(nc.semaphore("vec_l0_step"))
        vec_step = es.enter_context(nc.semaphore("vec_step"))
        act_step = es.enter_context(nc.semaphore("act_step"))
        ld_const = es.enter_context(nc.semaphore("ld_const"))
        ld_w = es.enter_context(nc.semaphore("ld_w"))
        ld_pair = [es.enter_context(nc.semaphore(f"ld_pair{p}")) for p in range(PAIRS)]
        ld_s0 = es.enter_context(nc.semaphore("ld_s0"))
        ld_cmask = es.enter_context(nc.semaphore("ld_cmask"))
        v_swap = es.enter_context(nc.semaphore("v_swap"))
        st_out = es.enter_context(nc.semaphore("st_out"))
        ready = es.enter_context(nc.semaphore("ready"))
        ready_pool = es.enter_context(nc.semaphore("ready_pool"))

        def at(g, name, k):
            return (g + 1) * PER[name] + k

        class Steps:
            def __init__(self, name):
                self.name, self.n = name, 0

            def start(self, g):
                self.g, self.n = g, 0

            def next(self):
                self.n += 1
                return self.g * CHAIN[self.name] + self.n

            def end(self):
                assert self.n == CHAIN[self.name], (self.name, self.n)

        cols = sb("cols", N_COLS)
        rows = sb("rows", N_ROWS)
        wts = sb("wts", N_WTS)

        def col(name, t=0):
            o = COLS[name][0] + t
            return cols[:, o:o + 1]

        def row(name):
            o, n = ROWS[name]
            return rows[:, o:o + n]

        def w(name, t=0):
            o, _, n = WTS[name]
            return wts[:, o + t * n:o + (t + 1) * n]

        ident = w("ident")
        bq8 = sb("bq8", 4)
        nhalf = sb("nhalf", 2 * TOK)
        selfm = sb("selfm", L)
        selfb = sb("selfb", L)
        x_t = sb("x_t", PAIRS, C)
        c_t = sb("c_t", PAIRS, C)
        st0 = sb("st0", 16)
        xn = sb("xn", C)
        q0 = sb("q0", 4, C)
        k0 = sb("k0", 4, C)
        v0 = sb("v0", 2, 512)
        nm0 = sb("nm0", 2, 2)
        p0 = sb("p0", 2, 2, C)
        pt0 = sb("pt0", 2, 2, C)
        rs0 = sb("rs0", H0, 2)
        rr0 = sb("rr0", H0, 2)
        y0 = sb("y0", 2, 512)
        yT0 = sb("yT0", 4, C)
        x1 = sb("x1", PAIRS, C)
        xr = sb("xr", PAIRS, C)
        bst = sb("bst", PAIRS, 6)
        mv = sb("mv", PAIRS, 2)
        ve = sb("ve", PAIRS)
        rstd = sb("rstd", PAIRS)
        xh = sb("xh", PAIRS, C)
        hT = sb("hT", CT, TOK)
        ctxT = sb("ctxT", CT, TOK)
        xs = sb("xs", CT, G, L + 1)
        sx = sb("sx", CT, TOK)
        xx = sb("xx", CT, TOK)
        tT = sb("tT", TOK)
        tg = sb("tg", TOK)
        mix = sb("mix", 5, CT, TOK)
        hd = sb("hd", TOK)
        e1 = sb("e1", CT, TOK)
        wsh = sb("wsh", CT, G, L)
        kT = sb("kT", CT, TOK)
        vT = sb("vT", CT, TOK)
        rT = sb("rT", CT, TOK)
        sg = sb("sg", CT, TOK)
        s0t = sb("s0t", G, CT, S1)
        av = sb("av", CT, S1, G, L)
        ybon = sb("ybon", CT, TOK)
        yc = sb("yc", CT, TOK)
        gq = sb("gq", CT, TOK)
        cmask = sb("cmask", PAIRS, L)
        crossm = sb("crossm", PAIRS, L)
        crossb = sb("crossb", PAIRS, L)
        kbd = sb("kbd", CT, 2, TOK)
        vsb = sb("vsb", PAIRS, C)[:]
        vsw = sb("vsw", PAIRS, C)
        vbd = sb("vbd", G, H2 // 2, 2, KV)
        pb = av[:, 0].rearrange("p a b c -> p (a b c)").rearrange("p (r h k) -> p r h k", r=4, k=L)
        mx = sb("mx", 4, 8)
        ptb = av[:, 1].rearrange("p a b c -> p (a b c)").rearrange("p (r j q) -> p r j q", r=4, q=P)
        rc = sb("rc", PAIRS, H2)
        cx = mix[:, 4]
        cT = mix[:, 3]
        tmp = sb("tmp", PAIRS, C)
        ub = av[:, 0].rearrange("p a b c -> p (a b c)").rearrange("p (j t) -> p j t", j=8)
        tb = av[:, 1].rearrange("p a b c -> p (a b c)").rearrange("p (j t) -> p j t", j=8)
        p3 = sb("p3", PAIRS, P)
        nm3 = sb("nm3", PAIRS)
        sm3 = sb("sm3", PAIRS)
        rc3 = sb("rc3", PAIRS)
        pT3 = sb("pT3", PAIRS, P)
        v3 = mix[:, 2]
        xo = sb("xo", PAIRS, C)

        ring = [es.enter_context(nc.psum_tensor(f"ring{i}", [P, 512], F32)) for i in range(2)]
        ptp = es.enter_context(nc.psum_tensor("ptp", [P, 512], F32))
        yp = es.enter_context(nc.psum_tensor("yp", [P, 512], F32))
        R = [es.enter_context(nc.psum_tensor(f"R{i}", [P, 512], F32)) for i in range(4)]

        def two(ap):
            return ap.rearrange("p (a b) -> p a b", a=2)

        block = es.enter_context(nc.Block())
        N_CONST = 4

        @block.sync
        def _(sp):
            for h in range(2):
                sp.dma_start(selfm[h * L:(h + 1) * L, :], mask_self[0, 0]).then_inc(ld_const, 16)
            sp.dma_start(cols[:], cols_d).then_inc(ld_const, 16)
            sp.dma_start(rows[:], rows_d.to_broadcast([P, N_ROWS])).then_inc(ld_const, 16)
            step = N_WTS // 4
            for i in range(4):
                hi = N_WTS if i == 3 else (i + 1) * step
                sp.dma_start(wts[:, i * step:hi], wts_d[:, i * step:hi]).then_inc(ld_w, 16)

            def loads(g):
                for p in range(PAIRS):
                    b0 = g * G + 2 * p
                    sp.wait_ge(sem["l0_x1"], at(g, "l0_x1", 2 * (p + 1) - 4))
                    sp.wait_ge(sem["ctx_tr"], at(g, "ctx_tr", 0))
                    sp.dma_start(x_t[:, p, :], x[bass.ds(b0, 2)].rearrange("b l c -> (b l) c")).then_inc(ld_pair[p], 16)
                    sp.dma_start(c_t[:, p, :], ctx[bass.ds(b0, 2)].rearrange("b l c -> (b l) c")).then_inc(ld_pair[p], 16)

            def loads_rest(g):
                sp.wait_ge(sem["wkv_s"], at(g, "wkv_s", 0))
                s0src = ctx[bass.ds(g * G, G), 2:2 + S1, :].rearrange("b s c -> b (s c)")
                for t in range(CT):
                    sp.dma_start(s0t[:, :, t, :], s0src[:, t * P * S1:(t + 1) * P * S1].rearrange("b (p t) -> p b t", t=S1)).then_inc(ld_s0, 16)
                sp.wait_ge(sem["cmask"], at(g, "cmask", 0))
                for p in range(PAIRS):
                    sp.dma_start(cmask[:, p, :], mask_cross[bass.ds(g * G + 2 * p, 2), 0].rearrange("b q k -> (b q) k")).then_inc(ld_cmask, 16)

            def swap(g, a):
                sp.wait_ge(sem["v_sb"], at(g, "v_sb", a + 1))
                sp.wait_ge(sem["v_bd"], at(g, "v_bd", a))
                sp.dma_start(vsw[0:L], vsb[L:P]).then_inc(v_swap, 16)
                sp.dma_start(vsw[L:P], vsb[0:L]).then_inc(v_swap, 16)

            def store(g):
                sp.wait_ge(sem["xo"], at(g, "xo", 1))
                for p in range(PAIRS):
                    sp.dma_start(out[bass.ds(g * G + 2 * p, 2)].rearrange("b l c -> (b l) c"), xo[:, p, :]).then_inc(st_out, 16)

            with sp.Fori(0, NG) as g:
                loads(g)
                loads_rest(g)
                swap(g, 0)
                swap(g, 1)
                store(g)
            sp.wait_ge(st_out, NG * PAIRS * 16)

        @block.tensor
        def _(pe):
            mm, tr = nc.tensor.matmul, nc.tensor.transpose
            pe.wait_ge(ld_w, 64)
            pe.wait_ge(ready, 2)
            use = [0]

            def ring_use(g):
                u = use[0] % (2 * PER["ring0"])
                use[0] += 1
                pe.wait_ge(sem[f"ring{u % 2}"], at(g, f"ring{u % 2}", u // 2))
                return ring[u % 2]

            def ring_done(g):
                u = (use[0] - 1) % (2 * PER["ring0"]) + 1
                pe.wait_ge(sem["ring0"], at(g, "ring0", (u + 1) // 2))
                pe.wait_ge(sem["ring1"], at(g, "ring1", u // 2))

            def l0_stats(g, p):
                pe.wait_ge(sem["l0_y"], at(g, "l0_y", 4 * p))
                for j in range(2):
                    pe.wait_ge(sem["l0_stat"], at(g, "l0_stat", 2 * p + j + 1))
                    mm(yp[:, j:j + 1], w("mean64"), st0[:, 6 + j:7 + j], start=True, stop=True).then_inc(sem["l0_mean"], 1)

            def l0_project(g, n):
                p, r = n // 2, slice(L * (n % 2), L * (n % 2) + L)
                pe.wait_ge(sem["l0_xn"], at(g, "l0_xn", p + 1))
                for name, src in (("l0_q", xn[r, :]), ("l0_k", c_t[r, p, :])):
                    for j in range(2):
                        bank = ring_use(g)
                        for i in range(2):
                            m = 2 * j + i
                            last = mm(bank[:, i * C:(i + 1) * C], w(name)[r, m * P:(m + 1) * P], src, start=True, stop=True)
                        last.then_inc(sem["l0_proj"], 1)
                for t in range(2):
                    bank = ring_use(g)
                    mm(bank[:, :], c_t[r, p, t * P:(t + 1) * P], w("l0_v")[r, :], start=True, stop=True).then_inc(sem["l0_proj"], 1)

            def l0_scores(g, n, h):
                r = slice(D0 * (h % 2), D0 * (h % 2) + D0)
                bank = ring_use(g)
                for t in range(2):
                    last = mm(bank[:, t * C:(t + 1) * C], q0[r, h // 2, t * P:(t + 1) * P], k0[r, h // 2, :], start=True, stop=True)
                last.then_inc(sem["l0_S"], 1)

            def l0_turn(g, n, h, u_use):
                pe.wait_ge(sem[f"ring{u_use % 2}"], at(g, f"ring{u_use % 2}", u_use // 2 + 1))
                pe.wait_ge(sem["l0_pt"], at(g, "l0_pt", 8 * n + h))
                if h == 0:
                    pe.wait_ge(sem["l0_x1"], at(g, "l0_x1", n))
                for kt in range(2):
                    for qt in range(2):
                        last = tr(ptp[:, kt * C + qt * P:kt * C + (qt + 1) * P], p0[:, h % 2, qt, kt * P:(kt + 1) * P], ident)
                last.then_inc(sem["l0_T"], 1)

            def l0_values(g, n, h):
                pe.wait_ge(sem["l0_pt"], at(g, "l0_pt", 8 * n + h + 1))
                if h % 4 == 0:
                    pe.wait_ge(sem["l0_y"], at(g, "l0_y", 2 * n + h // 4))
                for qt in range(2):
                    o = (h % 4) * P + qt * D0
                    for kt in range(2):
                        last = mm(yp[:, o:o + D0], pt0[:, h % 2, kt, qt * P:(qt + 1) * P], v0[:, kt, h * D0:(h + 1) * D0],
                                  start=kt == 0, stop=kt == 1)
                last.then_inc(sem["l0_AV"], 1)

            def l0_heads(g, n):
                ring_done(g)
                first = use[0] % (2 * PER["ring0"])
                for i in range(H0 + 2):
                    if i < H0:
                        l0_scores(g, n, i)
                    if 1 <= i <= H0:
                        l0_turn(g, n, i - 1, first + i - 1)
                    if i >= 2:
                        l0_values(g, n, i - 2)

            def l0_output(g, n):
                r = slice(L * (n % 2), L * (n % 2) + L)
                pe.wait_ge(sem["l0_y"], at(g, "l0_y", 2 * n + 2))
                for j in range(2):
                    bank = ring_use(g)
                    for i in range(2):
                        for qt in range(2):
                            last = tr(bank[:, i * C + qt * P:i * C + (qt + 1) * P], y0[:, qt, (2 * j + i) * P:(2 * j + i + 1) * P], ident)
                    last.then_inc(sem["l0_yT"], 1)
                ring_done(g)
                for t in range(4):
                    last = mm(ptp[r, 0:C], w("l0_o", t), yT0[:, t, :], start=t == 0, stop=t == 3)
                last.then_inc(sem["l0_out"], 1)

            def turn(g, bank, src, name):
                for p in range(PAIRS):
                    for t in range(CT):
                        last = tr(bank[:, t * TOK + p * P:t * TOK + (p + 1) * P], src[:, p, t * P:(t + 1) * P], ident)
                last.then_inc(sem[name], 1)

            def channel_major(bank, wname, src, name):
                for o in range(CT):
                    for t in range(CT):
                        last = mm(bank[:, o * TOK:(o + 1) * TOK], w(wname, t)[:, o * P:(o + 1) * P], src[:, t, :],
                                  start=t == 0, stop=t == CT - 1)
                last.then_inc(sem[name], 1)

            def token_major(bank, wname, src, name, tiles=CT):
                for p in range(PAIRS):
                    for t in range(tiles):
                        last = mm(bank[:, p * C:(p + 1) * C], src[:, t, p * P:(p + 1) * P], w(wname, t),
                                  start=t == 0, stop=t == tiles - 1)
                last.then_inc(sem[name], 1)

            def layer1(g):
                for p in range(PAIRS):
                    pe.wait_ge(ld_pair[p], g * 32 + 32)
                pe.wait_ge(sem["c3"], at(g, "c3", 0))
                pe.wait_ge(sem["xo"], at(g, "xo", 0))
                turn(g, R[1], c_t, "ctx_tr")
                pe.wait_ge(sem["ln_xh"], at(g, "ln_xh", 1))
                turn(g, R[0], xh, "ln_T")
                pe.wait_ge(sem["xxx"], at(g, "xxx", 1))
                for t in range(CT):
                    mm(R[0][:, 0:TOK], w("maa_w1", t)[:, 0:P], xx[:, t, :], start=t == 0, stop=t == 1)
                for t in range(CT):
                    last = mm(R[0][0:DM, TOK:2 * TOK], w("maa_w1", t)[:, P:P + DM], xx[:, t, :], start=t == 0, stop=t == 1)
                last.then_inc(sem["maa_p"], 1)
                pe.wait_ge(sem["maa_t"], at(g, "maa_t", 1))
                pe.wait_ge(sem["ctxT"], at(g, "ctxT", 1))
                for f in range(5):
                    if f == 4:
                        pe.wait_ge(sem["mix_tmp"], at(g, "mix_tmp", 1))
                    bank = R[(f + 1) % 4]
                    for o in range(CT):
                        if f < 4:
                            r = slice(DM * f, DM * (f + 1))
                            last = mm(bank[:, o * TOK:(o + 1) * TOK], w("maa_w2")[r, o * P:(o + 1) * P], tT[r, :], start=True, stop=True)
                        else:
                            last = mm(bank[:, o * TOK:(o + 1) * TOK], w("maa_w2g")[0:DM, o * P:(o + 1) * P], tg[0:DM, :], start=True, stop=True)
                    last.then_inc(sem["mix_p"], 1)
                pe.wait_ge(sem["mix_x"], at(g, "mix_x", 1))
                pe.wait_ge(sem["mix_tmp"], at(g, "mix_tmp", 2))
                for t in range(CT):
                    last = mm(R[2][0:DD, 0:TOK], w("dec_w1", t), mix[:, 0, t, :], start=t == 0, stop=t == 1)
                last.then_inc(sem["dech_p"], 1)
                pe.wait_ge(sem["mix_x"], at(g, "mix_x", 2))
                pe.wait_ge(sem["mix_tmp"], at(g, "mix_tmp", 4))
                channel_major(R[0], "Wk", mix[:, 1], "rkv_p")
                pe.wait_ge(sem["dech"], at(g, "dech", 1))
                for o in range(CT):
                    last = mm(R[3][:, o * TOK:(o + 1) * TOK], w("dec_w2")[0:DD, o * P:(o + 1) * P], hd[0:DD, :], start=True, stop=True)
                last.then_inc(sem["decw_p"], 1)
                pe.wait_ge(sem["mix_x"], at(g, "mix_x", 3))
                pe.wait_ge(sem["mix_tmp"], at(g, "mix_tmp", 5))
                channel_major(R[1], "Wv", mix[:, 2], "rkv_p")
                pe.wait_ge(sem["mix_x"], at(g, "mix_x", 4))
                channel_major(R[2], "Wr", mix[:, 3], "rkv_p")
                pe.wait_ge(sem["mix_x"], at(g, "mix_x", 5))
                pe.wait_ge(sem["decw"], at(g, "decw", 1))
                channel_major(R[3], "Wg", mix[:, 4], "rkv_p")
                pe.wait_ge(sem["ruk"], at(g, "ruk", 1))
                for o in range(CT):
                    last = mm(R[0][:, o * TOK:(o + 1) * TOK], w("sum8"), yc[:, o, :], start=True, stop=True)
                last.then_inc(sem["ruk_p"], 1)

                def spread(t):
                    for j in range(4):
                        k = 4 * t + j
                        if k >= 2:
                            pe.wait_ge(sem["wkv_a"], at(g, "wkv_a", k - 1))
                        else:
                            pe.wait_ge(sem["rkv"], at(g, "rkv", 3))
                        bank = R[1 + k % 2]
                        for i in range(2):
                            last = mm(bank[:, i * TOK:(i + 1) * TOK], w("spread", 2 * j + i), vT[:, t, :], start=True, stop=True)
                        last.then_inc(sem["spread_p"], 1)

                def gather(t):
                    if t == 0:
                        pe.wait_ge(sem["silu"], at(g, "silu", 1))
                    for j in range(4):
                        pe.wait_ge(sem["wkv_p"], at(g, "wkv_p", 4 * t + j + 1))
                        for i in range(2):
                            s = 2 * j + i
                            last = mm(R[3][:, t * TOK:(t + 1) * TOK], w("gather", s), av[:, t, s].rearrange("p b l -> p (b l)"),
                                      start=s == 0, stop=s == 7)
                    last.then_inc(sem["wkv_yp"], 1)

                spread(0)
                spread(1)
                gather(0)
                pe.wait_ge(sem["wkv_y"], at(g, "wkv_y", 1))
                gather(1)
                pe.wait_ge(sem["wkv_y"], at(g, "wkv_y", 2))
                pe.wait_ge(sem["bonus"], at(g, "bonus", 1))
                mm(R[0][:, :], w("mean8"), yc[:].rearrange("p a b -> p (a b)"), start=True, stop=True).then_inc(sem["gm_p"], 1)
                pe.wait_ge(sem["gsq"], at(g, "gsq", 1))
                mm(R[1][:, :], w("mean8"), gq[:].rearrange("p a b -> p (a b)"), start=True, stop=True).then_inc(sem["gv_p"], 1)
                pe.wait_ge(sem["yg"], at(g, "yg", 1))
                token_major(R[2], "Wo", yc, "wo_p")
                pe.wait_ge(sem["ln_xh"], at(g, "ln_xh", 2))
                turn(g, R[0], xh, "ln_T")
                pe.wait_ge(sem["ffn_in"], at(g, "ffn_in", 1))
                channel_major(R[0], "fWk", mix[:, 0], "fk_p")
                token_major(R[1], "fWr", mix[:, 1], "fr_p")
                pe.wait_ge(sem["fkk"], at(g, "fkk", 1))
                token_major(R[2], "fWv", mix[:, 2], "fv_p")

            def attention(g, a):
                q, k, v, o = (("sa_q", "sa_k", "sa_v", "sa_o"), ("ca_q", "ca_k", "ca_v", "ca_o"))[a]
                src = hT if a == 0 else ctxT
                pe.wait_ge(sem["ln_xh"], at(g, "ln_xh", 3 + a))
                turn(g, R[0], xh, "ln_T")
                if a == 0:
                    pe.wait_ge(sem["ln_out"], at(g, "ln_out", 3))
                channel_major(R[1], k, src, "qkv_p")
                token_major(R[2], v, src, "qkv_p")
                pe.wait_ge(sem["ln_out"], at(g, "ln_out", 3 + a))
                channel_major(R[0], q, hT, "qkv_p")
                pe.wait_ge(sem["q_T"], at(g, "q_T", a + 1))
                pe.wait_ge(sem["k_bd"], at(g, "k_bd", a + 1))
                pe.wait_ge(sem["v_sb"], at(g, "v_sb", a + 1))
                for r4 in range(4):
                    r = slice(32 * r4, 32 * r4 + 32)
                    for b in range(G):
                        for t in range(CT):
                            oo = (b // 2) * C + t * P
                            last = mm(R[r4][L * (b % 2):L * (b % 2) + L, oo:oo + P], hTq[r, t, b * L:(b + 1) * L],
                                      kbd[r, t, :, b * L:(b + 1) * L], start=True, stop=True)
                    last.then_inc(sem["s_p"], 1)
                for r4 in range(4):
                    pe.wait_ge(sem["pexp"], at(g, "pexp", 4 * a + r4 + 1))
                    for j in range(4):
                        last = tr(R[r4][:, j * P:(j + 1) * P], pb[:, r4, 2 * j:2 * j + 2, :].rearrange("p a b -> p (a b)"), ident)
                    last.then_inc(sem["pt_p"], 1)
                pe.wait_ge(sem["pt_a"], at(g, "pt_a", 2 * a + 2))
                pe.wait_ge(sem["pt_v"], at(g, "pt_v", 2 * a + 2))
                pe.wait_ge(sem["v_bd"], at(g, "v_bd", a + 1))
                for p in range(PAIRS):
                    for b2 in range(2):
                        for t in range(CT):
                            for r4 in range(4):
                                hp = t * 4 + r4
                                last = mm(R[p][L * b2:L * b2 + L, hp * 2 * KV:(hp + 1) * 2 * KV],
                                          ptb[:, r4, 2 * p + t, L * b2:L * b2 + L],
                                          vbd[:, 2 * p + b2, hp].rearrange("p a b -> p (a b)"), start=True, stop=True)
                    last.then_inc(sem["av_p"], 1)
                pe.wait_ge(sem["cx"], at(g, "cx", 2 * a + 2))
                turn(g, R[2], cx, "cxT_p")
                pe.wait_ge(sem["cxT"], at(g, "cxT", a + 1))
                token_major(R[3], o, cT, "ao_p")

            hTq = sx

            def mlp(g):
                pe.wait_ge(sem["ln_xh"], at(g, "ln_xh", 5))
                pe.wait_ge(sem["ao"], at(g, "ao", 2))
                turn(g, R[0], xh, "ln_T")
                pe.wait_ge(sem["ln_out"], at(g, "ln_out", 5))
                for c in range(4):
                    for i in range(2):
                        j = 2 * c + i
                        for t in range(CT):
                            last = mm(R[c][:, i * TOK:(i + 1) * TOK], w("w1", t)[:, j * P:(j + 1) * P], hT[:, t, :],
                                      start=t == 0, stop=t == 1)
                    last.then_inc(sem["h1_p"], 1)
                pe.wait_ge(sem["ug"], at(g, "ug", 4))
                token_major(R[0], "w2", tb, "w2_p", tiles=8)

            def layer3(g):
                channel_major(R[2], "x_k", ctxT, "x3qk_p")
                token_major(R[3], "x_v", ctxT, "x3qk_p")
                pe.wait_ge(sem["x5"], at(g, "x5", 1))
                turn(g, R[0], xr, "ln_T")
                pe.wait_ge(sem["ln_out"], at(g, "ln_out", 6))
                channel_major(R[1], "x_q", hT, "x3qk_p")
                pe.wait_ge(sem["x3q"], at(g, "x3q", 1))
                pe.wait_ge(sem["x3k"], at(g, "x3k", 1))
                for b in range(G):
                    for t in range(CT):
                        o = (b // 2) * P + (b % 2) * L
                        last = mm(R[0][L * (b % 2):L * (b % 2) + L, o:o + L], sx[:, t, b * L:(b + 1) * L],
                                  kbd[:, 0, 0:2, :].rearrange("p a b -> p (a b)")[:, t * TOK + b * L:t * TOK + (b + 1) * L], start=t == 0, stop=t == 1)
                last.then_inc(sem["s3_p"], 1)
                pe.wait_ge(sem["pn3"], at(g, "pn3", 1))
                for p in range(PAIRS):
                    last = tr(R[1][:, p * P:(p + 1) * P], p3[:, p, :], ident)
                last.then_inc(sem["pt3_p"], 1)
                pe.wait_ge(sem["pt3"], at(g, "pt3", 1))
                pe.wait_ge(sem["x3v"], at(g, "x3v", 1))
                for p in range(PAIRS):
                    for t in range(CT):
                        last = mm(R[2][:, t * TOK + p * P:t * TOK + (p + 1) * P], v3[:, p, t * P:(t + 1) * P], pT3[:, p, :], start=True, stop=True)
                last.then_inc(sem["c3_p"], 1)
                pe.wait_ge(sem["c3"], at(g, "c3", 1))
                token_major(R[3], "x_o", cT, "d3_p")

            with pe.Fori(0, NG) as g:
                use[0] = 0
                for n in range(G):
                    if n % 2 == 0:
                        pe.wait_ge(ld_pair[n // 2], g * 32 + 32)
                        l0_stats(g, n // 2)
                    l0_project(g, n)
                    l0_heads(g, n)
                    l0_output(g, n)
                layer1(g)
                attention(g, 0)
                attention(g, 1)
                mlp(g)
                layer3(g)

        @block.scalar
        def _(act):
            A = nc.scalar.activation
            steps = Steps("act")
            act.wait_ge(ld_const, 16 * N_CONST)
            act.wait_ge(ready, 2)
            use = [0]

            def l0_qk(g, n):
                for i, (dst, scale) in enumerate(((q0, 0.125), (q0, 0.125), (k0, 1.0), (k0, 1.0))):
                    act.wait_ge(sem["l0_proj"], at(g, "l0_proj", 6 * n + i + 1))
                    for j in range(2):
                        m = 2 * (i % 2) + j
                        bias = bq8[:, m:m + 1] if i < 2 else col("l0_bk", m)
                        last = A(dst[:, m, :], ring[i % 2][:, j * C:(j + 1) * C], ACT.Identity, bias=bias, scale=scale)
                    last.then_inc(sem[f"ring{i % 2}"], 1)

            def l0_exp(g, n, h):
                u = 8 * n + h
                act.wait_ge(sem["l0_nm"], at(g, "l0_nm", u + 1))
                act.wait_ge(sem["l0_T"], at(g, "l0_T", u - 1))
                for qt in range(2):
                    last = A(p0[:, h % 2, qt, :], ring[h % 2][:, qt * C:(qt + 1) * C], ACT.Exp, bias=nm0[:, h % 2, qt:qt + 1],
                             accum_out=rs0[:, h, qt:qt + 1])
                last.then_inc(sem[f"ring{h % 2}"], 1)

            def l0_yT(g, n):
                for j in range(2):
                    act.wait_ge(sem["l0_yT"], at(g, "l0_yT", 2 * n + j + 1))
                    A(yT0[:, 2 * j:2 * j + 2, :], two(ring[j][:]), ACT.Copy).then_inc(sem[f"ring{j}"], 1)

            def norm_out(g, k, dst, scale, bias):
                act.wait_ge(sem["ln_T"], at(g, "ln_T", k))
                for t in range(CT):
                    last = A(dst(t), R[0][:, t * TOK:(t + 1) * TOK].rearrange("p (b l) -> p b l", l=L), ACT.Identity,
                             bias=col(bias, t), scale=col(scale, t))
                last.then_inc(sem["ln_out"], 1)

            def copy(dst, src, name):
                A(dst, src, ACT.Copy).then_inc(sem[name], 1)

            def flat(t):
                return t[:].rearrange("p a b -> p (a b)")

            def hT_out(t):
                return hT[:, t, :].rearrange("p (b l) -> p b l", l=L)

            def xs_out(t):
                return xs[:, t, :, 1:L + 1]

            def layer1(g):
                act.wait_ge(sem["ctx_tr"], at(g, "ctx_tr", 1))
                copy(flat(ctxT), R[1][:], "ctxT")
                norm_out(g, 1, xs_out, "ln1_w", "ln1_b")
                act.wait_ge(sem["maa_p"], at(g, "maa_p", 1))
                A(tT[:], R[0][:, 0:TOK], ACT.Tanh)
                A(tg[0:DM, :], R[0][0:DM, TOK:2 * TOK], ACT.Tanh).then_inc(sem["maa_t"], 1)
                act.wait_ge(sem["dech_p"], at(g, "dech_p", 1))
                A(hd[0:DD, :], R[2][0:DD, 0:TOK], ACT.Tanh).then_inc(sem["dech"], 1)
                act.wait_ge(sem["rkv_p"], at(g, "rkv_p", 1))
                copy(flat(kT), R[0][:], "rkv")
                act.wait_ge(sem["decw_p"], at(g, "decw_p", 1))
                for t in range(CT):
                    last = A(e1[:, t, :], R[3][:, t * TOK:(t + 1) * TOK], ACT.Exp, bias=col("time_decay", t))
                last.then_inc(act_step, 1)
                act.wait_ge(act_step, steps.next())
                for t in range(CT):
                    last = A(wsh[:, t, :, 1:L], e1[:, t, :].rearrange("p (b l) -> p b l", l=L)[:, :, 0:L - 1], ACT.Exp, scale=-1.0)
                last.then_inc(sem["decw"], 1)
                act.wait_ge(sem["rkv_p"], at(g, "rkv_p", 2))
                copy(flat(vT), R[1][:], "rkv")
                act.wait_ge(sem["rkv_p"], at(g, "rkv_p", 3))
                copy(flat(rT), R[2][:], "rkv")
                act.wait_ge(sem["rkv_p"], at(g, "rkv_p", 4))
                A(flat(sg), R[3][:], ACT.Tanh, scale=0.5).then_inc(sem["eg"], 1)
                act.wait_ge(sem["gd"], at(g, "gd", 1))
                A(flat(gq), flat(yc), ACT.Square).then_inc(sem["gsq"], 1)
                act.wait_ge(sem["gve"], at(g, "gve", 1))
                A(flat(gq), flat(gq), ACT.Sqrt).then_inc(sem["grs"], 1)
                norm_out(g, 2, xs_out, "ln2_w", "ln2_b")
                act.wait_ge(sem["frelu"], at(g, "frelu", 1))
                A(mix[:, 2], mix[:, 3], ACT.Square).then_inc(sem["fkk"], 1)
                act.wait_ge(sem["fr_p"], at(g, "fr_p", 1))
                A(flat(e1), R[1][:], ACT.Tanh, scale=0.5).then_inc(sem["fe"], 1)

            def attention(g, a):
                norm_out(g, 3 + a, hT_out, ("sa_s", "ca_s")[a], ("sa_b", "ca_b")[a])
                act.wait_ge(sem["qkv_p"], at(g, "qkv_p", 3 * a + 3))
                for t in range(CT):
                    last = A(sx[:, t, :], R[0][:, t * TOK:(t + 1) * TOK], ACT.Identity, bias=col(("sa_bq", "ca_bq")[a], t))
                last.then_inc(sem["q_T"], 1)
                for r4 in range(4):
                    act.wait_ge(sem["sub"], at(g, "sub", 4 * a + r4 + 1))
                    pf = pb[:, r4].rearrange("p a b -> p (a b)")
                    A(pf, pf, ACT.Exp).then_inc(sem["pexp"], 1)
                for r4 in (0, 2):
                    act.wait_ge(sem["pt_p"], at(g, "pt_p", 4 * a + r4 + 1))
                    copy(ptb[:, r4].rearrange("p a b -> p (a b)"), R[r4][:], "pt_a")
                act.wait_ge(sem["cxT_p"], at(g, "cxT_p", a + 1))
                copy(flat(cT), R[2][:], "cxT")

            def mlp(g):
                norm_out(g, 5, hT_out, "ml_s", "ml_b")
                for c in range(4):
                    act.wait_ge(sem["u"], at(g, "u", c + 1))
                    A(tb[:, 2 * c:2 * c + 2, :], ub[:, 2 * c:2 * c + 2, :], ACT.Square).then_inc(sem["usq"], 1)
                for c in range(4):
                    act.wait_ge(sem["utu"], at(g, "utu", c + 1))
                    A(tb[:, 2 * c:2 * c + 2, :], tb[:, 2 * c:2 * c + 2, :], ACT.Tanh, scale=0.7978845608028654).then_inc(sem["uth"], 1)

            def layer3(g):
                act.wait_ge(sem["ln_T"], at(g, "ln_T", 6))
                copy(flat(hT), R[0][:], "ln_out")
                act.wait_ge(sem["x3qk_p"], at(g, "x3qk_p", 3))
                copy(flat(sx), R[1][:], "x3q")
                act.wait_ge(sem["nm3"], at(g, "nm3", 1))
                for p in range(PAIRS):
                    for b2 in range(2):
                        r = slice(L * b2, L * b2 + L)
                        last = A(p3[r, p, L * b2:L * b2 + L], R[0][r, p * P + L * b2:p * P + L * b2 + L], ACT.Exp,
                                 bias=nm3[r, p:p + 1], scale=0.0625, accum_out=sm3[r, p:p + 1])
                last.then_inc(sem["e3"], 1)
                act.wait_ge(sem["pt3_p"], at(g, "pt3_p", 1))
                copy(flat(pT3), R[1][:, 0:PAIRS * P], "pt3")
                act.wait_ge(sem["c3_p"], at(g, "c3_p", 1))
                copy(flat(cT), R[2][:], "c3")

            with act.Fori(0, NG) as g:
                steps.start(g)
                for n in range(G):
                    l0_qk(g, n)
                    for h in range(H0):
                        l0_exp(g, n, h)
                    l0_yT(g, n)
                layer1(g)
                attention(g, 0)
                attention(g, 1)
                mlp(g)
                layer3(g)
                steps.end()

        @block.gpsimd
        def _(pool):
            GT = nc.gpsimd.tensor_tensor
            pool.memset(nhalf[:], -0.5)
            pool.memset(wsh[:, :, :, 0:1], 0.0)
            pool.memset(p3[:], 0.0).then_inc(ready_pool, 1)
            pool.wait_ge(ready_pool, 1)

            def l0(g):
                for p in range(PAIRS):
                    pool.wait_ge(sem["l0_var"], at(g, "l0_var", p + 1))
                    GT(st0[:, 10:11], st0[:, 9:10], nhalf[:, 0:1], ALU.pow).then_inc(sem["l0_rstd"], 1)

            def norm(g, k):
                pool.wait_ge(sem["ln_var"], at(g, "ln_var", k))
                GT(rstd[:], ve[:], nhalf[:, 0:PAIRS], ALU.pow).then_inc(sem["ln_rstd"], 1)

            def layer1(g):
                norm(g, 1)
                xa = xs[:].rearrange("p t b l -> p (t b) l")[:, :, 1:L + 1]
                for f in range(5):
                    pool.wait_ge(sem["mix_tmp"], at(g, "mix_tmp", f + 1))
                    m = mix[:, f].rearrange("p t (b l) -> p (t b) l", l=L)
                    GT(m, m, xa, ALU.add).then_inc(sem["mix_x"], 1)
                for t in range(CT):
                    for j in range(4):
                        pool.wait_ge(sem["wkv_s"], at(g, "wkv_s", 8 * t + 2 * j + 2))
                        a2 = av[:, t, 2 * j:2 * j + 2].rearrange("p s b l -> p s (b l)")
                        GT(a2, a2, rT[:, t:t + 1, :].to_broadcast([P, 2, TOK]), ALU.mult).then_inc(sem["wkv_p"], 1)
                norm(g, 2)

            def attention(g, a):
                norm(g, 3 + a)
                for r4 in range(4):
                    pool.wait_ge(sem["mskd"], at(g, "mskd", 4 * a + r4 + 1))
                    if a == 0:
                        GT(pb[:, r4], pb[:, r4], selfb[:].unsqueeze(1).to_broadcast([P, 8, L]), ALU.add).then_inc(sem["mbias"], 1)
                    else:
                        s = pb[:, r4].rearrange("p (r h) k -> p r h k", r=PAIRS)
                        GT(s, s, crossb[:].unsqueeze(2).to_broadcast([P, PAIRS, 4, L]), ALU.add).then_inc(sem["mbias"], 1)

            def mlp(g):
                norm(g, 5)
                for c in range(4):
                    pool.wait_ge(sem["ut"], at(g, "ut", c + 1))
                    s = slice(2 * c, 2 * c + 2)
                    GT(tb[:, s, :], tb[:, s, :], ub[:, s, :], ALU.mult).then_inc(sem["utu"], 1)

            with pool.Fori(0, NG) as g:
                l0(g)
                layer1(g)
                attention(g, 0)
                attention(g, 1)
                mlp(g)

        @block.vector
        def _(dve):
            V = nc.vector
            for name, per in PER.items():
                dve.sem_inc(sem[name], per)
            dve.wait_ge(ld_const, 16 * N_CONST)
            V.memset(vbd[:], 0.0)
            V.tensor_scalar(selfb[:], selfm[:], 10000.0, -10000.0, ALU.mult, ALU.add).then_inc(ready, 1)
            dve.wait_ge(ready, 1)
            V.memset(vbd[0:L, :, :, 0, D2:KV], 1.0)
            V.memset(vbd[L:P, :, :, 1, D2:KV], 1.0)
            V.tensor_scalar(selfm[:], selfm[:], 0.25, None, ALU.mult)
            V.tensor_scalar(bq8[:], cols[:, COLS["l0_bq"][0]:COLS["l0_bq"][0] + 4], 0.125, None, ALU.mult).then_inc(ready, 1)
            dve.wait_ge(ready, 2)
            dve.wait_ge(ready_pool, 1)
            l0_steps = Steps("vec_l0")
            steps = Steps("vec")

            def l0_norm(g, p):
                dve.wait_ge(ld_pair[p], g * 32 + 32)
                V.bn_stats(st0[:, 0:6], x_t[:, p, :]).then_inc(vec_l0_step, 1)
                dve.wait_ge(vec_l0_step, l0_steps.next())
                V.memset(st0[:, 15:16], 0.0)
                V.bn_aggr(st0[:, 6:8], st0[:, 0:6]).then_inc(vec_l0_step, 1)
                dve.wait_ge(vec_l0_step, l0_steps.next())
                V.tensor_copy(st0[:, 12:13], st0[:, 7:8]).then_inc(sem["l0_stat"], 1)
                dve.wait_ge(sem["l0_mean"], at(g, "l0_mean", 2 * p + 1))
                V.tensor_tensor(st0[:, 8:9], st0[:, 6:7], yp[:, 0:1], ALU.subtract).then_inc(vec_l0_step, 1)
                dve.wait_ge(vec_l0_step, l0_steps.next())
                V.tensor_copy(st0[:, 11:12], yp[:, 0:1])
                V.tensor_tensor(st0[:, 9:10], st0[:, 8:9], st0[:, 8:9], ALU.mult).then_inc(vec_l0_step, 1)
                dve.wait_ge(vec_l0_step, l0_steps.next())
                V.tensor_tensor(st0[:, 7:8], st0[:, 12:13], st0[:, 9:10], ALU.add).then_inc(sem["l0_stat"], 1)
                dve.wait_ge(sem["l0_mean"], at(g, "l0_mean", 2 * p + 2))
                V.tensor_scalar(st0[:, 9:10], yp[:, 1:2], EPS, None, ALU.add).then_inc(sem["l0_var"], 1)
                dve.wait_ge(sem["l0_rstd"], at(g, "l0_rstd", p + 1))
                V.tensor_tensor(st0[:, 10:11], st0[:, 10:11], col("l0_gamma"), ALU.mult).then_inc(vec_l0_step, 1)
                dve.wait_ge(vec_l0_step, l0_steps.next())
                V.tensor_scalar(xn[:], x_t[:, p, :], st0[:, 11:12], st0[:, 10:11], ALU.subtract, ALU.mult).then_inc(vec_l0_step, 1)
                dve.wait_ge(vec_l0_step, l0_steps.next())
                V.tensor_scalar(xn[:], xn[:], col("l0_beta"), None, ALU.add).then_inc(sem["l0_xn"], 1)

            def l0_v(g, n):
                for t in range(2):
                    dve.wait_ge(sem["l0_proj"], at(g, "l0_proj", 6 * n + 5 + t))
                    V.tensor_tensor(v0[:, t, :], ring[t][:], row("l0_bv"), ALU.add).then_inc(sem[f"ring{t}"], 1)

            def l0_max(g, n, h):
                dve.wait_ge(sem["l0_S"], at(g, "l0_S", 8 * n + h + 1))
                V.tensor_reduce(nm0[:, h % 2, :], two(ring[h % 2][:]), AX, ALU.max, negate=True).then_inc(sem["l0_nm"], 1)

            def l0_pt(g, n, h):
                dve.wait_ge(sem["l0_T"], at(g, "l0_T", 8 * n + h + 1))
                dve.wait_ge(sem["l0_AV"], at(g, "l0_AV", 8 * n + h - 1))
                V.tensor_copy(pt0[:, h % 2], two(ptp[:])).then_inc(sem["l0_pt"], 1)

            def l0_y(g, n, q):
                dve.wait_ge(sem["l0_AV"], at(g, "l0_AV", 8 * n + 4 * q + 4))
                s = slice(4 * q, 4 * q + 4)
                V.reciprocal(rr0[:, s, :], rs0[:, s, :]).then_inc(vec_l0_step, 1)
                dve.wait_ge(vec_l0_step, l0_steps.next())
                V.tensor_tensor(y0[:].rearrange("p q (h d) -> p h q d", d=D0)[:, s], yp[:].rearrange("p (h q d) -> p h q d", h=4, q=2),
                                    rr0[:, s, :].unsqueeze(3).to_broadcast([P, 4, 2, D0]), ALU.mult).then_inc(sem["l0_y"], 1)

            def l0_x1(g, n):
                r = slice(L * (n % 2), L * (n % 2) + L)
                dve.wait_ge(sem["l0_out"], at(g, "l0_out", n + 1))
                V.scalar_tensor_tensor(x1[r, n // 2, :], ptp[r, 0:C], cols[r, COLS["l0_bo"][0]:COLS["l0_bo"][0] + 1], x_t[r, n // 2, :],
                                           ALU.add, ALU.add).then_inc(sem["l0_x1"], 1)

            def l0_batch(g, n):
                if n % 2 == 0:
                    l0_norm(g, n // 2)
                l0_v(g, n)
                for i in range(H0 + 1):
                    if i < H0:
                        l0_max(g, n, i)
                    if i >= 1:
                        l0_pt(g, n, i - 1)
                        if i == 6:
                            l0_y(g, n, 0)
                l0_y(g, n, 1)
                l0_x1(g, n)

            def norm(g, k):
                for p in range(PAIRS):
                    last = V.bn_stats(bst[:, p, :], xr[:, p, :])
                last.then_inc(vec_step, 1)
                dve.wait_ge(vec_step, steps.next())
                V.memset(st0[:, 15:16], 0.0)
                for p in range(PAIRS):
                    last = V.bn_aggr(mv[:, p, :], bst[:, p, :])
                last.then_inc(vec_step, 1)
                dve.wait_ge(vec_step, steps.next())
                V.tensor_scalar(ve[:], mv[:, :, 1], EPS, None, ALU.add).then_inc(sem["ln_var"], 1)
                dve.wait_ge(sem["ln_rstd"], at(g, "ln_rstd", k))
                for p in range(PAIRS):
                    last = V.tensor_scalar(xh[:, p, :], xr[:, p, :], mv[:, p, 0:1], rstd[:, p:p + 1], ALU.subtract, ALU.mult)
                last.then_inc(sem["ln_xh"], 1)

            def shift(g, k, row_of_state):
                dve.wait_ge(sem["ctxT"], at(g, "ctxT", 1))
                V.tensor_copy(xs[:, :, :, 0], ctxT[:].rearrange("p t (b l) -> p t b l", l=L)[:, :, :, row_of_state]).then_inc(vec_step, 1)
                dve.wait_ge(vec_step, steps.next())
                dve.wait_ge(sem["ln_out"], at(g, "ln_out", k))
                xf = xs[:].rearrange("p t b l -> p (t b) l")
                V.tensor_tensor(sx[:].rearrange("p t (b l) -> p (t b) l", l=L), xf[:, :, 0:L], xf[:, :, 1:L + 1], ALU.subtract).then_inc(vec_step, 1)
                dve.wait_ge(vec_step, steps.next())

            def bl(ap):
                return ap.rearrange("p (b l) -> p b l", l=L)

            def lerp(dst, name):
                for t in range(CT):
                    last = V.scalar_tensor_tensor(bl(dst[:, t, :]), bl(sx[:, t, :]), col(name, t), xs[:, t, :, 1:L + 1], ALU.mult, ALU.add)
                return last

            def flat(t):
                return t[:].rearrange("p a b -> p (a b)")

            def layer1(g):
                dve.wait_ge(sem["l0_x1"], at(g, "l0_x1", 4))
                V.tensor_copy(flat(xr), flat(x1)).then_inc(vec_step, 1)
                dve.wait_ge(vec_step, steps.next())
                norm(g, 1)
                shift(g, 1, 1)
                lerp(xx, "maa_x").then_inc(sem["xxx"], 1)
                for f, name in enumerate(("maa_w", "maa_k", "maa_v", "maa_r", "maa_g")):
                    dve.wait_ge(sem["mix_p"], at(g, "mix_p", f + 1))
                    for t in range(CT):
                        last = V.scalar_tensor_tensor(mix[:, f, t, :], R[(f + 1) % 4][:, t * TOK:(t + 1) * TOK], col(name, t), sx[:, t, :], ALU.add, ALU.mult)
                    last.then_inc(sem["mix_tmp"], 1)
                dve.wait_ge(sem["rkv"], at(g, "rkv", 3))
                for t in range(CT):
                    last = V.scalar_tensor_tensor(yc[:, t, :], rT[:, t, :], col("faaaa", t), kT[:, t, :], ALU.mult, ALU.mult)
                last.then_inc(sem["ruk"], 1)
                dve.wait_ge(ld_s0, g * 32 + 32)
                for t in range(CT):
                    last = V.tensor_copy(av[:, t, :, :, 0], s0t[:, :, t, :].rearrange("p b s -> p s b"))
                last.then_inc(vec_step, 1)
                dve.wait_ge(vec_step, steps.next())

                def outer(t, j):
                    dve.wait_ge(sem["spread_p"], at(g, "spread_p", 4 * t + j + 1))
                    k = 4 * t + j
                    vb = R[1 + k % 2][:].rearrange("p (s b l) -> p s b l", s=2, l=L)[:, :, :, 0:L - 1]
                    kk = bl(kT[:, t, :]).unsqueeze(1).to_broadcast([P, 2, G, L])[:, :, :, 0:L - 1]
                    V.tensor_tensor(av[:, t, 2 * j:2 * j + 2, :, 1:L], vb, kk, ALU.mult).then_inc(sem["wkv_a"], 1)

                def scans(t, j):
                    dve.wait_ge(sem["wkv_a"], at(g, "wkv_a", 4 * t + j + 1))
                    for i in range(2):
                        s = av[:, t, 2 * j + i].rearrange("p b l -> p (b l)")
                        V.tensor_tensor_scan(s, wsh[:, t].rearrange("p b l -> p (b l)"), s, 0.0, ALU.mult, ALU.add).then_inc(sem["wkv_s"], 1)

                dve.wait_ge(sem["decw"], at(g, "decw", 1))
                outer(0, 0)
                outer(0, 1)
                for k in range(8):
                    scans(k // 4, k % 4)
                    if k + 2 < 8:
                        outer((k + 2) // 4, (k + 2) % 4)
                    if k == 1:
                        dve.wait_ge(sem["ruk_p"], at(g, "ruk_p", 1))
                        V.tensor_tensor(flat(ybon), R[0][:], flat(vT), ALU.mult).then_inc(sem["bonus"], 1)
                    if k == 3:
                        dve.wait_ge(sem["eg"], at(g, "eg", 1))
                        V.tensor_scalar(flat(sg), flat(sg), 0.5, 0.5, ALU.mult, ALU.add).then_inc(vec_step, 1)
                        dve.wait_ge(vec_step, steps.next())
                        V.tensor_tensor(flat(sg), R[3][:], flat(sg), ALU.mult).then_inc(sem["silu"], 1)
                dve.wait_ge(sem["bonus"], at(g, "bonus", 1))
                for t in range(CT):
                    dve.wait_ge(sem["wkv_yp"], at(g, "wkv_yp", t + 1))
                    V.tensor_tensor(yc[:, t, :], R[3][:, t * TOK:(t + 1) * TOK], ybon[:, t, :], ALU.add).then_inc(sem["wkv_y"], 1)
                dve.wait_ge(sem["gm_p"], at(g, "gm_p", 1))
                V.tensor_tensor(flat(yc), flat(yc), R[0][:], ALU.subtract).then_inc(sem["gd"], 1)
                dve.wait_ge(sem["gv_p"], at(g, "gv_p", 1))
                V.tensor_scalar(flat(gq), R[1][:], EPS, None, ALU.add).then_inc(sem["gve"], 1)
                dve.wait_ge(sem["grs"], at(g, "grs", 1))
                V.reciprocal(flat(gq), flat(gq)).then_inc(vec_step, 1)
                dve.wait_ge(vec_step, steps.next())
                dve.wait_ge(sem["silu"], at(g, "silu", 1))
                for t in range(CT):
                    last = V.scalar_tensor_tensor(yc[:, t, :], yc[:, t, :], col("gn_w", t), gq[:, t, :], ALU.mult, ALU.mult)
                last.then_inc(vec_step, 1)
                dve.wait_ge(vec_step, steps.next())
                for t in range(CT):
                    last = V.scalar_tensor_tensor(yc[:, t, :], yc[:, t, :], col("gn_b", t), sg[:, t, :], ALU.add, ALU.mult)
                last.then_inc(sem["yg"], 1)
                dve.wait_ge(sem["wo_p"], at(g, "wo_p", 1))
                V.tensor_tensor(flat(xr), R[2][:], flat(xr), ALU.add).then_inc(sem["x2"], 1)
                dve.wait_ge(sem["x2"], at(g, "x2", 1))
                norm(g, 2)
                shift(g, 2, 0)
                lerp(mix[:, 0], "fmaa_k")
                lerp(mix[:, 1], "fmaa_r").then_inc(sem["ffn_in"], 1)
                dve.wait_ge(sem["fk_p"], at(g, "fk_p", 1))
                V.tensor_scalar(mix[:, 3].rearrange("p a b -> p (a b)"), R[0][:], 0.0, None, ALU.max).then_inc(sem["frelu"], 1)
                dve.wait_ge(sem["fe"], at(g, "fe", 1))
                V.tensor_scalar(flat(e1), flat(e1), 0.5, 0.5, ALU.mult, ALU.add).then_inc(vec_step, 1)
                dve.wait_ge(vec_step, steps.next())
                dve.wait_ge(sem["fv_p"], at(g, "fv_p", 1))
                V.tensor_tensor(flat(tmp), R[2][:], flat(e1), ALU.mult).then_inc(vec_step, 1)
                dve.wait_ge(vec_step, steps.next())
                V.tensor_tensor(flat(xr), flat(xr), flat(tmp), ALU.add).then_inc(sem["x3"], 1)
                dve.wait_ge(sem["x3"], at(g, "x3", 1))

            def attention(g, a):
                norm(g, 3 + a)
                dve.wait_ge(sem["qkv_p"], at(g, "qkv_p", 3 * a + 1))
                for t in range(CT):
                    for e, parity in enumerate(("even_head", "odd_head")):
                        last = V.tensor_scalar(kbd[:, t, e, :], R[1][:, t * TOK:(t + 1) * TOK], col(("sa_bk", "ca_bk")[a], t), col(parity),
                                               ALU.add, ALU.mult)
                last.then_inc(sem["k_bd"], 1)
                dve.wait_ge(sem["qkv_p"], at(g, "qkv_p", 3 * a + 2))
                dve.wait_ge(sem["v_bd"], at(g, "v_bd", a))
                V.tensor_tensor(vsb, two(R[2][:]), row(("sa_bv", "ca_bv")[a]).unsqueeze(1).to_broadcast([P, PAIRS, C]), ALU.add).then_inc(sem["v_sb"], 1)
                if a == 1:
                    dve.wait_ge(ld_cmask, g * 32 + 32)
                    V.tensor_scalar(crossm[:], cmask[:], 0.25, None, ALU.mult)
                    V.tensor_scalar(crossb[:], cmask[:], 10000.0, -10000.0, ALU.mult, ALU.add).then_inc(sem["cmask"], 1)
                    dve.wait_ge(sem["cmask"], at(g, "cmask", 1))
                for r4 in range(4):
                    dve.wait_ge(sem["s_p"], at(g, "s_p", 4 * a + r4 + 1))
                    if a == 0:
                        last = V.tensor_tensor(pb[:, r4], R[r4][:].rearrange("p (h k) -> p h k", k=L),
                                               selfm[:].unsqueeze(1).to_broadcast([P, 8, L]), ALU.mult)
                    else:
                        last = V.tensor_tensor(pb[:, r4].rearrange("p (r h) k -> p r h k", r=PAIRS), R[r4][:].rearrange("p (r h k) -> p r h k", r=PAIRS, k=L),
                                               crossm[:].unsqueeze(2).to_broadcast([P, PAIRS, 4, L]), ALU.mult)
                    last.then_inc(sem["mskd"], 1)
                vh = vsb.rearrange("p r (h e d) -> p r h e d", e=2, d=D2)
                vw = vsw[:].rearrange("p r (h e d) -> p r h e d", e=2, d=D2)
                vo = vbd[:].rearrange("p (r b) h e d -> p r b h e d", b=2)
                V.tensor_copy(vo[0:L, :, 0, :, 0, 0:D2], vh[0:L, :, :, 0, :])
                V.tensor_copy(vo[L:P, :, 1, :, 1, 0:D2], vh[L:P, :, :, 1, :])
                dve.wait_ge(v_swap, g * 64 + 32 * (a + 1))
                V.tensor_copy(vo[0:L, :, 1, :, 0, 0:D2], vw[0:L, :, :, 0, :])
                V.tensor_copy(vo[L:P, :, 0, :, 1, 0:D2], vw[L:P, :, :, 1, :]).then_inc(sem["v_bd"], 1)
                for r4 in range(4):
                    dve.wait_ge(sem["mbias"], at(g, "mbias", 4 * a + r4 + 1))
                    V.tensor_reduce(mx[:, r4, :], pb[:, r4], AX, ALU.max).then_inc(vec_step, 1)
                    dve.wait_ge(vec_step, steps.next())
                    V.tensor_tensor(pb[:, r4], pb[:, r4], mx[:, r4, :].unsqueeze(2).to_broadcast([P, 8, L]), ALU.subtract).then_inc(sem["sub"], 1)
                for r4 in (1, 3):
                    dve.wait_ge(sem["pt_p"], at(g, "pt_p", 4 * a + r4 + 1))
                    V.tensor_copy(ptb[:, r4].rearrange("p a b -> p (a b)"), R[r4][:]).then_inc(sem["pt_v"], 1)
                for p in range(PAIRS):
                    dve.wait_ge(sem["av_p"], at(g, "av_p", 2 * a + p + 1))
                    y = R[p][:, 0:H2 * KV].rearrange("p (h d) -> p h d", d=KV)
                    V.reciprocal(rc[:, p, :], y[:, :, D2]).then_inc(vec_step, 1)
                    dve.wait_ge(vec_step, steps.next())
                    V.tensor_tensor(cx[:, p, :].rearrange("p (h d) -> p h d", d=D2), y[:, :, 0:D2],
                                        rc[:, p, :].unsqueeze(2).to_broadcast([P, H2, D2]), ALU.mult).then_inc(sem["cx"], 1)
                dve.wait_ge(sem["ao_p"], at(g, "ao_p", a + 1))
                V.tensor_tensor(tmp[:], two(R[3][:]), row(("sa_bo", "ca_bo")[a]).unsqueeze(1).to_broadcast([P, PAIRS, C]), ALU.add).then_inc(vec_step, 1)
                dve.wait_ge(vec_step, steps.next())
                V.tensor_tensor(flat(xr), flat(xr), flat(tmp), ALU.add).then_inc(sem["ao"], 1)
                dve.wait_ge(sem["ao"], at(g, "ao", a + 1))

            def mlp(g):
                norm(g, 5)
                for c in range(4):
                    dve.wait_ge(sem["h1_p"], at(g, "h1_p", c + 1))
                    for i in range(2):
                        j = 2 * c + i
                        last = V.tensor_scalar(ub[:, j, :], R[c][:, i * TOK:(i + 1) * TOK], col("b1", j), None, ALU.add)
                    last.then_inc(sem["u"], 1)
                for c in range(4):
                    dve.wait_ge(sem["usq"], at(g, "usq", c + 1))
                    s = slice(2 * c, 2 * c + 2)
                    V.tensor_scalar(tb[:, s, :], tb[:, s, :], 0.044715, 1.0, ALU.mult, ALU.add).then_inc(sem["ut"], 1)
                for c in range(4):
                    dve.wait_ge(sem["uth"], at(g, "uth", c + 1))
                    s = slice(2 * c, 2 * c + 2)
                    V.scalar_tensor_tensor(tb[:, s, :], tb[:, s, :], 1.0, ub[:, s, :], ALU.add, ALU.mult).then_inc(sem["ug"], 1)
                dve.wait_ge(sem["w2_p"], at(g, "w2_p", 1))
                for p in range(PAIRS):
                    last = V.scalar_tensor_tensor(tmp[:, p, :], R[0][:, p * C:(p + 1) * C], 0.5, row("b2"), ALU.mult, ALU.add)
                last.then_inc(vec_step, 1)
                dve.wait_ge(vec_step, steps.next())
                V.tensor_tensor(flat(xr), flat(xr), flat(tmp), ALU.add).then_inc(sem["x5"], 1)

            def layer3(g):
                dve.wait_ge(sem["x3qk_p"], at(g, "x3qk_p", 1))
                V.tensor_copy(kbd[:, 0].rearrange("p a b -> p (a b)"), R[2][:]).then_inc(sem["x3k"], 1)
                dve.wait_ge(sem["x3qk_p"], at(g, "x3qk_p", 2))
                V.tensor_copy(v3[:].rearrange("p a b -> p (a b)"), R[3][:]).then_inc(sem["x3v"], 1)
                dve.wait_ge(sem["s3_p"], at(g, "s3_p", 1))
                for b2 in range(2):
                    r = slice(L * b2, L * b2 + L)
                    last = V.tensor_reduce(nm3[r, :], R[0][r, 0:PAIRS * P].rearrange("p (r e k) -> p r e k", r=PAIRS, k=L)[:, :, b2, :], AX, ALU.max, negate=True)
                last.then_inc(vec_step, 1)
                dve.wait_ge(vec_step, steps.next())
                V.tensor_scalar(nm3[:], nm3[:], 0.0625, None, ALU.mult).then_inc(sem["nm3"], 1)
                dve.wait_ge(sem["e3"], at(g, "e3", 1))
                V.reciprocal(rc3[:], sm3[:]).then_inc(vec_step, 1)
                dve.wait_ge(vec_step, steps.next())
                for p in range(PAIRS):
                    last = V.tensor_scalar(p3[:, p, :], p3[:, p, :], rc3[:, p:p + 1], None, ALU.mult)
                last.then_inc(sem["pn3"], 1)
                dve.wait_ge(sem["d3_p"], at(g, "d3_p", 1))
                for p in range(PAIRS):
                    last = V.scalar_tensor_tensor(xo[:, p, :], R[3][:, p * C:(p + 1) * C], col("alpha"), xr[:, p, :], ALU.mult, ALU.add)
                last.then_inc(sem["xo"], 1)

            with dve.Fori(0, NG) as g:
                l0_steps.start(g)
                steps.start(g)
                for n in range(G):
                    l0_batch(g, n)
                l0_steps.end()
                layer1(g)
                attention(g, 0)
                attention(g, 1)
                mlp(g)
                layer3(g)
                steps.end()


def constants():
    import numpy as np
    i = np.arange(P)
    eye = np.eye(P, dtype=np.float32)
    mean64 = ((i[:, None] // L) == (i[None, :] // L)).astype(np.float32) / L
    sum8 = ((i[:, None] // S1) == (i[None, :] // S1)).astype(np.float32)
    spread = np.stack([sum8 * ((i[:, None] % S1) == t) for t in range(S1)], 1).astype(np.float32)
    gather = np.stack([sum8 * ((i[None, :] % S1) == t) for t in range(S1)], 1).astype(np.float32)
    return dict(ident=eye, mean64=mean64, sum8=sum8, mean8=sum8 / S1,
                spread=spread.reshape(P, -1), gather=gather.reshape(P, -1))


def kernel(**inputs):
    import numpy as np
    import concourse.bacc as bacc
    from concourse import mybir as mb
    from concourse.bass_utils import run_bass_kernel_spmd as run

    a = {k: np.asarray(v) for k, v in inputs.items()}
    l0 = {k[9:]: v for k, v in a.items() if k.startswith("L0_xattn_")}
    l1 = {k[9:]: v for k, v in a.items() if k.startswith("L1_xattn_")}
    l2 = {k[9:]: v for k, v in a.items() if k.startswith("L2_xattn_")}
    l3 = {k[9:]: v for k, v in a.items() if k.startswith("L3_xattn_")}

    def column(v):
        return np.reshape(v, (-1, P)).T

    def twice(v):
        return np.concatenate([v, v], 0)

    half = np.arange(P) // D2 % 2
    col = dict(l0_gamma=twice(l0["gamma"]), l0_beta=twice(l0["beta"]), l0_bq=l0["bq"], l0_bk=l0["bkv"][:512],
               l0_bo=twice(l0["bo"]), sa_s=l2["ln1_s"], sa_b=l2["ln1_b"], ca_s=l2["ln2_s"], ca_b=l2["ln2_b"],
               ml_s=l2["ln3_s"], ml_b=l2["ln3_b"], sa_bq=l2["b_qkv"][:C], sa_bk=l2["b_qkv"][C:2 * C],
               ca_bq=l2["b_q"], ca_bk=l2["b_kv"][:C], b1=l2["b1"], alpha=np.broadcast_to(l3["alpha"], (P,)),
               even_head=(half == 0).astype(np.float32), odd_head=(half == 1).astype(np.float32))
    cols = np.ascontiguousarray(np.concatenate([column(col[n] if n in col else l1[n]) for n in COLS], 1))
    row = dict(l0_bv=l0["bkv"][512:], sa_bv=l2["b_qkv"][2 * C:], sa_bo=l2["b_ao"], ca_bv=l2["b_kv"][C:], ca_bo=l2["b_co"], b2=l2["b2"])
    rows = np.ascontiguousarray(np.concatenate([row[n] for n in ROWS])[None])

    def tiles(m):
        return np.reshape(np.transpose(np.reshape(m, (-1, P, m.shape[1])), (1, 0, 2)), (P, -1))

    def padded(m):
        return np.concatenate([m, np.zeros((P - m.shape[0], m.shape[1]), m.dtype)], 0)

    w2 = np.reshape(l1["maa_w2"], (5 * DM, C))
    mats = dict(l0_q=twice(l0["Wq"].T), l0_k=twice(l0["Wkv"][:512].T), l0_v=twice(l0["Wkv"][512:].T), l0_o=tiles(l0["Wo"].T),
                maa_w1=tiles(l1["maa_w1"]), maa_w2=w2[:P], maa_w2g=padded(w2[P:]), dec_w1=tiles(l1["decay_w1"]), dec_w2=padded(l1["decay_w2"]),
                **{n: tiles(l1[n].T) for n in ("Wk", "Wv", "Wr", "Wg", "Wo", "fWk", "fWr", "fWv")},
                sa_q=tiles(l2["w_qkv"][:, :C]), sa_k=tiles(l2["w_qkv"][:, C:2 * C]), sa_v=tiles(l2["w_qkv"][:, 2 * C:]), sa_o=tiles(l2["w_ao"]),
                ca_q=tiles(l2["w_q"]), ca_k=tiles(l2["w_kv"][:, :C]), ca_v=tiles(l2["w_kv"][:, C:]), ca_o=tiles(l2["w_co"]),
                w1=tiles(l2["w1"]), w2=tiles(l2["w2"]),
                x_q=tiles(l3["w_q"].T), x_k=tiles(l3["w_k"].T), x_v=tiles(l3["w_v"].T), x_o=tiles(l3["w_o"].T), **constants())
    wts = np.ascontiguousarray(np.concatenate([mats[n] for n in WTS], 1))

    nc = bacc.Bacc("TRN2", target_bir_lowering=False, num_devices=1)
    arrays, args = {}, []
    for name, v in (("x", a["x"]), ("ctx", a["ctx_2048"]), ("mask_self", a["mask_1x1xSxS2_fc1"]), ("mask_cross", a["mask_Bx1xSxS2_ff1"]),
                    ("cols", cols), ("rows", rows), ("wts", wts)):
        v = np.ascontiguousarray(v)
        arrays[f"in_{name}_dram"] = v
        args.append(nc.dram_tensor(f"in_{name}_dram", v.shape, mb.dt.from_np(v.dtype), kind="ExternalInput").ap())
    args.append(nc.dram_tensor("out_0_dram", (B, L, C), mb.dt.float32, kind="ExternalOutput").ap())
    program(nc, *args)
    r = run(nc, [arrays], core_ids=[0])
    return r.results[0]["out_0_dram"]
```

```python
from contextlib import ExitStack

import concourse.bass as bass
from concourse import mybir

F32 = mybir.dt.float32
ALU = mybir.AluOpType
ACT = mybir.ActivationFunctionType
AX = mybir.AxisListType.X

P = 128
B, L, C = 64, 64, 256
CT = C // P
G = 4
NG = B // G
PAIRS = G // 2
TOK = G * L
EPS = 1e-5
H0, D0 = 8, 64
H1, S1 = 32, 8
H2, D2 = 16, 16
KV = D2 + 1
DM, DD = 32, 64
FF = 4 * C

COLS = {}
for _name, _n in (("l0_gamma", 1), ("l0_beta", 1), ("l0_bq", 4), ("l0_bk", 4), ("l0_bo", 1),
                  ("ln1_w", 2), ("ln1_b", 2), ("ln2_w", 2), ("ln2_b", 2), ("maa_x", 2),
                  ("maa_w", 2), ("maa_k", 2), ("maa_v", 2), ("maa_r", 2), ("maa_g", 2),
                  ("time_decay", 2), ("faaaa", 2), ("gn_w", 2), ("gn_b", 2), ("fmaa_k", 2), ("fmaa_r", 2),
                  ("sa_s", 2), ("sa_b", 2), ("ca_s", 2), ("ca_b", 2), ("ml_s", 2), ("ml_b", 2),
                  ("sa_bq", 2), ("sa_bk", 2), ("ca_bq", 2), ("ca_bk", 2), ("b1", 8), ("alpha", 1),
                  ("even_head", 1), ("odd_head", 1)):
    COLS[_name] = (sum(n for _, n in COLS.values()), _n)
N_COLS = sum(n for _, n in COLS.values())
ROWS = {}
for _name, _n in (("l0_bv", H0 * D0), ("sa_bv", C), ("sa_bo", C), ("ca_bv", C), ("ca_bo", C), ("b2", C)):
    ROWS[_name] = (sum(n for _, n in ROWS.values()), _n)
N_ROWS = sum(n for _, n in ROWS.values())
WTS = {}
for _name, _t, _n in (("l0_q", 2, 512), ("l0_k", 2, 512), ("l0_v", 2, 512), ("l0_o", 4, 64),
                      ("ident", 1, 128), ("mean64", 1, 128), ("sum8", 1, 128), ("mean8", 1, 128),
                      ("spread", 8, 128), ("gather", 8, 128),
                      ("maa_w1", 2, 160), ("maa_w2", 1, 256), ("maa_w2g", 1, 256), ("dec_w1", 2, 64), ("dec_w2", 1, 256),
                      ("Wk", 2, 256), ("Wv", 2, 256), ("Wr", 2, 256), ("Wg", 2, 256), ("Wo", 2, 256),
                      ("fWk", 2, 256), ("fWr", 2, 256), ("fWv", 2, 256),
                      ("sa_q", 2, 256), ("sa_k", 2, 256), ("sa_v", 2, 256), ("sa_o", 2, 256),
                      ("ca_q", 2, 256), ("ca_k", 2, 256), ("ca_v", 2, 256), ("ca_o", 2, 256),
                      ("w1", 2, 1024), ("w2", 8, 256),
                      ("x_q", 2, 256), ("x_k", 2, 256), ("x_v", 2, 256), ("x_o", 2, 256)):
    WTS[_name] = (sum(t * n for _, t, n in WTS.values()), _t, _n)
N_WTS = sum(t * n for _, t, n in WTS.values())

PER = dict(
    l0_stat=4, l0_mean=4, l0_var=2, l0_rstd=2, l0_xn=2, l0_proj=24, l0_S=32, l0_nm=32, l0_T=32, l0_pt=32,
    l0_AV=32, l0_y=8, l0_yT=8, l0_out=4, l0_x1=4, ring0=32, ring1=32,
    ctx_tr=1, ctxT=1,
    ln_var=5, ln_rstd=5, ln_xh=5, ln_T=6, ln_out=6, xr_free=1,
    xxx=1, maa_p=1, maa_t=1, mix_p=5, mix_tmp=5, mix_x=5,
    dech_p=1, dech=1, decw_p=1, decw=1, rkv_p=4, rkv=3, eg=1, silu=1,
    ruk=1, ruk_p=1, bonus=1, spread_p=8, wkv_a=8, wkv_s=16, wkv_p=8, wkv_yp=2, wkv_y=2,
    gm_p=1, gd=1, gsq=1, gv_p=1, gve=1, grs=1, yg=1, wo_p=1, x2=1,
    ffn_in=1, fk_p=1, frelu=1, fkk=1, fr_p=1, fe=1, fv_p=1, x3=1,
    qkv_p=6, q_T=2, k_bd=2, v_sb=2, v_bd=2, s_p=8, mskd=8, mbias=8, sub=8, pexp=8, pt_p=8, pt_a=4, pt_v=4,
    av_p=4, cx=4, cxT_p=2, cxT=2, ao_p=2, ao=2, cmask=1,
    h1_p=4, u=4, usq=4, ut=4, utu=4, uth=4, ug=4, w2_p=1, x5=1,
    x3qk_p=3, x3q=1, x3k=1, x3v=1, s3_p=1, nm3=1, e3=1, pn3=1, pt3_p=1, pt3=1, c3_p=1, c3=1, d3_p=1, xo=1,
)
HEAD_STEPS = H0 + 2
BATCH_PIECES = 1 + HEAD_STEPS + 1
PAIR_PIECES = 4 + 2 * BATCH_PIECES
PIECES = PAIRS * PAIR_PIECES
ATTENTION_POINTS = ("turn", "qkv", "scores_a", "scores", "softmax", "turned_a", "turned", "values", "ctx_turn", "out")
POINTS = ("ctx_turn", "ln1_turn", "token_mix_in", "token_mix", "decay_in", "keys", "values", "receptance", "gate",
          *(f"spread{k}" for k in range(1, 8)), "gather0", "gather1", "gn_mean", "gn_var", "gn_out", "wkv_out",
          "ln2_turn", "channel_mix_in", "channel_mix", *("self_" + p for p in ATTENTION_POINTS),
          *("cross_" + p for p in ATTENTION_POINTS), "mlp_turn", "mlp_in_a", "mlp_in", "gelu", "mlp_out",
          "x3_turn", "x3_q", "x3_scores", "x3_turned", "x3_ctx", "x3_out")
CHAIN = dict(vec_l0=18, vec=38, act=1)


def program(nc, x, ctx, mask_self, mask_cross, cols_d, rows_d, wts_d, out):
    with ExitStack() as es:
        def sb(name, *shape):
            return es.enter_context(nc.sbuf_tensor(name, [P, *shape], F32))

        sem = {n: es.enter_context(nc.semaphore(n)) for n in PER}
        vec_l0_step = es.enter_context(nc.semaphore("vec_l0_step"))
        vec_step = es.enter_context(nc.semaphore("vec_step"))
        act_step = es.enter_context(nc.semaphore("act_step"))
        ld_const = es.enter_context(nc.semaphore("ld_const"))
        ld_w = es.enter_context(nc.semaphore("ld_w"))
        ld_pair = [es.enter_context(nc.semaphore(f"ld_pair{p}")) for p in range(PAIRS)]
        ld_s0 = es.enter_context(nc.semaphore("ld_s0"))
        ld_cmask = es.enter_context(nc.semaphore("ld_cmask"))
        v_swap = es.enter_context(nc.semaphore("v_swap"))
        st_out = es.enter_context(nc.semaphore("st_out"))
        ready = es.enter_context(nc.semaphore("ready"))
        ready_pool = es.enter_context(nc.semaphore("ready_pool"))

        def at(g, name, k):
            return (g + 1) * PER[name] + k

        class Steps:
            def __init__(self, name):
                self.name, self.n = name, 0

            def start(self, g):
                self.g, self.n = g, 0

            def next(self):
                self.n += 1
                return self.g * CHAIN[self.name] + self.n

            def end(self):
                assert self.n == CHAIN[self.name], (self.name, self.n)

        cols = sb("cols", N_COLS)
        rows = sb("rows", N_ROWS)
        wts = sb("wts", N_WTS)

        def col(name, t=0):
            o = COLS[name][0] + t
            return cols[:, o:o + 1]

        def row(name):
            o, n = ROWS[name]
            return rows[:, o:o + n]

        def w(name, t=0):
            o, _, n = WTS[name]
            return wts[:, o + t * n:o + (t + 1) * n]

        ident = w("ident")
        bq8 = sb("bq8", 4)
        nhalf = sb("nhalf", 2 * TOK)
        selfm = sb("selfm", L)
        selfb = sb("selfb", L)
        x_t = sb("x_t", PAIRS, C)
        c_t = sb("c_t", PAIRS, C)
        st0 = sb("st0", 16)
        xn = sb("xn", C)
        q0 = sb("q0", 4, C)
        k0 = sb("k0", 4, C)
        v0 = sb("v0", 2, 512)
        nm0 = sb("nm0", 2, 2)
        p0 = sb("p0", 2, 2, C)
        pt0 = sb("pt0", 2, 2, C)
        rs0 = sb("rs0", H0, 2)
        rr0 = sb("rr0", H0, 2)
        y0 = sb("y0", 2, 512)
        yT0 = sb("yT0", 4, C)
        x1 = sb("x1", PAIRS, C)
        xr = sb("xr", PAIRS, C)
        bst = sb("bst", PAIRS, 6)
        mv = sb("mv", PAIRS, 2)
        ve = sb("ve", PAIRS)
        rstd = sb("rstd", PAIRS)
        xh = sb("xh", PAIRS, C)
        hT = sb("hT", CT, TOK)
        ctxT = sb("ctxT", CT, TOK)
        xs = sb("xs", CT, G, L + 1)
        sx = sb("sx", CT, TOK)
        tT = sb("tT", TOK)
        tg = sb("tg", TOK)
        mix = sb("mix", 5, CT, TOK)
        hd = sb("hd", TOK)
        e1 = sb("e1", CT, TOK)
        wsh = sb("wsh", CT, G, L)
        kT = sb("kT", CT, TOK)
        vT = sb("vT", CT, TOK)
        rT = sb("rT", CT, TOK)
        sg = sb("sg", CT, TOK)
        s0t = sb("s0t", G, CT, S1)
        av = sb("av", CT, S1, G, L)
        ybon = sb("ybon", CT, TOK)
        xx = ybon
        yc = sb("yc", CT, TOK)
        gq = sb("gq", CT, TOK)
        cmask = sb("cmask", PAIRS, L)
        crossm = sb("crossm", PAIRS, L)
        crossb = sb("crossb", PAIRS, L)
        kbd = sb("kbd", CT, 2, TOK)
        vsb = sb("vsb", PAIRS, C)[:]
        vsw = sb("vsw", PAIRS, C)
        vbd = sb("vbd", G, H2 // 2, 2, KV)
        pb = av[:, 0].rearrange("p a b c -> p (a b c)").rearrange("p (r h k) -> p r h k", r=4, k=L)
        mx = sb("mx", 4, 8)
        ptb = av[:, 1].rearrange("p a b c -> p (a b c)").rearrange("p (r j q) -> p r j q", r=4, q=P)
        rc = sb("rc", PAIRS, H2)
        cx = mix[:, 4]
        cT = mix[:, 3]
        tmp = gq
        ub = av[:, 0].rearrange("p a b c -> p (a b c)").rearrange("p (j t) -> p j t", j=8)
        tb = av[:, 1].rearrange("p a b c -> p (a b c)").rearrange("p (j t) -> p j t", j=8)
        p3 = sb("p3", PAIRS, P)
        nm3 = sb("nm3", PAIRS)
        sm3 = sb("sm3", PAIRS)
        rc3 = sb("rc3", PAIRS)
        pT3 = sb("pT3", PAIRS, P)
        v3 = mix[:, 2]
        xo = sb("xo", PAIRS, C)

        ring = [es.enter_context(nc.psum_tensor(f"ring{i}", [P, 512], F32)) for i in range(2)]
        ptp = es.enter_context(nc.psum_tensor("ptp", [P, 512], F32))
        yp = es.enter_context(nc.psum_tensor("yp", [P, 512], F32))
        R = [es.enter_context(nc.psum_tensor(f"R{i}", [P, 512], F32)) for i in range(4)]

        def two(ap):
            return ap.rearrange("p (a b) -> p a b", a=2)

        def piece_of(k):
            p, j = divmod(k, PAIR_PIECES)
            if j < 4:
                return p, j, None, None
            n, step = divmod(j - 4, BATCH_PIECES)
            return p, None, 2 * p + n, step

        class Along:
            def __init__(self, piece, g):
                self.piece, self.g, self.k = piece, g, 0

            def __call__(self, point):
                upto = (POINTS.index(point) + 1) * PIECES // len(POINTS)
                while self.piece is not None and self.k < upto:
                    self.piece(self.g, self.k)
                    self.k += 1

        block = es.enter_context(nc.Block())
        N_CONST = 4

        @block.sync
        def _(sp):
            for h in range(2):
                sp.dma_start(selfm[h * L:(h + 1) * L, :], mask_self[0, 0]).then_inc(ld_const, 16)
            sp.dma_start(cols[:], cols_d).then_inc(ld_const, 16)
            sp.dma_start(rows[:], rows_d.to_broadcast([P, N_ROWS])).then_inc(ld_const, 16)
            step = N_WTS // 4
            for i in range(4):
                hi = N_WTS if i == 3 else (i + 1) * step
                sp.dma_start(wts[:, i * step:hi], wts_d[:, i * step:hi]).then_inc(ld_w, 16)

            def loads(g, b0):
                for p in range(PAIRS):
                    sp.wait_ge(sem["l0_x1"], at(g, "l0_x1", 2 * (p + 1) - 4))
                    sp.dma_start(x_t[:, p, :], x[bass.ds(b0[p], 2)].rearrange("b l c -> (b l) c")).then_inc(ld_pair[p], 16)
                sp.wait_ge(sem["ctx_tr"], at(g, "ctx_tr", 0))
                for p in range(PAIRS):
                    sp.dma_start(c_t[:, p, :], ctx[bass.ds(b0[p], 2)].rearrange("b l c -> (b l) c")).then_inc(ld_pair[p], 16)

            def loads_rest(g, b0):
                sp.wait_ge(sem["wkv_s"], at(g, "wkv_s", 0))
                for t in range(CT):
                    for p in range(PAIRS):
                        s0src = ctx[bass.ds(b0[p], 2), 2:2 + S1, :].rearrange("b s c -> b (s c)")
                        sp.dma_start(s0t[:, 2 * p:2 * p + 2, t, :],
                                     s0src[:, t * P * S1:(t + 1) * P * S1].rearrange("b (p t) -> p b t", t=S1)).then_inc(ld_s0, 16)
                sp.wait_ge(sem["cmask"], at(g, "cmask", 0))
                for p in range(PAIRS):
                    sp.dma_start(cmask[:, p, :], mask_cross[bass.ds(b0[p], 2), 0].rearrange("b q k -> (b q) k")).then_inc(ld_cmask, 16)

            def swap(g, a):
                sp.wait_ge(sem["v_sb"], at(g, "v_sb", a + 1))
                sp.wait_ge(sem["v_bd"], at(g, "v_bd", a))
                sp.dma_start(vsw[0:L], vsb[L:P]).then_inc(v_swap, 16)
                sp.dma_start(vsw[L:P], vsb[0:L]).then_inc(v_swap, 16)

            def store(g):
                sp.wait_ge(sem["xo"], at(g, "xo", 1))
                of_group = out.rearrange("(n p b) l c -> n (b l) p c", n=NG, p=PAIRS)
                sp.dma_start(of_group[bass.ds(g, 1)].rearrange("n r p c -> (n r) p c"), xo[:]).then_inc(st_out, 16)

            def group(g, b0):
                loads_rest(g, b0)
                swap(g, 0)
                swap(g, 1)
                store(g)

            loads(0, (0, 2))
            with sp.Fori(0, NG - 1) as g:
                now = [sp.snap(g * G + 2 * p) for p in range(PAIRS)]
                following = [sp.snap(g * G + G + 2 * p) for p in range(PAIRS)]
                loads(g + 1, following)
                group(g, now)
            group(NG - 1, [(NG - 1) * G + 2 * p for p in range(PAIRS)])
            sp.wait_ge(st_out, (NG + 1) * 16)

        @block.tensor
        def _(pe):
            mm, tr = nc.tensor.matmul, nc.tensor.transpose
            pe.wait_ge(ld_w, 64)
            pe.wait_ge(ready, 2)
            use, first = [0], [0]

            def ring_use(g):
                u = use[0]
                use[0] += 1
                pe.wait_ge(sem[f"ring{u % 2}"], at(g, f"ring{u % 2}", u // 2))
                return ring[u % 2]

            def ring_done(g):
                u = use[0]
                pe.wait_ge(sem["ring0"], at(g, "ring0", (u + 1) // 2))
                pe.wait_ge(sem["ring1"], at(g, "ring1", u // 2))

            def l0_stats(g, p, j):
                if j == 0:
                    pe.wait_ge(sem["l0_y"], at(g, "l0_y", 4 * p))
                pe.wait_ge(sem["l0_stat"], at(g, "l0_stat", 2 * p + j + 1))
                mm(yp[:, j:j + 1], w("mean64"), st0[:, 6 + j:7 + j], start=True, stop=True).then_inc(sem["l0_mean"], 1)

            def l0_project(g, n):
                p = n // 2
                pe.wait_ge(ld_pair[p], g * 32 + 32)
                pe.wait_ge(sem["l0_xn"], at(g, "l0_xn", p + 1))
                for name, src in (("l0_q", xn[:]), ("l0_k", c_t[:, p, :])):
                    for j in range(2):
                        bank = ring_use(g)
                        for i in range(2):
                            m = 2 * j + i
                            last = mm(bank[:, i * C:(i + 1) * C], w(name, n % 2)[:, m * P:(m + 1) * P], src, start=True, stop=True)
                        last.then_inc(sem["l0_proj"], 1)
                for t in range(2):
                    bank = ring_use(g)
                    mm(bank[:, :], c_t[:, p, t * P:(t + 1) * P], w("l0_v", n % 2), start=True, stop=True).then_inc(sem["l0_proj"], 1)

            def l0_scores(g, n, h):
                r = slice(D0 * (h % 2), D0 * (h % 2) + D0)
                bank = ring_use(g)
                for t in range(2):
                    last = mm(bank[:, t * C:(t + 1) * C], q0[r, h // 2, t * P:(t + 1) * P], k0[r, h // 2, :], start=True, stop=True)
                last.then_inc(sem["l0_S"], 1)

            def l0_turn(g, n, h, u_use):
                pe.wait_ge(sem[f"ring{u_use % 2}"], at(g, f"ring{u_use % 2}", u_use // 2 + 1))
                pe.wait_ge(sem["l0_pt"], at(g, "l0_pt", 8 * n + h))
                if h == 0:
                    pe.wait_ge(sem["l0_x1"], at(g, "l0_x1", n))
                for kt in range(2):
                    for qt in range(2):
                        last = tr(ptp[:, kt * C + qt * P:kt * C + (qt + 1) * P], p0[:, h % 2, qt, kt * P:(kt + 1) * P], ident)
                last.then_inc(sem["l0_T"], 1)

            def l0_values(g, n, h):
                pe.wait_ge(sem["l0_pt"], at(g, "l0_pt", 8 * n + h + 1))
                if h % 4 == 0:
                    pe.wait_ge(sem["l0_y"], at(g, "l0_y", 2 * n + h // 4))
                for qt in range(2):
                    o = (h % 4) * P + qt * D0
                    for kt in range(2):
                        last = mm(yp[:, o:o + D0], pt0[:, h % 2, kt, qt * P:(qt + 1) * P], v0[:, kt, h * D0:(h + 1) * D0],
                                  start=kt == 0, stop=kt == 1)
                last.then_inc(sem["l0_AV"], 1)

            def l0_head_step(g, n, i):
                if i == 0:
                    ring_done(g)
                    first[0] = use[0]
                if i < H0:
                    l0_scores(g, n, i)
                if 1 <= i <= H0:
                    l0_turn(g, n, i - 1, first[0] + i - 1)
                if i >= 2:
                    l0_values(g, n, i - 2)

            def l0_output(g, n):
                r = slice(L * (n % 2), L * (n % 2) + L)
                pe.wait_ge(sem["l0_y"], at(g, "l0_y", 2 * n + 2))
                for j in range(2):
                    bank = ring_use(g)
                    for i in range(2):
                        for qt in range(2):
                            last = tr(bank[:, i * C + qt * P:i * C + (qt + 1) * P], y0[:, qt, (2 * j + i) * P:(2 * j + i + 1) * P], ident)
                    last.then_inc(sem["l0_yT"], 1)
                ring_done(g)
                for t in range(4):
                    last = mm(ptp[r, 0:C], w("l0_o", t), yT0[:, t, :], start=t == 0, stop=t == 3)
                last.then_inc(sem["l0_out"], 1)

            def l0_piece(g, k):
                p, part, n, step = piece_of(k)
                if k == 0:
                    use[0] = 0
                if part in (0, 1):
                    l0_stats(g, p, part)
                elif step == 0:
                    l0_project(g, n)
                elif step == BATCH_PIECES - 1:
                    l0_output(g, n)
                elif step is not None:
                    l0_head_step(g, n, step - 1)

            def turn(g, bank, src, name):
                for p in range(PAIRS):
                    for t in range(CT):
                        last = tr(bank[:, t * TOK + p * P:t * TOK + (p + 1) * P], src[:, p, t * P:(t + 1) * P], ident)
                last.then_inc(sem[name], 1)

            def channel_major(bank, wname, src, name):
                for o in range(CT):
                    for t in range(CT):
                        last = mm(bank[:, o * TOK:(o + 1) * TOK], w(wname, t)[:, o * P:(o + 1) * P], src[:, t, :],
                                  start=t == 0, stop=t == CT - 1)
                last.then_inc(sem[name], 1)

            def token_major(bank, wname, src, name, tiles=CT):
                for p in range(PAIRS):
                    for t in range(tiles):
                        last = mm(bank[:, p * C:(p + 1) * C], src[:, t, p * P:(p + 1) * P], w(wname, t),
                                  start=t == 0, stop=t == tiles - 1)
                last.then_inc(sem[name], 1)

            def layer1(g, along):
                for p in range(PAIRS):
                    pe.wait_ge(ld_pair[p], g * 32 + 32)
                pe.wait_ge(sem["c3"], at(g, "c3", 0))
                pe.wait_ge(sem["xo"], at(g, "xo", 0))
                turn(g, R[1], c_t, "ctx_tr")
                along("ctx_turn")
                pe.wait_ge(sem["ln_xh"], at(g, "ln_xh", 1))
                turn(g, R[0], xh, "ln_T")
                along("ln1_turn")
                pe.wait_ge(sem["xxx"], at(g, "xxx", 1))
                for t in range(CT):
                    mm(R[0][:, 0:TOK], w("maa_w1", t)[:, 0:P], xx[:, t, :], start=t == 0, stop=t == 1)
                for t in range(CT):
                    last = mm(R[0][0:DM, TOK:2 * TOK], w("maa_w1", t)[:, P:P + DM], xx[:, t, :], start=t == 0, stop=t == 1)
                last.then_inc(sem["maa_p"], 1)
                along("token_mix_in")
                pe.wait_ge(sem["maa_t"], at(g, "maa_t", 1))
                pe.wait_ge(sem["ctxT"], at(g, "ctxT", 1))
                for f in range(5):
                    if f == 4:
                        along("token_mix")
                        pe.wait_ge(sem["mix_tmp"], at(g, "mix_tmp", 1))
                    bank = R[(f + 1) % 4]
                    for o in range(CT):
                        if f < 4:
                            r = slice(DM * f, DM * (f + 1))
                            last = mm(bank[:, o * TOK:(o + 1) * TOK], w("maa_w2")[r, o * P:(o + 1) * P], tT[r, :], start=True, stop=True)
                        else:
                            last = mm(bank[:, o * TOK:(o + 1) * TOK], w("maa_w2g")[0:DM, o * P:(o + 1) * P], tg[0:DM, :], start=True, stop=True)
                    last.then_inc(sem["mix_p"], 1)
                pe.wait_ge(sem["mix_x"], at(g, "mix_x", 1))
                pe.wait_ge(sem["mix_tmp"], at(g, "mix_tmp", 2))
                for t in range(CT):
                    last = mm(R[2][0:DD, 0:TOK], w("dec_w1", t), mix[:, 0, t, :], start=t == 0, stop=t == 1)
                last.then_inc(sem["dech_p"], 1)
                along("decay_in")
                pe.wait_ge(sem["mix_x"], at(g, "mix_x", 2))
                pe.wait_ge(sem["mix_tmp"], at(g, "mix_tmp", 4))
                channel_major(R[0], "Wk", mix[:, 1], "rkv_p")
                along("keys")
                pe.wait_ge(sem["dech"], at(g, "dech", 1))
                for o in range(CT):
                    last = mm(R[3][:, o * TOK:(o + 1) * TOK], w("dec_w2")[0:DD, o * P:(o + 1) * P], hd[0:DD, :], start=True, stop=True)
                last.then_inc(sem["decw_p"], 1)
                pe.wait_ge(sem["mix_x"], at(g, "mix_x", 3))
                pe.wait_ge(sem["mix_tmp"], at(g, "mix_tmp", 5))
                channel_major(R[1], "Wv", mix[:, 2], "rkv_p")
                along("values")
                pe.wait_ge(sem["mix_x"], at(g, "mix_x", 4))
                channel_major(R[2], "Wr", mix[:, 3], "rkv_p")
                along("receptance")
                pe.wait_ge(sem["mix_x"], at(g, "mix_x", 5))
                pe.wait_ge(sem["decw"], at(g, "decw", 1))
                channel_major(R[3], "Wg", mix[:, 4], "rkv_p")
                pe.wait_ge(sem["ruk"], at(g, "ruk", 1))
                for o in range(CT):
                    last = mm(R[0][:, o * TOK:(o + 1) * TOK], w("sum8"), yc[:, o, :], start=True, stop=True)
                last.then_inc(sem["ruk_p"], 1)

                def spread(k):
                    if k >= 2:
                        pe.wait_ge(sem["wkv_a"], at(g, "wkv_a", k - 1))
                    else:
                        pe.wait_ge(sem["rkv"], at(g, "rkv", 3))
                    bank = R[1 + k % 2]
                    for i in range(2):
                        last = mm(bank[:, i * TOK:(i + 1) * TOK], w("spread", 2 * (k % 4) + i), vT[:, k // 4, :], start=True, stop=True)
                    last.then_inc(sem["spread_p"], 1)

                def gather(t):
                    if t == 0:
                        pe.wait_ge(sem["silu"], at(g, "silu", 1))
                    for j in range(4):
                        pe.wait_ge(sem["wkv_p"], at(g, "wkv_p", 4 * t + j + 1))
                        for i in range(2):
                            s = 2 * j + i
                            last = mm(R[3][:, t * TOK:(t + 1) * TOK], w("gather", s), av[:, t, s].rearrange("p b l -> p (b l)"),
                                      start=s == 0, stop=s == 7)
                    last.then_inc(sem["wkv_yp"], 1)

                along("gate")
                spread(0)
                for k in range(1, 8):
                    spread(k)
                    along(f"spread{k}")
                gather(0)
                along("gather0")
                pe.wait_ge(sem["wkv_y"], at(g, "wkv_y", 1))
                gather(1)
                along("gather1")
                pe.wait_ge(sem["wkv_y"], at(g, "wkv_y", 2))
                pe.wait_ge(sem["bonus"], at(g, "bonus", 1))
                mm(R[0][:, :], w("mean8"), yc[:].rearrange("p a b -> p (a b)"), start=True, stop=True).then_inc(sem["gm_p"], 1)
                along("gn_mean")
                pe.wait_ge(sem["gsq"], at(g, "gsq", 1))
                mm(R[1][:, :], w("mean8"), gq[:].rearrange("p a b -> p (a b)"), start=True, stop=True).then_inc(sem["gv_p"], 1)
                along("gn_var")
                along("gn_out")
                pe.wait_ge(sem["yg"], at(g, "yg", 1))
                token_major(R[2], "Wo", yc, "wo_p")
                along("wkv_out")
                pe.wait_ge(sem["ln_xh"], at(g, "ln_xh", 2))
                turn(g, R[0], xh, "ln_T")
                along("ln2_turn")
                pe.wait_ge(sem["ffn_in"], at(g, "ffn_in", 1))
                channel_major(R[0], "fWk", mix[:, 0], "fk_p")
                token_major(R[1], "fWr", mix[:, 1], "fr_p")
                along("channel_mix_in")
                pe.wait_ge(sem["fkk"], at(g, "fkk", 1))
                token_major(R[2], "fWv", mix[:, 2], "fv_p")
                along("channel_mix")

            def attention(g, a, along):
                at_point = ("self_", "cross_")[a]
                q, k, v, o = (("sa_q", "sa_k", "sa_v", "sa_o"), ("ca_q", "ca_k", "ca_v", "ca_o"))[a]
                src = hT if a == 0 else ctxT
                pe.wait_ge(sem["ln_xh"], at(g, "ln_xh", 3 + a))
                turn(g, R[0], xh, "ln_T")
                along(at_point + "turn")
                if a == 0:
                    pe.wait_ge(sem["ln_out"], at(g, "ln_out", 3))
                channel_major(R[1], k, src, "qkv_p")
                token_major(R[2], v, src, "qkv_p")
                pe.wait_ge(sem["ln_out"], at(g, "ln_out", 3 + a))
                channel_major(R[0], q, hT, "qkv_p")
                along(at_point + "qkv")
                pe.wait_ge(sem["q_T"], at(g, "q_T", a + 1))
                pe.wait_ge(sem["k_bd"], at(g, "k_bd", a + 1))
                pe.wait_ge(sem["v_sb"], at(g, "v_sb", a + 1))
                for r4 in range(4):
                    r = slice(32 * r4, 32 * r4 + 32)
                    for b in range(G):
                        for t in range(CT):
                            oo = (b // 2) * C + t * P
                            last = mm(R[r4][L * (b % 2):L * (b % 2) + L, oo:oo + P], hTq[r, t, b * L:(b + 1) * L],
                                      kbd[r, t, :, b * L:(b + 1) * L], start=True, stop=True)
                    last.then_inc(sem["s_p"], 1)
                    if r4 == 1:
                        along(at_point + "scores_a")
                along(at_point + "scores")
                along(at_point + "softmax")
                for r4 in range(4):
                    pe.wait_ge(sem["pexp"], at(g, "pexp", 4 * a + r4 + 1))
                    for j in range(4):
                        last = tr(R[r4][:, j * P:(j + 1) * P], pb[:, r4, 2 * j:2 * j + 2, :].rearrange("p a b -> p (a b)"), ident)
                    last.then_inc(sem["pt_p"], 1)
                    if r4 == 1:
                        along(at_point + "turned_a")
                along(at_point + "turned")
                pe.wait_ge(sem["pt_a"], at(g, "pt_a", 2 * a + 2))
                pe.wait_ge(sem["pt_v"], at(g, "pt_v", 2 * a + 2))
                pe.wait_ge(sem["v_bd"], at(g, "v_bd", a + 1))
                for p in range(PAIRS):
                    for b2 in range(2):
                        for t in range(CT):
                            for r4 in range(4):
                                hp = t * 4 + r4
                                last = mm(R[p][L * b2:L * b2 + L, hp * 2 * KV:(hp + 1) * 2 * KV],
                                          ptb[:, r4, 2 * p + t, L * b2:L * b2 + L],
                                          vbd[:, 2 * p + b2, hp].rearrange("p a b -> p (a b)"), start=True, stop=True)
                    last.then_inc(sem["av_p"], 1)
                along(at_point + "values")
                pe.wait_ge(sem["cx"], at(g, "cx", 2 * a + 2))
                turn(g, R[2], cx, "cxT_p")
                along(at_point + "ctx_turn")
                pe.wait_ge(sem["cxT"], at(g, "cxT", a + 1))
                token_major(R[3], o, cT, "ao_p")
                along(at_point + "out")

            hTq = sx

            def mlp(g, along):
                pe.wait_ge(sem["ln_xh"], at(g, "ln_xh", 5))
                pe.wait_ge(sem["ao"], at(g, "ao", 2))
                turn(g, R[0], xh, "ln_T")
                along("mlp_turn")
                pe.wait_ge(sem["ln_out"], at(g, "ln_out", 5))
                for c in range(4):
                    for i in range(2):
                        j = 2 * c + i
                        for t in range(CT):
                            last = mm(R[c][:, i * TOK:(i + 1) * TOK], w("w1", t)[:, j * P:(j + 1) * P], hT[:, t, :],
                                      start=t == 0, stop=t == 1)
                    last.then_inc(sem["h1_p"], 1)
                    if c == 1:
                        along("mlp_in_a")
                along("mlp_in")
                along("gelu")
                pe.wait_ge(sem["ug"], at(g, "ug", 4))
                token_major(R[0], "w2", tb, "w2_p", tiles=8)
                along("mlp_out")

            def layer3(g, along):
                channel_major(R[2], "x_k", ctxT, "x3qk_p")
                token_major(R[3], "x_v", ctxT, "x3qk_p")
                pe.wait_ge(sem["x5"], at(g, "x5", 1))
                turn(g, R[0], xr, "ln_T")
                along("x3_turn")
                pe.wait_ge(sem["ln_out"], at(g, "ln_out", 6))
                channel_major(R[1], "x_q", hT, "x3qk_p")
                along("x3_q")
                pe.wait_ge(sem["x3q"], at(g, "x3q", 1))
                pe.wait_ge(sem["x3k"], at(g, "x3k", 1))
                for b in range(G):
                    for t in range(CT):
                        o = (b // 2) * P + (b % 2) * L
                        last = mm(R[0][L * (b % 2):L * (b % 2) + L, o:o + L], sx[:, t, b * L:(b + 1) * L],
                                  kbd[:, 0, 0:2, :].rearrange("p a b -> p (a b)")[:, t * TOK + b * L:t * TOK + (b + 1) * L], start=t == 0, stop=t == 1)
                last.then_inc(sem["s3_p"], 1)
                along("x3_scores")
                pe.wait_ge(sem["pn3"], at(g, "pn3", 1))
                for p in range(PAIRS):
                    last = tr(R[1][:, p * P:(p + 1) * P], p3[:, p, :], ident)
                last.then_inc(sem["pt3_p"], 1)
                along("x3_turned")
                pe.wait_ge(sem["pt3"], at(g, "pt3", 1))
                pe.wait_ge(sem["x3v"], at(g, "x3v", 1))
                for p in range(PAIRS):
                    for t in range(CT):
                        last = mm(R[2][:, t * TOK + p * P:t * TOK + (p + 1) * P], v3[:, p, t * P:(t + 1) * P], pT3[:, p, :], start=True, stop=True)
                last.then_inc(sem["c3_p"], 1)
                along("x3_ctx")
                pe.wait_ge(sem["c3"], at(g, "c3", 1))
                token_major(R[3], "x_o", cT, "d3_p")
                along("x3_out")

            def group(g, along):
                layer1(g, along)
                attention(g, 0, along)
                attention(g, 1, along)
                mlp(g, along)
                layer3(g, along)
                along(POINTS[-1])

            for k in range(PIECES):
                l0_piece(0, k)
            with pe.Fori(0, NG - 1) as g:
                group(g, Along(l0_piece, g + 1))
            group(NG - 1, Along(None, None))

        @block.scalar
        def _(act):
            A = nc.scalar.activation
            steps = Steps("act")
            act.wait_ge(ld_const, 16 * N_CONST)
            act.wait_ge(ready, 2)

            def l0_qk(g, n):
                for i, (dst, scale) in enumerate(((q0, 0.125), (q0, 0.125), (k0, 1.0), (k0, 1.0))):
                    act.wait_ge(sem["l0_proj"], at(g, "l0_proj", 6 * n + i + 1))
                    for j in range(2):
                        m = 2 * (i % 2) + j
                        bias = bq8[:, m:m + 1] if i < 2 else col("l0_bk", m)
                        last = A(dst[:, m, :], ring[i % 2][:, j * C:(j + 1) * C], ACT.Identity, bias=bias, scale=scale)
                    last.then_inc(sem[f"ring{i % 2}"], 1)

            def l0_exp(g, n, h):
                u = 8 * n + h
                act.wait_ge(sem["l0_nm"], at(g, "l0_nm", u + 1))
                act.wait_ge(sem["l0_T"], at(g, "l0_T", u - 1))
                for qt in range(2):
                    last = A(p0[:, h % 2, qt, :], ring[h % 2][:, qt * C:(qt + 1) * C], ACT.Exp, bias=nm0[:, h % 2, qt:qt + 1],
                             accum_out=rs0[:, h, qt:qt + 1])
                last.then_inc(sem[f"ring{h % 2}"], 1)

            def l0_yT(g, n):
                for j in range(2):
                    act.wait_ge(sem["l0_yT"], at(g, "l0_yT", 2 * n + j + 1))
                    A(yT0[:, 2 * j:2 * j + 2, :], two(ring[j][:]), ACT.Copy).then_inc(sem[f"ring{j}"], 1)

            def norm_out(g, k, dst, scale, bias):
                act.wait_ge(sem["ln_T"], at(g, "ln_T", k))
                for t in range(CT):
                    last = A(dst(t), R[0][:, t * TOK:(t + 1) * TOK].rearrange("p (b l) -> p b l", l=L), ACT.Identity,
                             bias=col(bias, t), scale=col(scale, t))
                last.then_inc(sem["ln_out"], 1)

            def copy(dst, src, name):
                A(dst, src, ACT.Copy).then_inc(sem[name], 1)

            def flat(t):
                return t[:].rearrange("p a b -> p (a b)")

            def hT_out(t):
                return hT[:, t, :].rearrange("p (b l) -> p b l", l=L)

            def xs_out(t):
                return xs[:, t, :, 1:L + 1]

            def l0_piece(g, k):
                p, part, n, step = piece_of(k)
                if step == 0:
                    l0_qk(g, n)
                elif step == BATCH_PIECES - 1:
                    l0_yT(g, n)
                elif step is not None and step <= H0:
                    l0_exp(g, n, step - 1)

            def layer1(g, along):
                act.wait_ge(sem["ctx_tr"], at(g, "ctx_tr", 1))
                copy(flat(ctxT), R[1][:], "ctxT")
                along("ctx_turn")
                norm_out(g, 1, xs_out, "ln1_w", "ln1_b")
                along("ln1_turn")
                act.wait_ge(sem["maa_p"], at(g, "maa_p", 1))
                A(tT[:], R[0][:, 0:TOK], ACT.Tanh)
                A(tg[0:DM, :], R[0][0:DM, TOK:2 * TOK], ACT.Tanh).then_inc(sem["maa_t"], 1)
                along("token_mix_in")
                along("token_mix")
                act.wait_ge(sem["dech_p"], at(g, "dech_p", 1))
                A(hd[0:DD, :], R[2][0:DD, 0:TOK], ACT.Tanh).then_inc(sem["dech"], 1)
                along("decay_in")
                act.wait_ge(sem["rkv_p"], at(g, "rkv_p", 1))
                copy(flat(kT), R[0][:], "rkv")
                along("keys")
                act.wait_ge(sem["decw_p"], at(g, "decw_p", 1))
                for t in range(CT):
                    last = A(e1[:, t, :], R[3][:, t * TOK:(t + 1) * TOK], ACT.Exp, bias=col("time_decay", t))
                last.then_inc(act_step, 1)
                act.wait_ge(act_step, steps.next())
                for t in range(CT):
                    last = A(wsh[:, t, :, 1:L], e1[:, t, :].rearrange("p (b l) -> p b l", l=L)[:, :, 0:L - 1], ACT.Exp, scale=-1.0)
                last.then_inc(sem["decw"], 1)
                act.wait_ge(sem["rkv_p"], at(g, "rkv_p", 2))
                copy(flat(vT), R[1][:], "rkv")
                along("values")
                act.wait_ge(sem["rkv_p"], at(g, "rkv_p", 3))
                copy(flat(rT), R[2][:], "rkv")
                along("receptance")
                act.wait_ge(sem["rkv_p"], at(g, "rkv_p", 4))
                A(flat(sg), R[3][:], ACT.Tanh, scale=0.5).then_inc(sem["eg"], 1)
                along("gather1")
                act.wait_ge(sem["gd"], at(g, "gd", 1))
                A(flat(gq), flat(yc), ACT.Square).then_inc(sem["gsq"], 1)
                along("gn_mean")
                act.wait_ge(sem["gve"], at(g, "gve", 1))
                A(flat(gq), flat(gq), ACT.Sqrt).then_inc(sem["grs"], 1)
                along("gn_var")
                along("wkv_out")
                norm_out(g, 2, xs_out, "ln2_w", "ln2_b")
                along("ln2_turn")
                act.wait_ge(sem["frelu"], at(g, "frelu", 1))
                A(mix[:, 2], mix[:, 3], ACT.Square).then_inc(sem["fkk"], 1)
                act.wait_ge(sem["fr_p"], at(g, "fr_p", 1))
                A(flat(e1), R[1][:], ACT.Tanh, scale=0.5).then_inc(sem["fe"], 1)
                along("channel_mix_in")

            def attention(g, a, along):
                at_point = ("self_", "cross_")[a]
                along(("channel_mix", "self_out")[a])
                norm_out(g, 3 + a, hT_out, ("sa_s", "ca_s")[a], ("sa_b", "ca_b")[a])
                along(at_point + "turn")
                act.wait_ge(sem["qkv_p"], at(g, "qkv_p", 3 * a + 3))
                for t in range(CT):
                    last = A(sx[:, t, :], R[0][:, t * TOK:(t + 1) * TOK], ACT.Identity, bias=col(("sa_bq", "ca_bq")[a], t))
                last.then_inc(sem["q_T"], 1)
                along(at_point + "qkv")
                along(at_point + "scores_a")
                for r4 in range(4):
                    if r4 == 2:
                        along(at_point + "scores")
                    act.wait_ge(sem["sub"], at(g, "sub", 4 * a + r4 + 1))
                    pf = pb[:, r4].rearrange("p a b -> p (a b)")
                    A(pf, pf, ACT.Exp).then_inc(sem["pexp"], 1)
                for r4 in (0, 2):
                    if r4 == 0:
                        along(at_point + "softmax")
                    act.wait_ge(sem["pt_p"], at(g, "pt_p", 4 * a + r4 + 1))
                    copy(ptb[:, r4].rearrange("p a b -> p (a b)"), R[r4][:], "pt_a")
                    along(at_point + ("turned_a" if r4 == 0 else "turned"))
                along(at_point + "values")
                act.wait_ge(sem["cxT_p"], at(g, "cxT_p", a + 1))
                copy(flat(cT), R[2][:], "cxT")
                along(at_point + "ctx_turn")

            def mlp(g, along):
                along("cross_out")
                norm_out(g, 5, hT_out, "ml_s", "ml_b")
                along("mlp_turn")
                for c in range(4):
                    if c == 2:
                        along("mlp_in_a")
                    act.wait_ge(sem["u"], at(g, "u", c + 1))
                    A(tb[:, 2 * c:2 * c + 2, :], ub[:, 2 * c:2 * c + 2, :], ACT.Square).then_inc(sem["usq"], 1)
                for c in range(4):
                    if c == 0:
                        along("mlp_in")
                    act.wait_ge(sem["utu"], at(g, "utu", c + 1))
                    A(tb[:, 2 * c:2 * c + 2, :], tb[:, 2 * c:2 * c + 2, :], ACT.Tanh, scale=0.7978845608028654).then_inc(sem["uth"], 1)

            def layer3(g, along):
                along("mlp_out")
                act.wait_ge(sem["ln_T"], at(g, "ln_T", 6))
                copy(flat(hT), R[0][:], "ln_out")
                along("x3_turn")
                act.wait_ge(sem["x3qk_p"], at(g, "x3qk_p", 3))
                copy(flat(sx), R[1][:], "x3q")
                along("x3_q")
                act.wait_ge(sem["nm3"], at(g, "nm3", 1))
                for p in range(PAIRS):
                    for b2 in range(2):
                        r = slice(L * b2, L * b2 + L)
                        last = A(p3[r, p, L * b2:L * b2 + L], R[0][r, p * P + L * b2:p * P + L * b2 + L], ACT.Exp,
                                 bias=nm3[r, p:p + 1], scale=0.0625, accum_out=sm3[r, p:p + 1])
                last.then_inc(sem["e3"], 1)
                along("x3_scores")
                act.wait_ge(sem["pt3_p"], at(g, "pt3_p", 1))
                copy(flat(pT3), R[1][:, 0:PAIRS * P], "pt3")
                along("x3_turned")
                act.wait_ge(sem["c3_p"], at(g, "c3_p", 1))
                copy(flat(cT), R[2][:], "c3")

            def group(g, along):
                steps.start(g)
                layer1(g, along)
                attention(g, 0, along)
                attention(g, 1, along)
                mlp(g, along)
                layer3(g, along)
                along(POINTS[-1])
                steps.end()

            for k in range(PIECES):
                l0_piece(0, k)
            with act.Fori(0, NG - 1) as g:
                group(g, Along(l0_piece, g + 1))
            group(NG - 1, Along(None, None))

        @block.gpsimd
        def _(pool):
            GT = nc.gpsimd.tensor_tensor
            pool.memset(nhalf[:], -0.5)
            pool.memset(wsh[:, :, :, 0:1], 0.0)
            pool.memset(p3[:], 0.0).then_inc(ready_pool, 1)
            pool.wait_ge(ready_pool, 1)

            def l0_piece(g, k):
                p, part, n, step = piece_of(k)
                if part == 2:
                    pool.wait_ge(sem["l0_var"], at(g, "l0_var", p + 1))
                    GT(st0[:, 10:11], st0[:, 9:10], nhalf[:, 0:1], ALU.pow).then_inc(sem["l0_rstd"], 1)

            def norm(g, k):
                pool.wait_ge(sem["ln_var"], at(g, "ln_var", k))
                GT(rstd[:], ve[:], nhalf[:, 0:PAIRS], ALU.pow).then_inc(sem["ln_rstd"], 1)

            def layer1(g, along):
                norm(g, 1)
                along("token_mix_in")
                xa = xs[:].rearrange("p t b l -> p (t b) l")[:, :, 1:L + 1]
                for f in range(5):
                    pool.wait_ge(sem["mix_tmp"], at(g, "mix_tmp", f + 1))
                    m = mix[:, f].rearrange("p t (b l) -> p (t b) l", l=L)
                    GT(m, m, xa, ALU.add).then_inc(sem["mix_x"], 1)
                    if f == 3:
                        along("token_mix")
                for t in range(CT):
                    for j in range(4):
                        along(f"spread{min(4 * t + j + 1, 7)}")
                        pool.wait_ge(sem["wkv_s"], at(g, "wkv_s", 8 * t + 2 * j + 2))
                        a2 = av[:, t, 2 * j:2 * j + 2].rearrange("p s b l -> p s (b l)")
                        GT(a2, a2, rT[:, t:t + 1, :].to_broadcast([P, 2, TOK]), ALU.mult).then_inc(sem["wkv_p"], 1)
                along("gn_out")
                norm(g, 2)

            def attention(g, a, along):
                at_point = ("self_", "cross_")[a]
                along(("channel_mix_in", "self_ctx_turn")[a])
                norm(g, 3 + a)
                along(at_point + "qkv")
                for r4 in range(4):
                    if r4 == 2:
                        along(at_point + "scores_a")
                    pool.wait_ge(sem["mskd"], at(g, "mskd", 4 * a + r4 + 1))
                    if a == 0:
                        GT(pb[:, r4], pb[:, r4], selfb[:].unsqueeze(1).to_broadcast([P, 8, L]), ALU.add).then_inc(sem["mbias"], 1)
                    else:
                        s = pb[:, r4].rearrange("p (r h) k -> p r h k", r=PAIRS)
                        GT(s, s, crossb[:].unsqueeze(2).to_broadcast([P, PAIRS, 4, L]), ALU.add).then_inc(sem["mbias"], 1)

            def mlp(g, along):
                along("cross_ctx_turn")
                norm(g, 5)
                for c in range(4):
                    if c % 2 == 0:
                        along(("mlp_in_a", "mlp_in")[c // 2])
                    pool.wait_ge(sem["ut"], at(g, "ut", c + 1))
                    s = slice(2 * c, 2 * c + 2)
                    GT(tb[:, s, :], tb[:, s, :], ub[:, s, :], ALU.mult).then_inc(sem["utu"], 1)

            def group(g, along):
                layer1(g, along)
                attention(g, 0, along)
                attention(g, 1, along)
                mlp(g, along)
                along(POINTS[-1])

            for k in range(PIECES):
                l0_piece(0, k)
            with pool.Fori(0, NG - 1) as g:
                group(g, Along(l0_piece, g + 1))
            group(NG - 1, Along(None, None))

        @block.vector
        def _(dve):
            V = nc.vector
            for name, per in PER.items():
                dve.sem_inc(sem[name], per)
            dve.sem_inc(st_out, 16)
            dve.wait_ge(ld_const, 16 * N_CONST)
            V.memset(vbd[:], 0.0)
            V.tensor_scalar(selfb[:], selfm[:], 10000.0, -10000.0, ALU.mult, ALU.add).then_inc(ready, 1)
            dve.wait_ge(ready, 1)
            V.memset(vbd[0:L, :, :, 0, D2:KV], 1.0)
            V.memset(vbd[L:P, :, :, 1, D2:KV], 1.0)
            V.tensor_scalar(selfm[:], selfm[:], 0.25, None, ALU.mult)
            V.tensor_scalar(bq8[:], cols[:, COLS["l0_bq"][0]:COLS["l0_bq"][0] + 4], 0.125, None, ALU.mult).then_inc(ready, 1)
            dve.wait_ge(ready, 2)
            dve.wait_ge(ready_pool, 1)
            l0_steps = Steps("vec_l0")
            steps = Steps("vec")

            def l0_norm(g, p, part):
                if part == 0:
                    dve.wait_ge(ld_pair[p], g * 32 + 32)
                    V.bn_stats(st0[:, 0:6], x_t[:, p, :]).then_inc(vec_l0_step, 1)
                    dve.wait_ge(vec_l0_step, l0_steps.next())
                    V.memset(st0[:, 15:16], 0.0)
                    V.bn_aggr(st0[:, 6:8], st0[:, 0:6]).then_inc(sem["l0_stat"], 1)
                elif part == 1:
                    dve.wait_ge(sem["l0_mean"], at(g, "l0_mean", 2 * p + 1))
                    V.tensor_copy(st0[:, 11:12], yp[:, 0:1])
                    V.tensor_tensor(st0[:, 8:9], st0[:, 6:7], yp[:, 0:1], ALU.subtract).then_inc(vec_l0_step, 1)
                    dve.wait_ge(vec_l0_step, l0_steps.next())
                    V.tensor_tensor(st0[:, 9:10], st0[:, 8:9], st0[:, 8:9], ALU.mult).then_inc(vec_l0_step, 1)
                    dve.wait_ge(vec_l0_step, l0_steps.next())
                    V.tensor_tensor(st0[:, 7:8], st0[:, 7:8], st0[:, 9:10], ALU.add).then_inc(sem["l0_stat"], 1)
                elif part == 2:
                    dve.wait_ge(sem["l0_mean"], at(g, "l0_mean", 2 * p + 2))
                    V.tensor_scalar(st0[:, 9:10], yp[:, 1:2], EPS, None, ALU.add).then_inc(sem["l0_var"], 1)
                else:
                    dve.wait_ge(sem["l0_rstd"], at(g, "l0_rstd", p + 1))
                    V.tensor_tensor(st0[:, 10:11], st0[:, 10:11], col("l0_gamma"), ALU.mult).then_inc(vec_l0_step, 1)
                    dve.wait_ge(vec_l0_step, l0_steps.next())
                    V.tensor_scalar(xn[:], x_t[:, p, :], st0[:, 11:12], st0[:, 10:11], ALU.subtract, ALU.mult).then_inc(vec_l0_step, 1)
                    dve.wait_ge(vec_l0_step, l0_steps.next())
                    V.tensor_scalar(xn[:], xn[:], col("l0_beta"), None, ALU.add).then_inc(sem["l0_xn"], 1)

            def l0_v(g, n):
                for t in range(2):
                    dve.wait_ge(sem["l0_proj"], at(g, "l0_proj", 6 * n + 5 + t))
                    V.tensor_tensor(v0[:, t, :], ring[t][:], row("l0_bv"), ALU.add).then_inc(sem[f"ring{t}"], 1)

            def l0_max(g, n, h):
                dve.wait_ge(sem["l0_S"], at(g, "l0_S", 8 * n + h + 1))
                V.tensor_reduce(nm0[:, h % 2, :], two(ring[h % 2][:]), AX, ALU.max, negate=True).then_inc(sem["l0_nm"], 1)

            def l0_pt(g, n, h):
                dve.wait_ge(sem["l0_T"], at(g, "l0_T", 8 * n + h + 1))
                dve.wait_ge(sem["l0_AV"], at(g, "l0_AV", 8 * n + h - 1))
                V.tensor_copy(pt0[:, h % 2], two(ptp[:])).then_inc(sem["l0_pt"], 1)

            def l0_y(g, n, q):
                dve.wait_ge(sem["l0_AV"], at(g, "l0_AV", 8 * n + 4 * q + 4))
                s = slice(4 * q, 4 * q + 4)
                V.reciprocal(rr0[:, s, :], rs0[:, s, :]).then_inc(vec_l0_step, 1)
                dve.wait_ge(vec_l0_step, l0_steps.next())
                V.tensor_tensor(y0[:].rearrange("p q (h d) -> p h q d", d=D0)[:, s], yp[:].rearrange("p (h q d) -> p h q d", h=4, q=2),
                                    rr0[:, s, :].unsqueeze(3).to_broadcast([P, 4, 2, D0]), ALU.mult).then_inc(sem["l0_y"], 1)

            def l0_x1(g, n):
                r = slice(L * (n % 2), L * (n % 2) + L)
                dve.wait_ge(sem["l0_out"], at(g, "l0_out", n + 1))
                V.scalar_tensor_tensor(x1[r, n // 2, :], ptp[r, 0:C], cols[r, COLS["l0_bo"][0]:COLS["l0_bo"][0] + 1], x_t[r, n // 2, :],
                                           ALU.add, ALU.add).then_inc(sem["l0_x1"], 1)

            def l0_piece(g, k):
                p, part, n, step = piece_of(k)
                if k == 0:
                    l0_steps.start(g)
                if part is not None:
                    l0_norm(g, p, part)
                elif step == 0:
                    l0_v(g, n)
                elif step == BATCH_PIECES - 1:
                    l0_y(g, n, 1)
                    l0_x1(g, n)
                else:
                    i = step - 1
                    if i < H0:
                        l0_max(g, n, i)
                    if 1 <= i <= H0:
                        l0_pt(g, n, i - 1)
                    if i == 6:
                        l0_y(g, n, 0)
                if k == PIECES - 1:
                    l0_steps.end()

            def norm(g, k):
                for p in range(PAIRS):
                    last = V.bn_stats(bst[:, p, :], xr[:, p, :])
                last.then_inc(vec_step, 1)
                dve.wait_ge(vec_step, steps.next())
                V.memset(st0[:, 15:16], 0.0)
                for p in range(PAIRS):
                    last = V.bn_aggr(mv[:, p, :], bst[:, p, :])
                last.then_inc(vec_step, 1)
                dve.wait_ge(vec_step, steps.next())
                V.tensor_scalar(ve[:], mv[:, :, 1], EPS, None, ALU.add).then_inc(sem["ln_var"], 1)
                dve.wait_ge(sem["ln_rstd"], at(g, "ln_rstd", k))
                for p in range(PAIRS):
                    last = V.tensor_scalar(xh[:, p, :], xr[:, p, :], mv[:, p, 0:1], rstd[:, p:p + 1], ALU.subtract, ALU.mult)
                last.then_inc(sem["ln_xh"], 1)

            def shift(g, k, row_of_state):
                dve.wait_ge(sem["ctxT"], at(g, "ctxT", 1))
                V.tensor_copy(xs[:, :, :, 0], ctxT[:].rearrange("p t (b l) -> p t b l", l=L)[:, :, :, row_of_state]).then_inc(vec_step, 1)
                dve.wait_ge(vec_step, steps.next())
                dve.wait_ge(sem["ln_out"], at(g, "ln_out", k))
                xf = xs[:].rearrange("p t b l -> p (t b) l")
                V.tensor_tensor(sx[:].rearrange("p t (b l) -> p (t b) l", l=L), xf[:, :, 0:L], xf[:, :, 1:L + 1], ALU.subtract).then_inc(vec_step, 1)
                dve.wait_ge(vec_step, steps.next())

            def bl(ap):
                return ap.rearrange("p (b l) -> p b l", l=L)

            def lerp(dst, name):
                for t in range(CT):
                    last = V.scalar_tensor_tensor(bl(dst[:, t, :]), bl(sx[:, t, :]), col(name, t), xs[:, t, :, 1:L + 1], ALU.mult, ALU.add)
                return last

            def flat(t):
                return t[:].rearrange("p a b -> p (a b)")

            def layer1(g, along):
                dve.wait_ge(sem["l0_x1"], at(g, "l0_x1", 4))
                V.tensor_copy(flat(xr), flat(x1)).then_inc(vec_step, 1)
                dve.wait_ge(vec_step, steps.next())
                norm(g, 1)
                along("ctx_turn")
                shift(g, 1, 1)
                lerp(xx, "maa_x").then_inc(sem["xxx"], 1)
                along("token_mix_in")
                for f, name in enumerate(("maa_w", "maa_k", "maa_v", "maa_r", "maa_g")):
                    dve.wait_ge(sem["mix_p"], at(g, "mix_p", f + 1))
                    for t in range(CT):
                        last = V.scalar_tensor_tensor(mix[:, f, t, :], R[(f + 1) % 4][:, t * TOK:(t + 1) * TOK], col(name, t), sx[:, t, :], ALU.add, ALU.mult)
                    last.then_inc(sem["mix_tmp"], 1)
                    if f == 3:
                        along("token_mix")
                along("values")
                dve.wait_ge(sem["rkv"], at(g, "rkv", 3))
                for t in range(CT):
                    last = V.scalar_tensor_tensor(yc[:, t, :], rT[:, t, :], col("faaaa", t), kT[:, t, :], ALU.mult, ALU.mult)
                last.then_inc(sem["ruk"], 1)
                dve.wait_ge(ld_s0, g * 64 + 64)
                for t in range(CT):
                    last = V.tensor_copy(av[:, t, :, :, 0], s0t[:, :, t, :].rearrange("p b s -> p s b"))
                last.then_inc(vec_step, 1)
                dve.wait_ge(vec_step, steps.next())

                along("receptance")
                dve.wait_ge(sem["ruk_p"], at(g, "ruk_p", 1))
                V.tensor_tensor(flat(ybon), R[0][:], flat(vT), ALU.mult).then_inc(sem["bonus"], 1)
                dve.wait_ge(sem["eg"], at(g, "eg", 1))
                V.tensor_scalar(flat(sg), flat(sg), 0.5, 0.5, ALU.mult, ALU.add).then_inc(vec_step, 1)
                dve.wait_ge(vec_step, steps.next())
                V.tensor_tensor(flat(sg), R[3][:], flat(sg), ALU.mult).then_inc(sem["silu"], 1)

                along("gate")
                
                def outer(t, j):
                    dve.wait_ge(sem["spread_p"], at(g, "spread_p", 4 * t + j + 1))
                    k = 4 * t + j
                    vb = R[1 + k % 2][:].rearrange("p (s b l) -> p s b l", s=2, l=L)[:, :, :, 0:L - 1]
                    kk = bl(kT[:, t, :]).unsqueeze(1).to_broadcast([P, 2, G, L])[:, :, :, 0:L - 1]
                    V.tensor_tensor(av[:, t, 2 * j:2 * j + 2, :, 1:L], vb, kk, ALU.mult).then_inc(sem["wkv_a"], 1)

                def scans(t, j):
                    dve.wait_ge(sem["wkv_a"], at(g, "wkv_a", 4 * t + j + 1))
                    for i in range(2):
                        s = av[:, t, 2 * j + i].rearrange("p b l -> p (b l)")
                        V.tensor_tensor_scan(s, wsh[:, t].rearrange("p b l -> p (b l)"), s, 0.0, ALU.mult, ALU.add).then_inc(sem["wkv_s"], 1)

                dve.wait_ge(sem["decw"], at(g, "decw", 1))
                outer(0, 0)
                outer(0, 1)
                along("spread1")
                for k in range(8):
                    scans(k // 4, k % 4)
                    if k + 2 < 8:
                        outer((k + 2) // 4, (k + 2) % 4)
                        along(f"spread{k + 2}")
                dve.wait_ge(sem["bonus"], at(g, "bonus", 1))
                for t in range(CT):
                    dve.wait_ge(sem["wkv_yp"], at(g, "wkv_yp", t + 1))
                    V.tensor_tensor(yc[:, t, :], R[3][:, t * TOK:(t + 1) * TOK], ybon[:, t, :], ALU.add).then_inc(sem["wkv_y"], 1)
                    along(f"gather{t}")
                dve.wait_ge(sem["gm_p"], at(g, "gm_p", 1))
                V.tensor_tensor(flat(yc), flat(yc), R[0][:], ALU.subtract).then_inc(sem["gd"], 1)
                along("gn_mean")
                dve.wait_ge(sem["gv_p"], at(g, "gv_p", 1))
                V.tensor_scalar(flat(gq), R[1][:], EPS, None, ALU.add).then_inc(sem["gve"], 1)
                along("gn_var")
                dve.wait_ge(sem["grs"], at(g, "grs", 1))
                V.reciprocal(flat(gq), flat(gq)).then_inc(vec_step, 1)
                dve.wait_ge(vec_step, steps.next())
                dve.wait_ge(sem["silu"], at(g, "silu", 1))
                for t in range(CT):
                    last = V.scalar_tensor_tensor(yc[:, t, :], yc[:, t, :], col("gn_w", t), gq[:, t, :], ALU.mult, ALU.mult)
                last.then_inc(vec_step, 1)
                dve.wait_ge(vec_step, steps.next())
                for t in range(CT):
                    last = V.scalar_tensor_tensor(yc[:, t, :], yc[:, t, :], col("gn_b", t), sg[:, t, :], ALU.add, ALU.mult)
                last.then_inc(sem["yg"], 1)
                along("gn_out")
                dve.wait_ge(sem["wo_p"], at(g, "wo_p", 1))
                V.tensor_tensor(flat(xr), R[2][:], flat(xr), ALU.add).then_inc(sem["x2"], 1)
                dve.wait_ge(sem["x2"], at(g, "x2", 1))
                norm(g, 2)
                along("wkv_out")
                shift(g, 2, 0)
                lerp(mix[:, 0], "fmaa_k")
                lerp(mix[:, 1], "fmaa_r").then_inc(sem["ffn_in"], 1)
                along("ln2_turn")
                dve.wait_ge(sem["fk_p"], at(g, "fk_p", 1))
                V.tensor_scalar(mix[:, 3].rearrange("p a b -> p (a b)"), R[0][:], 0.0, None, ALU.max).then_inc(sem["frelu"], 1)
                dve.wait_ge(sem["fe"], at(g, "fe", 1))
                V.tensor_scalar(flat(e1), flat(e1), 0.5, 0.5, ALU.mult, ALU.add).then_inc(vec_step, 1)
                dve.wait_ge(vec_step, steps.next())
                along("channel_mix_in")
                dve.wait_ge(sem["fv_p"], at(g, "fv_p", 1))
                V.tensor_tensor(flat(tmp), R[2][:], flat(e1), ALU.mult).then_inc(vec_step, 1)
                dve.wait_ge(vec_step, steps.next())
                V.tensor_tensor(flat(xr), flat(xr), flat(tmp), ALU.add).then_inc(sem["x3"], 1)
                dve.wait_ge(sem["x3"], at(g, "x3", 1))

            def attention(g, a, along):
                at_point = ("self_", "cross_")[a]
                norm(g, 3 + a)
                along(("channel_mix", "self_out")[a])
                along(at_point + "turn")
                dve.wait_ge(sem["qkv_p"], at(g, "qkv_p", 3 * a + 1))
                for t in range(CT):
                    for e, parity in enumerate(("even_head", "odd_head")):
                        last = V.tensor_scalar(kbd[:, t, e, :], R[1][:, t * TOK:(t + 1) * TOK], col(("sa_bk", "ca_bk")[a], t), col(parity),
                                               ALU.add, ALU.mult)
                last.then_inc(sem["k_bd"], 1)
                dve.wait_ge(sem["qkv_p"], at(g, "qkv_p", 3 * a + 2))
                dve.wait_ge(sem["v_bd"], at(g, "v_bd", a))
                V.tensor_tensor(vsb, two(R[2][:]), row(("sa_bv", "ca_bv")[a]).unsqueeze(1).to_broadcast([P, PAIRS, C]), ALU.add).then_inc(sem["v_sb"], 1)
                along(at_point + "qkv")
                if a == 1:
                    dve.wait_ge(ld_cmask, g * 32 + 32)
                    V.tensor_scalar(crossm[:], cmask[:], 0.25, None, ALU.mult)
                    V.tensor_scalar(crossb[:], cmask[:], 10000.0, -10000.0, ALU.mult, ALU.add).then_inc(sem["cmask"], 1)
                    dve.wait_ge(sem["cmask"], at(g, "cmask", 1))
                for r4 in range(4):
                    dve.wait_ge(sem["s_p"], at(g, "s_p", 4 * a + r4 + 1))
                    if a == 0:
                        last = V.tensor_tensor(pb[:, r4], R[r4][:].rearrange("p (h k) -> p h k", k=L),
                                               selfm[:].unsqueeze(1).to_broadcast([P, 8, L]), ALU.mult)
                    else:
                        last = V.tensor_tensor(pb[:, r4].rearrange("p (r h) k -> p r h k", r=PAIRS), R[r4][:].rearrange("p (r h k) -> p r h k", r=PAIRS, k=L),
                                               crossm[:].unsqueeze(2).to_broadcast([P, PAIRS, 4, L]), ALU.mult)
                    last.then_inc(sem["mskd"], 1)
                    if r4 == 1:
                        along(at_point + "scores_a")
                vh = vsb.rearrange("p r (h e d) -> p r h e d", e=2, d=D2)
                vw = vsw[:].rearrange("p r (h e d) -> p r h e d", e=2, d=D2)
                vo = vbd[:].rearrange("p (r b) h e d -> p r b h e d", b=2)
                V.tensor_copy(vo[0:L, :, 0, :, 0, 0:D2], vh[0:L, :, :, 0, :])
                V.tensor_copy(vo[L:P, :, 1, :, 1, 0:D2], vh[L:P, :, :, 1, :])
                dve.wait_ge(v_swap, g * 64 + 32 * (a + 1))
                V.tensor_copy(vo[0:L, :, 1, :, 0, 0:D2], vw[0:L, :, :, 0, :])
                V.tensor_copy(vo[L:P, :, 0, :, 1, 0:D2], vw[L:P, :, :, 1, :]).then_inc(sem["v_bd"], 1)
                for r4 in range(4):
                    dve.wait_ge(sem["mbias"], at(g, "mbias", 4 * a + r4 + 1))
                    V.tensor_reduce(mx[:, r4, :], pb[:, r4], AX, ALU.max).then_inc(vec_step, 1)
                    dve.wait_ge(vec_step, steps.next())
                    V.tensor_tensor(pb[:, r4], pb[:, r4], mx[:, r4, :].unsqueeze(2).to_broadcast([P, 8, L]), ALU.subtract).then_inc(sem["sub"], 1)
                    if r4 == 1:
                        along(at_point + "scores")
                along(at_point + "softmax")
                for r4 in (1, 3):
                    dve.wait_ge(sem["pt_p"], at(g, "pt_p", 4 * a + r4 + 1))
                    V.tensor_copy(ptb[:, r4].rearrange("p a b -> p (a b)"), R[r4][:]).then_inc(sem["pt_v"], 1)
                    along(at_point + ("turned_a" if r4 == 1 else "turned"))
                for p in range(PAIRS):
                    dve.wait_ge(sem["av_p"], at(g, "av_p", 2 * a + p + 1))
                    y = R[p][:, 0:H2 * KV].rearrange("p (h d) -> p h d", d=KV)
                    V.reciprocal(rc[:, p, :], y[:, :, D2]).then_inc(vec_step, 1)
                    dve.wait_ge(vec_step, steps.next())
                    V.tensor_tensor(cx[:, p, :].rearrange("p (h d) -> p h d", d=D2), y[:, :, 0:D2],
                                        rc[:, p, :].unsqueeze(2).to_broadcast([P, H2, D2]), ALU.mult).then_inc(sem["cx"], 1)
                along(at_point + "ctx_turn")
                dve.wait_ge(sem["ao_p"], at(g, "ao_p", a + 1))
                V.tensor_tensor(tmp[:], two(R[3][:]), row(("sa_bo", "ca_bo")[a]).unsqueeze(1).to_broadcast([P, PAIRS, C]), ALU.add).then_inc(vec_step, 1)
                dve.wait_ge(vec_step, steps.next())
                V.tensor_tensor(flat(xr), flat(xr), flat(tmp), ALU.add).then_inc(sem["ao"], 1)
                dve.wait_ge(sem["ao"], at(g, "ao", a + 1))

            def mlp(g, along):
                norm(g, 5)
                along("mlp_turn")
                for c in range(4):
                    dve.wait_ge(sem["h1_p"], at(g, "h1_p", c + 1))
                    for i in range(2):
                        j = 2 * c + i
                        last = V.tensor_scalar(ub[:, j, :], R[c][:, i * TOK:(i + 1) * TOK], col("b1", j), None, ALU.add)
                    last.then_inc(sem["u"], 1)
                    if c == 1:
                        along("mlp_in_a")
                for c in range(4):
                    dve.wait_ge(sem["usq"], at(g, "usq", c + 1))
                    s = slice(2 * c, 2 * c + 2)
                    V.tensor_scalar(tb[:, s, :], tb[:, s, :], 0.044715, 1.0, ALU.mult, ALU.add).then_inc(sem["ut"], 1)
                    if c == 1:
                        along("mlp_in")
                for c in range(4):
                    dve.wait_ge(sem["uth"], at(g, "uth", c + 1))
                    s = slice(2 * c, 2 * c + 2)
                    V.scalar_tensor_tensor(tb[:, s, :], tb[:, s, :], 1.0, ub[:, s, :], ALU.add, ALU.mult).then_inc(sem["ug"], 1)
                along("gelu")
                dve.wait_ge(sem["w2_p"], at(g, "w2_p", 1))
                for p in range(PAIRS):
                    last = V.scalar_tensor_tensor(tmp[:, p, :], R[0][:, p * C:(p + 1) * C], 0.5, row("b2"), ALU.mult, ALU.add)
                last.then_inc(vec_step, 1)
                dve.wait_ge(vec_step, steps.next())
                V.tensor_tensor(flat(xr), flat(xr), flat(tmp), ALU.add).then_inc(sem["x5"], 1)

            def layer3(g, along):
                along("mlp_out")
                dve.wait_ge(sem["x3qk_p"], at(g, "x3qk_p", 1))
                V.tensor_copy(kbd[:, 0].rearrange("p a b -> p (a b)"), R[2][:]).then_inc(sem["x3k"], 1)
                dve.wait_ge(sem["x3qk_p"], at(g, "x3qk_p", 2))
                V.tensor_copy(v3[:].rearrange("p a b -> p (a b)"), R[3][:]).then_inc(sem["x3v"], 1)
                along("x3_q")
                dve.wait_ge(sem["s3_p"], at(g, "s3_p", 1))
                for b2 in range(2):
                    r = slice(L * b2, L * b2 + L)
                    last = V.tensor_reduce(nm3[r, :], R[0][r, 0:PAIRS * P].rearrange("p (r e k) -> p r e k", r=PAIRS, k=L)[:, :, b2, :], AX, ALU.max, negate=True)
                last.then_inc(vec_step, 1)
                dve.wait_ge(vec_step, steps.next())
                V.tensor_scalar(nm3[:], nm3[:], 0.0625, None, ALU.mult).then_inc(sem["nm3"], 1)
                dve.wait_ge(sem["e3"], at(g, "e3", 1))
                V.reciprocal(rc3[:], sm3[:]).then_inc(vec_step, 1)
                dve.wait_ge(vec_step, steps.next())
                for p in range(PAIRS):
                    last = V.tensor_scalar(p3[:, p, :], p3[:, p, :], rc3[:, p:p + 1], None, ALU.mult)
                last.then_inc(sem["pn3"], 1)
                along("x3_scores")
                along("x3_ctx")
                dve.wait_ge(sem["d3_p"], at(g, "d3_p", 1))
                dve.wait_ge(st_out, (g + 1) * 16)
                for p in range(PAIRS):
                    last = V.scalar_tensor_tensor(xo[:, p, :], R[3][:, p * C:(p + 1) * C], col("alpha"), xr[:, p, :], ALU.mult, ALU.add)
                last.then_inc(sem["xo"], 1)

            def group(g, along):
                steps.start(g)
                layer1(g, along)
                attention(g, 0, along)
                attention(g, 1, along)
                mlp(g, along)
                layer3(g, along)
                along(POINTS[-1])
                steps.end()

            for k in range(PIECES):
                l0_piece(0, k)
            with dve.Fori(0, NG - 1) as g:
                group(g, Along(l0_piece, g + 1))
            group(NG - 1, Along(None, None))


def constants():
    import numpy as np
    i = np.arange(P)
    eye = np.eye(P, dtype=np.float32)
    mean64 = ((i[:, None] // L) == (i[None, :] // L)).astype(np.float32) / L
    sum8 = ((i[:, None] // S1) == (i[None, :] // S1)).astype(np.float32)
    spread = np.stack([sum8 * ((i[:, None] % S1) == t) for t in range(S1)], 1).astype(np.float32)
    gather = np.stack([sum8 * ((i[None, :] % S1) == t) for t in range(S1)], 1).astype(np.float32)
    return dict(ident=eye, mean64=mean64, sum8=sum8, mean8=sum8 / S1,
                spread=spread.reshape(P, -1), gather=gather.reshape(P, -1))


def kernel(**inputs):
    import numpy as np
    import concourse.bacc as bacc
    from concourse import mybir as mb
    from concourse.bass_utils import run_bass_kernel_spmd as run

    a = {k: np.asarray(v) for k, v in inputs.items()}
    l0 = {k[9:]: v for k, v in a.items() if k.startswith("L0_xattn_")}
    l1 = {k[9:]: v for k, v in a.items() if k.startswith("L1_xattn_")}
    l2 = {k[9:]: v for k, v in a.items() if k.startswith("L2_xattn_")}
    l3 = {k[9:]: v for k, v in a.items() if k.startswith("L3_xattn_")}

    def column(v):
        return np.reshape(v, (-1, P)).T

    def twice(v):
        return np.concatenate([v, v], 0)

    half = np.arange(P) // D2 % 2
    col = dict(l0_gamma=twice(l0["gamma"]), l0_beta=twice(l0["beta"]), l0_bq=l0["bq"], l0_bk=l0["bkv"][:512],
               l0_bo=twice(l0["bo"]), sa_s=l2["ln1_s"], sa_b=l2["ln1_b"], ca_s=l2["ln2_s"], ca_b=l2["ln2_b"],
               ml_s=l2["ln3_s"], ml_b=l2["ln3_b"], sa_bq=l2["b_qkv"][:C], sa_bk=l2["b_qkv"][C:2 * C],
               ca_bq=l2["b_q"], ca_bk=l2["b_kv"][:C], b1=l2["b1"], alpha=np.broadcast_to(l3["alpha"], (P,)),
               even_head=(half == 0).astype(np.float32), odd_head=(half == 1).astype(np.float32))
    cols = np.ascontiguousarray(np.concatenate([column(col[n] if n in col else l1[n]) for n in COLS], 1))
    row = dict(l0_bv=l0["bkv"][512:], sa_bv=l2["b_qkv"][2 * C:], sa_bo=l2["b_ao"], ca_bv=l2["b_kv"][C:], ca_bo=l2["b_co"], b2=l2["b2"])
    rows = np.ascontiguousarray(np.concatenate([row[n] for n in ROWS])[None])

    def tiles(m):
        return np.reshape(np.transpose(np.reshape(m, (-1, P, m.shape[1])), (1, 0, 2)), (P, -1))

    def padded(m):
        return np.concatenate([m, np.zeros((P - m.shape[0], m.shape[1]), m.dtype)], 0)

    def either(m):
        z = np.zeros_like(m)
        return np.concatenate([np.concatenate([m, z], 0), np.concatenate([z, m], 0)], 1)

    w2 = np.reshape(l1["maa_w2"], (5 * DM, C))
    mats = dict(l0_q=either(l0["Wq"].T), l0_k=either(l0["Wkv"][:512].T), l0_v=either(l0["Wkv"][512:].T), l0_o=tiles(l0["Wo"].T),
                maa_w1=tiles(l1["maa_w1"]), maa_w2=w2[:P], maa_w2g=padded(w2[P:]), dec_w1=tiles(l1["decay_w1"]), dec_w2=padded(l1["decay_w2"]),
                **{n: tiles(l1[n].T) for n in ("Wk", "Wv", "Wr", "Wg", "Wo", "fWk", "fWr", "fWv")},
                sa_q=tiles(l2["w_qkv"][:, :C]), sa_k=tiles(l2["w_qkv"][:, C:2 * C]), sa_v=tiles(l2["w_qkv"][:, 2 * C:]), sa_o=tiles(l2["w_ao"]),
                ca_q=tiles(l2["w_q"]), ca_k=tiles(l2["w_kv"][:, :C]), ca_v=tiles(l2["w_kv"][:, C:]), ca_o=tiles(l2["w_co"]),
                w1=tiles(l2["w1"]), w2=tiles(l2["w2"]),
                x_q=tiles(l3["w_q"].T), x_k=tiles(l3["w_k"].T), x_v=tiles(l3["w_v"].T), x_o=tiles(l3["w_o"].T), **constants())
    wts = np.ascontiguousarray(np.concatenate([mats[n] for n in WTS], 1))

    nc = bacc.Bacc("TRN2", target_bir_lowering=False, num_devices=1)
    arrays, args = {}, []
    for name, v in (("x", a["x"]), ("ctx", a["ctx_2048"]), ("mask_self", a["mask_1x1xSxS2_fc1"]), ("mask_cross", a["mask_Bx1xSxS2_ff1"]),
                    ("cols", cols), ("rows", rows), ("wts", wts)):
        v = np.ascontiguousarray(v)
        arrays[f"in_{name}_dram"] = v
        args.append(nc.dram_tensor(f"in_{name}_dram", v.shape, mb.dt.from_np(v.dtype), kind="ExternalInput").ap())
    args.append(nc.dram_tensor("out_0_dram", (B, L, C), mb.dt.float32, kind="ExternalOutput").ap())
    program(nc, *args)
    r = run(nc, [arrays], core_ids=[0])
    return r.results[0]["out_0_dram"]
```

```python
from contextlib import ExitStack

import concourse.bass as bass
from concourse import mybir

F32 = mybir.dt.float32
ALU = mybir.AluOpType
ACT = mybir.ActivationFunctionType
AX = mybir.AxisListType.X

P = 128
B, L, C = 64, 64, 256
CT = C // P
G = 4
NG = B // G
PAIRS = G // 2
TOK = G * L
EPS = 1e-5
H0, D0 = 8, 64
H1, S1 = 32, 8
H2, D2 = 16, 16
KV = D2 + 1
DM, DD = 32, 64
FF = 4 * C

COLS = {}
for _name, _n in (("l0_gamma", 1), ("l0_beta", 1), ("l0_bq", 4), ("l0_bk", 4), ("l0_bv", 4), ("l0_bo", 1),
                  ("ln1_w", 2), ("ln1_b", 2), ("ln2_w", 2), ("ln2_b", 2), ("maa_x", 2),
                  ("maa_w", 2), ("maa_k", 2), ("maa_v", 2), ("maa_r", 2), ("maa_g", 2),
                  ("time_decay", 2), ("faaaa", 2), ("gn_w", 2), ("gn_b", 2), ("fmaa_k", 2), ("fmaa_r", 2),
                  ("sa_s", 2), ("sa_b", 2), ("ca_s", 2), ("ca_b", 2), ("ml_s", 2), ("ml_b", 2),
                  ("sa_bq", 2), ("sa_bk", 2), ("ca_bq", 2), ("ca_bk", 2), ("b1", 8), ("alpha", 1),
                  ("even_head", 1), ("odd_head", 1)):
    COLS[_name] = (sum(n for _, n in COLS.values()), _n)
N_COLS = sum(n for _, n in COLS.values())
ROWS = {}
for _name, _n in (("sa_bv", C), ("sa_bo", C), ("ca_bv", C), ("ca_bo", C), ("b2", C)):
    ROWS[_name] = (sum(n for _, n in ROWS.values()), _n)
N_ROWS = sum(n for _, n in ROWS.values())
WTS = {}
for _name, _t, _n in (("l0_q", 2, 512), ("l0_k", 2, 512), ("l0_v", 4, 64), ("l0_o", 4, 64),
                      ("ident", 1, 128), ("mean64", 1, 128), ("halves", 1, 64), ("sum8", 1, 128), ("mean8", 1, 128),
                      ("spread", 8, 128), ("gather", 2, 32),
                      ("maa_w1", 2, 160), ("maa_w2", 1, 256), ("maa_w2g", 1, 256), ("dec_w1", 2, 64), ("dec_w2", 1, 256),
                      ("Wk", 2, 256), ("Wv", 2, 256), ("Wr", 2, 256), ("Wg", 2, 256), ("Wo", 2, 256),
                      ("fWk", 2, 256), ("fWr", 2, 256), ("fWv", 2, 256),
                      ("sa_q", 2, 256), ("sa_k", 2, 256), ("sa_v", 2, 256), ("sa_o", 2, 256),
                      ("ca_q", 2, 256), ("ca_k", 2, 256), ("ca_v", 2, 256), ("ca_o", 2, 256),
                      ("w1", 2, 1024), ("w2", 8, 256),
                      ("x_q", 2, 256), ("x_k", 2, 256), ("x_v", 2, 256), ("x_o", 2, 256)):
    WTS[_name] = (sum(t * n for _, t, n in WTS.values()), _t, _n)
N_WTS = sum(t * n for _, t, n in WTS.values())
N_WTS0 = WTS["sum8"][0]

PER = dict(
    l0_stat=2, l0_mean=2, l0_var=1, l0_rstd=1, l0_xn=1, l0_proj=24, l0_S=32, l0_nm=32, l0_P=32, l0_T=32, l0_pt=32,
    l0_AV=16, l0_y=4, l0_out=4, l0_x1=2, ring0=28, ring1=28,
    ctx_tr=1, ctxT=1,
    ln_var=5, ln_rstd=5, ln_xh=5, ln_T=6, ln_out=6, xr_free=1,
    xxx=1, maa_p=1, maa_t=1, mix_p=5, mix_tmp=5, mix_x=5,
    dech_p=1, dech=1, decw_p=1, decw=1, rkv_p=4, rkv=3, eg=1, silu=1,
    ruk=1, ruk_p=1, bonus=1, spread_p=8, wkv_a=8, wkv_s=16, wkv_p=8, wkv_yp=2, wkv_y=2,
    gm_p=1, gd=1, gsq=1, gv_p=1, gve=1, grs=1, yg=1, wo_p=1, x2=1,
    ffn_in=1, fk_p=1, frelu=1, fkk=1, fr_p=1, fe=1, fv_p=1, x3=1,
    qkv_p=6, q_T=2, k_bd=2, v_sb=2, v_bd=2, s_p=8, mskd=8, mbias=8, sub=8, pexp=8, pt_p=8, pt_a=4, pt_v=4,
    av_p=4, cx=4, cxT_p=2, cxT=2, ao_p=2, ao=2, cmask=1,
    h1_p=4, u=4, usq=4, ut=4, utu=4, uth=4, ug=4, w2_p=1, x5=1,
    x3kv_p=2, x3k=1, x3v=1, s3_p=1, nm3=1, e3=1, pn3=1, pt3_p=1, pt3=1, d3_p=1, xo=1,
)
HEAD_STEPS = H0 + 3
RING_USES = 6 + H0
PIECE_STEPS = [[("norm", part, None)] for part in range(6)]
for _n in range(G):
    PIECE_STEPS.append(([("sum", _n - 1, None)] if _n else []) + [("project", _n, None)])
    PIECE_STEPS += [[("head", _n, _i)] + ([("output", _n - 1, None)] if _n and _i == 0 else []) for _i in range(HEAD_STEPS)]
PIECE_STEPS += [[("sum", G - 1, None)], [("output", G - 1, None)]]
PIECES = len(PIECE_STEPS)
POINTS = dict(
    ctx_turn=0, ln1_turn=1, token_mix_in=0, token_mix=0, decay_in=2, keys=1, values=2, receptance=1, gate=2,
    spread1=1, spread2=0, spread3=2, spread4=0, spread5=0, spread6=1, spread7=1, gather0=2, gather1=1, gn_mean=1,
    gn_var=1, gn_out=2, wkv_out=2, ln2_turn=1, channel_mix_in=1, channel_mix=1, self_turn=1, self_qkv=1,
    self_scores_a=1, self_scores=1, self_softmax=1, self_turned_a=0, self_turned=2, self_values=2, self_ctx_turn=2,
    self_out=1, cross_turn=0, cross_qkv=1, cross_scores_a=0, cross_scores=0, cross_softmax=2, cross_turned_a=1,
    cross_turned=1, cross_values=1, cross_ctx_turn=1, cross_out=2, mlp_turn=1, mlp_in_a=1, mlp_in=0, gelu=1,
    mlp_out=1, x3_turn=2, x3_scores=2, x3_turned=1, x3_out=0,
)
assert sum(POINTS.values()) == PIECES
CHAIN = dict(vec_l0=5, vec=38, act=1, pool=32)


def program(nc, x, ctx, mask_self, mask_cross, cols_d, rows_d, wts_d, out):
    with ExitStack() as es:
        def sb(name, *shape):
            return es.enter_context(nc.sbuf_tensor(name, [P, *shape], F32))

        sem = {n: es.enter_context(nc.semaphore(n)) for n in PER}
        vec_l0_step = es.enter_context(nc.semaphore("vec_l0_step"))
        vec_step = es.enter_context(nc.semaphore("vec_step"))
        pool_step = es.enter_context(nc.semaphore("pool_step"))
        act_step = es.enter_context(nc.semaphore("act_step"))
        ld_const = es.enter_context(nc.semaphore("ld_const"))
        ld_w0 = es.enter_context(nc.semaphore("ld_w0"))
        fold_p = es.enter_context(nc.semaphore("fold_p"))
        fold = es.enter_context(nc.semaphore("fold"))
        ld_w = es.enter_context(nc.semaphore("ld_w"))
        ld_pair = [es.enter_context(nc.semaphore(f"ld_pair{p}")) for p in range(PAIRS)]
        ld_s0 = es.enter_context(nc.semaphore("ld_s0"))
        ld_cmask = es.enter_context(nc.semaphore("ld_cmask"))
        v_swap = es.enter_context(nc.semaphore("v_swap"))
        st_out = es.enter_context(nc.semaphore("st_out"))
        ready = es.enter_context(nc.semaphore("ready"))
        ready_pool = es.enter_context(nc.semaphore("ready_pool"))

        def at(g, name, k):
            return (g + 1) * PER[name] + k

        class Steps:
            def __init__(self, name):
                self.name, self.n = name, 0

            def start(self, g):
                self.g, self.n = g, 0

            def next(self):
                self.n += 1
                return self.g * CHAIN[self.name] + self.n

            def end(self):
                assert self.n == CHAIN[self.name], (self.name, self.n)

        cols = sb("cols", N_COLS)
        rows = sb("rows", N_ROWS)
        wts = sb("wts", N_WTS)

        def col(name, t=0):
            o = COLS[name][0] + t
            return cols[:, o:o + 1]

        def row(name):
            o, n = ROWS[name]
            return rows[:, o:o + n]

        def w(name, t=0):
            o, _, n = WTS[name]
            return wts[:, o + t * n:o + (t + 1) * n]

        ident = w("ident")
        bq8 = sb("bq8", 4)
        none = sb("none", 2)
        nhalf = sb("nhalf", PAIRS)
        selfm = sb("selfm", L)
        selfb = sb("selfb", L)
        x_t = sb("x_t", PAIRS, C)
        c_t = sb("c_t", PAIRS, C)
        st0 = sb("st0", PAIRS, 16)
        xn = sb("xn", PAIRS, C)
        uv = sb("uv", 2, 512)
        bvo = sb("bvo", 512)
        q0 = sb("q0", 4, C)
        k0 = sb("k0", 4, C)
        v0 = sb("v0", 2, 512)
        nm0 = sb("nm0", 2, 2)
        p0 = sb("p0", 4, 2, C)
        bvb = p0[:, 0].rearrange("p a (b c) -> p (a b) c", c=P)
        pt0 = sb("pt0", 4, 2, C)
        rs0 = sb("rs0", H0, 2)
        y0 = sb("y0", C)
        x1 = sb("x1", PAIRS, C)
        xr = sb("xr", PAIRS, C)
        bst = sb("bst", PAIRS, 6)
        mv = sb("mv", PAIRS, 2)
        ve = sb("ve", PAIRS)
        rstd = sb("rstd", PAIRS)
        xh = sb("xh", PAIRS, C)
        hT = sb("hT", CT, TOK)
        ctxT = sb("ctxT", CT, TOK)
        xs = sb("xs", CT, G, L + 1)
        sx = sb("sx", CT, TOK)
        tT = sb("tT", TOK)
        tg = sb("tg", TOK)
        mix = sb("mix", 5, CT, TOK)
        hd = sb("hd", TOK)
        e1 = sb("e1", CT, TOK)
        wsh = sb("wsh", CT, G, L)
        kT = sb("kT", CT, TOK)
        vT = sb("vT", CT, TOK)
        rT = sb("rT", CT, TOK)
        sg = sb("sg", CT, TOK)
        s0t = sb("s0t", G, CT, S1)
        av = sb("av", CT, S1, G, L)
        ybon = sb("ybon", CT, TOK)
        xx = ybon
        yc = sb("yc", CT, TOK)
        gq = sb("gq", CT, TOK)
        cmask = sb("cmask", PAIRS, L)
        crossm = sb("crossm", PAIRS, L)
        crossb = sb("crossb", PAIRS, L)
        kbd = sb("kbd", CT, 2, TOK)
        vsb = sb("vsb", PAIRS, C)[:]
        vsw = sb("vsw", PAIRS, C)
        vbd = sb("vbd", G, H2 // 2, 2, KV)
        pb = av[:, 0].rearrange("p a b c -> p (a b c)").rearrange("p (r h k) -> p r h k", r=4, k=L)
        mx = sb("mx", 4, 8)
        ptb = av[:, 1].rearrange("p a b c -> p (a b c)").rearrange("p (r j q) -> p r j q", r=4, q=P)
        rc = sb("rc", PAIRS, H2)
        cx = mix[:, 4]
        cT = mix[:, 3]
        tmp = gq
        ub = av[:, 0].rearrange("p a b c -> p (a b c)").rearrange("p (j t) -> p j t", j=8)
        tb = av[:, 1].rearrange("p a b c -> p (a b c)").rearrange("p (j t) -> p j t", j=8)
        p3 = sb("p3", PAIRS, P)
        nm3 = sb("nm3", PAIRS)
        sm3 = sb("sm3", PAIRS)
        rc3 = sb("rc3", PAIRS)
        pT3 = sb("pT3", PAIRS, P)
        v3 = mix[:, 2]
        xo = sb("xo", PAIRS, C)

        ring = [es.enter_context(nc.psum_tensor(f"ring{i}", [P, 512], F32)) for i in range(2)]
        ptp = es.enter_context(nc.psum_tensor("ptp", [P, 512], F32))
        yp = es.enter_context(nc.psum_tensor("yp", [P, 512], F32))
        R = [es.enter_context(nc.psum_tensor(f"R{i}", [P, 512], F32)) for i in range(4)]

        def two(ap):
            return ap.rearrange("p (a b) -> p a b", a=2)

        class Along:
            def __init__(self, piece, g):
                self.piece, self.g, self.k = piece, g, 0

            def __call__(self, point):
                names = list(POINTS)
                upto = sum(POINTS[n] for n in names[:names.index(point) + 1])
                while self.piece is not None and self.k < upto:
                    self.piece(self.g, self.k)
                    self.k += 1

        block = es.enter_context(nc.Block())
        N_CONST = 4

        @block.sync
        def _(sp):
            for h in range(2):
                sp.dma_start(selfm[h * L:(h + 1) * L, :], mask_self[0, 0]).then_inc(ld_const, 16)
            sp.dma_start(cols[:], cols_d).then_inc(ld_const, 16)
            sp.dma_start(rows[:], rows_d.to_broadcast([P, N_ROWS])).then_inc(ld_const, 16)
            for lo, hi in ((0, N_WTS0 // 2), (N_WTS0 // 2, N_WTS0)):
                sp.dma_start(wts[:, lo:hi], wts_d[:, lo:hi]).then_inc(ld_w0, 16)

            def loads(g, b0):
                for p in range(PAIRS):
                    sp.wait_ge(sem["l0_x1"], at(g, "l0_x1", p + 1 - PAIRS))
                    sp.dma_start(x_t[:, p, :], x[bass.ds(b0[p], 2)].rearrange("b l c -> (b l) c")).then_inc(ld_pair[p], 16)
                sp.wait_ge(sem["ctx_tr"], at(g, "ctx_tr", 0))
                for p in range(PAIRS):
                    sp.dma_start(c_t[:, p, :], ctx[bass.ds(b0[p], 2)].rearrange("b l c -> (b l) c")).then_inc(ld_pair[p], 16)

            def loads_rest(g, b0):
                sp.wait_ge(sem["wkv_s"], at(g, "wkv_s", 0))
                for t in range(CT):
                    for p in range(PAIRS):
                        s0src = ctx[bass.ds(b0[p], 2), 2:2 + S1, :].rearrange("b s c -> b (s c)")
                        sp.dma_start(s0t[:, 2 * p:2 * p + 2, t, :],
                                     s0src[:, t * P * S1:(t + 1) * P * S1].rearrange("b (p t) -> p b t", t=S1)).then_inc(ld_s0, 16)
                sp.wait_ge(sem["cmask"], at(g, "cmask", 0))
                for p in range(PAIRS):
                    sp.dma_start(cmask[:, p, :], mask_cross[bass.ds(b0[p], 2), 0].rearrange("b q k -> (b q) k")).then_inc(ld_cmask, 16)

            def swap(g, a):
                sp.wait_ge(sem["v_sb"], at(g, "v_sb", a + 1))
                sp.wait_ge(sem["v_bd"], at(g, "v_bd", a))
                sp.dma_start(vsw[0:L], vsb[L:P]).then_inc(v_swap, 16)
                sp.dma_start(vsw[L:P], vsb[0:L]).then_inc(v_swap, 16)

            def store(g):
                sp.wait_ge(sem["xo"], at(g, "xo", 1))
                of_group = out.rearrange("(n p b) l c -> n (b l) p c", n=NG, p=PAIRS)
                sp.dma_start(of_group[bass.ds(g, 1)].rearrange("n r p c -> (n r) p c"), xo[:]).then_inc(st_out, 16)

            def group(g, b0):
                loads_rest(g, b0)
                swap(g, 0)
                swap(g, 1)
                store(g)

            loads(0, (0, 2))
            step = (N_WTS - N_WTS0) // 4
            for i in range(4):
                lo, hi = N_WTS0 + i * step, N_WTS if i == 3 else N_WTS0 + (i + 1) * step
                sp.dma_start(wts[:, lo:hi], wts_d[:, lo:hi]).then_inc(ld_w, 16)
            with sp.Fori(0, NG - 1) as g:
                now = [sp.snap(g * G + 2 * p) for p in range(PAIRS)]
                following = [sp.snap(g * G + G + 2 * p) for p in range(PAIRS)]
                loads(g + 1, following)
                group(g, now)
            group(NG - 1, [(NG - 1) * G + 2 * p for p in range(PAIRS)])
            sp.wait_ge(st_out, (NG + 1) * 16)

        @block.tensor
        def _(pe):
            mm, tr = nc.tensor.matmul, nc.tensor.transpose
            pe.wait_ge(ld_w0, 32)
            for h in range(H0):
                r = slice(D0 * (h % 2), D0 * (h % 2) + D0)
                for b2 in range(2):
                    last = mm(R[h % 2][L * b2:L * b2 + L, h * D0:(h + 1) * D0], w("l0_v", h // 2)[r, :], w("l0_o", h // 2)[r, :], start=True, stop=True)
            last.then_inc(fold_p, 1)
            pe.wait_ge(ready, 2)
            for h in range(H0):
                r = slice(D0 * (h % 2), D0 * (h % 2) + D0)
                last = mm(R[2 + h % 2][:, h * D0:(h + 1) * D0], bvb[r, h // 2, :], w("l0_o", h // 2)[r, :], start=True, stop=True)
            last.then_inc(fold_p, 1)
            pe.wait_ge(fold, 1)
            use = [0]

            def ring_use(g):
                u = use[0]
                use[0] += 1
                pe.wait_ge(sem[f"ring{u % 2}"], at(g, f"ring{u % 2}", u // 2))
                return ring[u % 2]

            def ring_done(g):
                u = use[0]
                pe.wait_ge(sem["ring0"], at(g, "ring0", (u + 1) // 2))
                pe.wait_ge(sem["ring1"], at(g, "ring1", u // 2))

            def l0_stats(g, j):
                if j == 0:
                    pe.wait_ge(sem["l0_x1"], at(g, "l0_x1", 0))
                pe.wait_ge(sem["l0_stat"], at(g, "l0_stat", j + 1))
                mm(yp[:, C + 2 * j:C + 2 * j + 2], w("mean64"), st0[:, :, 6 + j], start=True, stop=True).then_inc(sem["l0_mean"], 1)

            def l0_project(g, n):
                p = n // 2
                pe.wait_ge(ld_pair[p], g * 32 + 32)
                pe.wait_ge(sem["l0_xn"], at(g, "l0_xn", 1))
                for name, src in (("l0_q", xn[:, p, :]), ("l0_k", c_t[:, p, :])):
                    for j in range(2):
                        bank = ring_use(g)
                        for i in range(2):
                            m = 2 * j + i
                            last = mm(bank[:, i * C:(i + 1) * C], w(name, n % 2)[:, m * P:(m + 1) * P], src, start=True, stop=True)
                        last.then_inc(sem["l0_proj"], 1)
                for t in range(2):
                    bank = ring_use(g)
                    mm(bank[:, :], c_t[:, p, t * P:(t + 1) * P], uv[:, n % 2, :], start=True, stop=True).then_inc(sem["l0_proj"], 1)

            def l0_scores(g, n, h):
                r = slice(D0 * (h % 2), D0 * (h % 2) + D0)
                bank = ring_use(g)
                for t in range(2):
                    last = mm(bank[:, t * C:(t + 1) * C], q0[r, h // 2, t * P:(t + 1) * P], k0[r, h // 2, :], start=True, stop=True)
                last.then_inc(sem["l0_S"], 1)

            def l0_turn(g, n, h):
                pe.wait_ge(sem["l0_P"], at(g, "l0_P", 8 * n + h + 1))
                pe.wait_ge(sem["l0_pt"], at(g, "l0_pt", 8 * n + h))
                for kt in range(2):
                    for qt in range(2):
                        last = tr(ptp[:, kt * C + qt * P:kt * C + (qt + 1) * P], p0[:, h % 4, qt, kt * P:(kt + 1) * P], ident)
                last.then_inc(sem["l0_T"], 1)

            def l0_values(g, n, h):
                pe.wait_ge(sem["l0_pt"], at(g, "l0_pt", 8 * n + h + 2))
                if h == 0:
                    pe.wait_ge(sem["l0_y"], at(g, "l0_y", n))
                for kt in range(2):
                    for e in range(2):
                        last = mm(yp[D0 * e:D0 * e + D0, 0:C], v0[:, kt, (h + e) * D0:(h + e + 1) * D0], pt0[:, (h + e) % 4, kt, :],
                                  start=h == 0 and kt == 0, stop=h == H0 - 2 and kt == 1)
                last.then_inc(sem["l0_AV"], 1)

            def l0_head_step(g, n, i):
                if i == 0:
                    ring_done(g)
                if i < H0:
                    l0_scores(g, n, i)
                if 2 <= i < H0 + 2:
                    l0_turn(g, n, i - 2)
                if i >= 4 and i % 2 == 0:
                    l0_values(g, n, i - 4)

            def l0_output(g, n):
                r = slice(L * (n % 2), L * (n % 2) + L)
                pe.wait_ge(sem["l0_y"], at(g, "l0_y", n + 1))
                pe.wait_ge(sem["l0_x1"], at(g, "l0_x1", n // 2))
                mm(yp[r, C:2 * C], w("halves"), y0[:], start=True, stop=True).then_inc(sem["l0_out"], 1)

            def l0_piece(g, k):
                if k == 0:
                    use[0] = 0
                for what, n, i in PIECE_STEPS[k]:
                    if what == "norm" and n in (1, 3):
                        l0_stats(g, n // 2)
                    elif what == "project":
                        l0_project(g, n)
                    elif what == "head":
                        l0_head_step(g, n, i)
                    elif what == "output":
                        l0_output(g, n)

            def turn(g, bank, src, name):
                for p in range(PAIRS):
                    for t in range(CT):
                        last = tr(bank[:, t * TOK + p * P:t * TOK + (p + 1) * P], src[:, p, t * P:(t + 1) * P], ident)
                last.then_inc(sem[name], 1)

            def channel_major(bank, wname, src, name):
                for o in range(CT):
                    for t in range(CT):
                        last = mm(bank[:, o * TOK:(o + 1) * TOK], w(wname, t)[:, o * P:(o + 1) * P], src[:, t, :],
                                  start=t == 0, stop=t == CT - 1)
                last.then_inc(sem[name], 1)

            def token_major(bank, wname, src, name):
                for p in range(PAIRS):
                    for t in range(CT):
                        last = mm(bank[:, p * C:(p + 1) * C], src[:, t, p * P:(p + 1) * P], w(wname, t),
                                  start=t == 0, stop=t == CT - 1)
                last.then_inc(sem[name], 1)

            def layer1(g, along):
                for p in range(PAIRS):
                    pe.wait_ge(ld_pair[p], g * 32 + 32)
                pe.wait_ge(sem["xo"], at(g, "xo", 0))
                turn(g, R[1], c_t, "ctx_tr")
                along("ctx_turn")
                pe.wait_ge(sem["ln_xh"], at(g, "ln_xh", 1))
                turn(g, R[0], xh, "ln_T")
                along("ln1_turn")
                pe.wait_ge(sem["xxx"], at(g, "xxx", 1))
                for t in range(CT):
                    mm(R[0][:, 0:TOK], w("maa_w1", t)[:, 0:P], xx[:, t, :], start=t == 0, stop=t == 1)
                for t in range(CT):
                    last = mm(R[0][0:DM, TOK:2 * TOK], w("maa_w1", t)[:, P:P + DM], xx[:, t, :], start=t == 0, stop=t == 1)
                last.then_inc(sem["maa_p"], 1)
                along("token_mix_in")
                pe.wait_ge(sem["maa_t"], at(g, "maa_t", 1))
                pe.wait_ge(sem["ctxT"], at(g, "ctxT", 1))
                for f in range(5):
                    if f == 4:
                        along("token_mix")
                        pe.wait_ge(sem["mix_tmp"], at(g, "mix_tmp", 1))
                    bank = R[(f + 1) % 4]
                    for o in range(CT):
                        if f < 4:
                            r = slice(DM * f, DM * (f + 1))
                            last = mm(bank[:, o * TOK:(o + 1) * TOK], w("maa_w2")[r, o * P:(o + 1) * P], tT[r, :], start=True, stop=True)
                        else:
                            last = mm(bank[:, o * TOK:(o + 1) * TOK], w("maa_w2g")[0:DM, o * P:(o + 1) * P], tg[0:DM, :], start=True, stop=True)
                    last.then_inc(sem["mix_p"], 1)
                pe.wait_ge(sem["mix_x"], at(g, "mix_x", 1))
                pe.wait_ge(sem["mix_tmp"], at(g, "mix_tmp", 2))
                for t in range(CT):
                    last = mm(R[2][0:DD, 0:TOK], w("dec_w1", t), mix[:, 0, t, :], start=t == 0, stop=t == 1)
                last.then_inc(sem["dech_p"], 1)
                along("decay_in")
                pe.wait_ge(sem["mix_x"], at(g, "mix_x", 2))
                pe.wait_ge(sem["mix_tmp"], at(g, "mix_tmp", 4))
                channel_major(R[0], "Wk", mix[:, 1], "rkv_p")
                along("keys")
                pe.wait_ge(sem["dech"], at(g, "dech", 1))
                for o in range(CT):
                    last = mm(R[3][:, o * TOK:(o + 1) * TOK], w("dec_w2")[0:DD, o * P:(o + 1) * P], hd[0:DD, :], start=True, stop=True)
                last.then_inc(sem["decw_p"], 1)
                pe.wait_ge(sem["mix_x"], at(g, "mix_x", 3))
                pe.wait_ge(sem["mix_tmp"], at(g, "mix_tmp", 5))
                channel_major(R[1], "Wv", mix[:, 2], "rkv_p")
                along("values")
                pe.wait_ge(sem["mix_x"], at(g, "mix_x", 4))
                channel_major(R[2], "Wr", mix[:, 3], "rkv_p")
                along("receptance")
                pe.wait_ge(sem["mix_x"], at(g, "mix_x", 5))
                pe.wait_ge(sem["decw"], at(g, "decw", 1))
                channel_major(R[3], "Wg", mix[:, 4], "rkv_p")
                pe.wait_ge(sem["ruk"], at(g, "ruk", 1))
                for o in range(CT):
                    last = mm(R[0][:, o * TOK:(o + 1) * TOK], w("sum8"), yc[:, o, :], start=True, stop=True)
                last.then_inc(sem["ruk_p"], 1)

                def spread(k):
                    if k >= 2:
                        pe.wait_ge(sem["wkv_a"], at(g, "wkv_a", k - 1))
                    else:
                        pe.wait_ge(sem["rkv"], at(g, "rkv", 3))
                    bank = R[1 + k % 2]
                    for i in range(2):
                        last = mm(bank[:, i * TOK:(i + 1) * TOK], w("spread", 2 * (k % 4) + i), vT[:, k // 4, :], start=True, stop=True)
                    last.then_inc(sem["spread_p"], 1)

                def gather(t):
                    if t == 0:
                        pe.wait_ge(sem["silu"], at(g, "silu", 1))
                    for i in range(2):
                        for j in range(4):
                            if i == 0:
                                pe.wait_ge(sem["wkv_p"], at(g, "wkv_p", 4 * t + j + 1))
                            last = mm(R[3][32 * j:32 * j + 32, t * TOK:(t + 1) * TOK], w("gather", i),
                                      av[:, t, 2 * j + i].rearrange("p b l -> p (b l)"), start=i == 0, stop=i == 1)
                    last.then_inc(sem["wkv_yp"], 1)

                along("gate")
                spread(0)
                for k in range(1, 8):
                    spread(k)
                    along(f"spread{k}")
                gather(0)
                along("gather0")
                pe.wait_ge(sem["wkv_y"], at(g, "wkv_y", 1))
                gather(1)
                along("gather1")
                pe.wait_ge(sem["wkv_y"], at(g, "wkv_y", 2))
                pe.wait_ge(sem["bonus"], at(g, "bonus", 1))
                mm(R[0][:, :], w("mean8"), yc[:].rearrange("p a b -> p (a b)"), start=True, stop=True).then_inc(sem["gm_p"], 1)
                along("gn_mean")
                pe.wait_ge(sem["gsq"], at(g, "gsq", 1))
                mm(R[1][:, :], w("mean8"), gq[:].rearrange("p a b -> p (a b)"), start=True, stop=True).then_inc(sem["gv_p"], 1)
                along("gn_var")
                along("gn_out")
                pe.wait_ge(sem["yg"], at(g, "yg", 1))
                token_major(R[2], "Wo", yc, "wo_p")
                along("wkv_out")
                pe.wait_ge(sem["ln_xh"], at(g, "ln_xh", 2))
                turn(g, R[0], xh, "ln_T")
                along("ln2_turn")
                pe.wait_ge(sem["ffn_in"], at(g, "ffn_in", 1))
                channel_major(R[0], "fWk", mix[:, 0], "fk_p")
                token_major(R[1], "fWr", mix[:, 1], "fr_p")
                along("channel_mix_in")
                pe.wait_ge(sem["fkk"], at(g, "fkk", 1))
                token_major(R[2], "fWv", mix[:, 2], "fv_p")
                along("channel_mix")

            def attention(g, a, along):
                at_point = ("self_", "cross_")[a]
                q, k, v, o = (("sa_q", "sa_k", "sa_v", "sa_o"), ("ca_q", "ca_k", "ca_v", "ca_o"))[a]
                src = hT if a == 0 else ctxT
                pe.wait_ge(sem["ln_xh"], at(g, "ln_xh", 3 + a))
                turn(g, R[0], xh, "ln_T")
                along(at_point + "turn")
                if a == 0:
                    pe.wait_ge(sem["ln_out"], at(g, "ln_out", 3))
                channel_major(R[1], k, src, "qkv_p")
                token_major(R[2], v, src, "qkv_p")
                pe.wait_ge(sem["ln_out"], at(g, "ln_out", 3 + a))
                channel_major(R[0], q, hT, "qkv_p")
                along(at_point + "qkv")
                pe.wait_ge(sem["q_T"], at(g, "q_T", a + 1))
                pe.wait_ge(sem["k_bd"], at(g, "k_bd", a + 1))
                pe.wait_ge(sem["v_sb"], at(g, "v_sb", a + 1))
                for r4 in range(4):
                    r = slice(32 * r4, 32 * r4 + 32)
                    for b in range(G):
                        for t in range(CT):
                            oo = (b // 2) * C + t * P
                            last = mm(R[r4][L * (b % 2):L * (b % 2) + L, oo:oo + P], hTq[r, t, b * L:(b + 1) * L],
                                      kbd[r, t, :, b * L:(b + 1) * L], start=True, stop=True)
                    last.then_inc(sem["s_p"], 1)
                    if r4 == 1:
                        along(at_point + "scores_a")
                along(at_point + "scores")
                along(at_point + "softmax")
                for r4 in range(4):
                    pe.wait_ge(sem["pexp"], at(g, "pexp", 4 * a + r4 + 1))
                    for j in range(4):
                        last = tr(R[r4][:, j * P:(j + 1) * P], pb[:, r4, 2 * j:2 * j + 2, :].rearrange("p a b -> p (a b)"), ident)
                    last.then_inc(sem["pt_p"], 1)
                    if r4 == 1:
                        along(at_point + "turned_a")
                along(at_point + "turned")
                pe.wait_ge(sem["pt_a"], at(g, "pt_a", 2 * a + 2))
                pe.wait_ge(sem["pt_v"], at(g, "pt_v", 2 * a + 2))
                pe.wait_ge(sem["v_bd"], at(g, "v_bd", a + 1))
                for p in range(PAIRS):
                    for b2 in range(2):
                        for t in range(CT):
                            for r4 in range(4):
                                hp = t * 4 + r4
                                last = mm(R[p][L * b2:L * b2 + L, hp * 2 * KV:(hp + 1) * 2 * KV],
                                          ptb[:, r4, 2 * p + t, L * b2:L * b2 + L],
                                          vbd[:, 2 * p + b2, hp].rearrange("p a b -> p (a b)"), start=True, stop=True)
                    last.then_inc(sem["av_p"], 1)
                along(at_point + "values")
                pe.wait_ge(sem["cx"], at(g, "cx", 2 * a + 2))
                turn(g, R[2], cx, "cxT_p")
                along(at_point + "ctx_turn")
                pe.wait_ge(sem["cxT"], at(g, "cxT", a + 1))
                token_major(R[3], o, cT, "ao_p")
                along(at_point + "out")

            hTq = sx

            def mlp(g, along):
                pe.wait_ge(sem["ln_xh"], at(g, "ln_xh", 5))
                pe.wait_ge(sem["ao"], at(g, "ao", 2))
                turn(g, R[0], xh, "ln_T")
                along("mlp_turn")
                pe.wait_ge(sem["ln_out"], at(g, "ln_out", 5))
                for c in range(4):
                    for i in range(2):
                        j = 2 * c + i
                        for t in range(CT):
                            last = mm(R[c][:, i * TOK:(i + 1) * TOK], w("w1", t)[:, j * P:(j + 1) * P], hT[:, t, :],
                                      start=t == 0, stop=t == 1)
                    last.then_inc(sem["h1_p"], 1)
                    if c == 1:
                        along("mlp_in_a")
                along("mlp_in")
                along("gelu")
                for t in range(FF // P):
                    if t % 2 == 0:
                        pe.wait_ge(sem["ug"], at(g, "ug", t // 2 + 1))
                    for p in range(PAIRS):
                        last = mm(R[p][:, 0:C], tb[:, t, p * P:(p + 1) * P], w("w2", t), start=t == 0, stop=t == FF // P - 1)
                last.then_inc(sem["w2_p"], 1)
                along("mlp_out")

            def layer3(g, along):
                channel_major(R[2], "x_k", ctxT, "x3kv_p")
                token_major(R[3], "x_v", ctxT, "x3kv_p")
                pe.wait_ge(sem["x5"], at(g, "x5", 1))
                turn(g, R[0], xr, "ln_T")
                along("x3_turn")
                pe.wait_ge(sem["ln_out"], at(g, "ln_out", 6))
                pe.wait_ge(sem["x3k"], at(g, "x3k", 1))
                for b in range(G):
                    for t in range(CT):
                        o = (b // 2) * P + (b % 2) * L
                        last = mm(R[0][L * (b % 2):L * (b % 2) + L, o:o + L], hT[:, t, b * L:(b + 1) * L],
                                  kbd[:, 0, 0:2, :].rearrange("p a b -> p (a b)")[:, t * TOK + b * L:t * TOK + (b + 1) * L], start=t == 0, stop=t == 1)
                last.then_inc(sem["s3_p"], 1)
                along("x3_scores")
                pe.wait_ge(sem["pn3"], at(g, "pn3", 1))
                for p in range(PAIRS):
                    last = tr(R[1][:, p * P:(p + 1) * P], p3[:, p, :], ident)
                last.then_inc(sem["pt3_p"], 1)
                along("x3_turned")
                pe.wait_ge(sem["pt3"], at(g, "pt3", 1))
                pe.wait_ge(sem["x3v"], at(g, "x3v", 1))
                for p in range(PAIRS):
                    last = mm(R[2][:, p * C:(p + 1) * C], pT3[:, p, :], v3[:, p, :], start=True, stop=True)
                last.then_inc(sem["d3_p"], 1)
                along("x3_out")

            def group(g, along):
                layer1(g, along)
                attention(g, 0, along)
                attention(g, 1, along)
                mlp(g, along)
                layer3(g, along)
                along("x3_out")

            for k in range(PIECES):
                l0_piece(0, k)
            pe.wait_ge(ld_w, 64)
            for bank, a, b in ((R[0], "x_k", "x_q"), (R[1], "x_v", "x_o")):
                for o in range(CT):
                    for t in range(CT):
                        last = mm(bank[:, o * C:(o + 1) * C], w(a, t)[:, o * P:(o + 1) * P], w(b, t), start=t == 0, stop=t == CT - 1)
                last.then_inc(fold_p, 1)
            pe.wait_ge(fold, 2)
            with pe.Fori(0, NG - 1) as g:
                group(g, Along(l0_piece, g + 1))
            group(NG - 1, Along(None, None))

        @block.scalar
        def _(act):
            A = nc.scalar.activation
            steps = Steps("act")
            act.wait_ge(ld_const, 16 * N_CONST)
            act.wait_ge(ready, 2)

            def l0_qk(g, n):
                for i, (dst, scale) in enumerate(((q0, 0.125), (q0, 0.125), (k0, 1.0), (k0, 1.0))):
                    act.wait_ge(sem["l0_proj"], at(g, "l0_proj", 6 * n + i + 1))
                    for j in range(2):
                        m = 2 * (i % 2) + j
                        bias = bq8[:, m:m + 1] if i < 2 else col("l0_bk", m)
                        last = A(dst[:, m, :], ring[i % 2][:, j * C:(j + 1) * C], ACT.Identity, bias=bias, scale=scale)
                    last.then_inc(sem[f"ring{i % 2}"], 1)

            def l0_exp(g, n, h):
                u = 8 * n + h
                act.wait_ge(sem["l0_nm"], at(g, "l0_nm", u + 1))
                act.wait_ge(sem["l0_T"], at(g, "l0_T", u - 3))
                for qt in range(2):
                    last = A(p0[:, h % 4, qt, :], ring[h % 2][:, qt * C:(qt + 1) * C], ACT.Exp, bias=nm0[:, h % 2, qt:qt + 1],
                             accum_out=rs0[:, h, qt:qt + 1])
                last.then_inc(sem[f"ring{h % 2}"], 1)

            def norm_out(g, k, dst, scale, bias):
                act.wait_ge(sem["ln_T"], at(g, "ln_T", k))
                for t in range(CT):
                    last = A(dst(t), R[0][:, t * TOK:(t + 1) * TOK].rearrange("p (b l) -> p b l", l=L), ACT.Identity,
                             bias=col(bias, t), scale=col(scale, t))
                last.then_inc(sem["ln_out"], 1)

            def copy(dst, src, name):
                A(dst, src, ACT.Copy).then_inc(sem[name], 1)

            def flat(t):
                return t[:].rearrange("p a b -> p (a b)")

            def hT_out(t):
                return hT[:, t, :].rearrange("p (b l) -> p b l", l=L)

            def xs_out(t):
                return xs[:, t, :, 1:L + 1]

            def l0_piece(g, k):
                for what, n, i in PIECE_STEPS[k]:
                    if what == "project":
                        l0_qk(g, n)
                    elif what == "head" and i < H0:
                        l0_exp(g, n, i)
                    elif what == "sum":
                        act.wait_ge(sem["l0_AV"], at(g, "l0_AV", (n + 1) * H0 // 2))
                        act.wait_ge(sem["l0_out"], at(g, "l0_out", n))
                        copy(y0[:], yp[:, 0:C], "l0_y")

            def layer1(g, along):
                act.wait_ge(sem["ctx_tr"], at(g, "ctx_tr", 1))
                copy(flat(ctxT), R[1][:], "ctxT")
                along("ctx_turn")
                norm_out(g, 1, xs_out, "ln1_w", "ln1_b")
                along("ln1_turn")
                act.wait_ge(sem["maa_p"], at(g, "maa_p", 1))
                A(tT[:], R[0][:, 0:TOK], ACT.Tanh)
                A(tg[0:DM, :], R[0][0:DM, TOK:2 * TOK], ACT.Tanh).then_inc(sem["maa_t"], 1)
                along("token_mix_in")
                along("token_mix")
                act.wait_ge(sem["dech_p"], at(g, "dech_p", 1))
                A(hd[0:DD, :], R[2][0:DD, 0:TOK], ACT.Tanh).then_inc(sem["dech"], 1)
                along("decay_in")
                act.wait_ge(sem["rkv_p"], at(g, "rkv_p", 1))
                copy(flat(kT), R[0][:], "rkv")
                along("keys")
                act.wait_ge(sem["decw_p"], at(g, "decw_p", 1))
                for t in range(CT):
                    last = A(e1[:, t, :], R[3][:, t * TOK:(t + 1) * TOK], ACT.Exp, bias=col("time_decay", t))
                last.then_inc(act_step, 1)
                act.wait_ge(act_step, steps.next())
                for t in range(CT):
                    last = A(wsh[:, t, :, 1:L], e1[:, t, :].rearrange("p (b l) -> p b l", l=L)[:, :, 0:L - 1], ACT.Exp, scale=-1.0)
                last.then_inc(sem["decw"], 1)
                act.wait_ge(sem["rkv_p"], at(g, "rkv_p", 2))
                copy(flat(vT), R[1][:], "rkv")
                along("values")
                act.wait_ge(sem["rkv_p"], at(g, "rkv_p", 3))
                copy(flat(rT), R[2][:], "rkv")
                along("receptance")
                act.wait_ge(sem["rkv_p"], at(g, "rkv_p", 4))
                A(flat(sg), R[3][:], ACT.Tanh, scale=0.5).then_inc(sem["eg"], 1)
                along("gather1")
                act.wait_ge(sem["gd"], at(g, "gd", 1))
                A(flat(gq), flat(yc), ACT.Square).then_inc(sem["gsq"], 1)
                along("gn_mean")
                act.wait_ge(sem["gve"], at(g, "gve", 1))
                A(flat(gq), flat(gq), ACT.Sqrt).then_inc(sem["grs"], 1)
                along("gn_var")
                along("wkv_out")
                norm_out(g, 2, xs_out, "ln2_w", "ln2_b")
                along("ln2_turn")
                act.wait_ge(sem["frelu"], at(g, "frelu", 1))
                A(mix[:, 2], mix[:, 3], ACT.Square).then_inc(sem["fkk"], 1)
                act.wait_ge(sem["fr_p"], at(g, "fr_p", 1))
                A(flat(e1), R[1][:], ACT.Tanh, scale=0.5).then_inc(sem["fe"], 1)
                along("channel_mix_in")

            def attention(g, a, along):
                at_point = ("self_", "cross_")[a]
                along(("channel_mix", "self_out")[a])
                norm_out(g, 3 + a, hT_out, ("sa_s", "ca_s")[a], ("sa_b", "ca_b")[a])
                along(at_point + "turn")
                act.wait_ge(sem["qkv_p"], at(g, "qkv_p", 3 * a + 3))
                for t in range(CT):
                    last = A(sx[:, t, :], R[0][:, t * TOK:(t + 1) * TOK], ACT.Identity, bias=col(("sa_bq", "ca_bq")[a], t))
                last.then_inc(sem["q_T"], 1)
                along(at_point + "qkv")
                along(at_point + "scores_a")
                for r4 in range(4):
                    if r4 == 2:
                        along(at_point + "scores")
                    act.wait_ge(sem["sub"], at(g, "sub", 4 * a + r4 + 1))
                    pf = pb[:, r4].rearrange("p a b -> p (a b)")
                    A(pf, pf, ACT.Exp).then_inc(sem["pexp"], 1)
                for r4 in (0, 2):
                    if r4 == 0:
                        along(at_point + "softmax")
                    act.wait_ge(sem["pt_p"], at(g, "pt_p", 4 * a + r4 + 1))
                    copy(ptb[:, r4].rearrange("p a b -> p (a b)"), R[r4][:], "pt_a")
                    along(at_point + ("turned_a" if r4 == 0 else "turned"))
                along(at_point + "values")
                act.wait_ge(sem["cxT_p"], at(g, "cxT_p", a + 1))
                copy(flat(cT), R[2][:], "cxT")
                along(at_point + "ctx_turn")

            def mlp(g, along):
                along("cross_out")
                norm_out(g, 5, hT_out, "ml_s", "ml_b")
                along("mlp_turn")
                for c in range(5):
                    if c in (2, 4):
                        along(("mlp_in_a", "mlp_in")[c // 2 - 1])
                    if c < 4:
                        act.wait_ge(sem["u"], at(g, "u", c + 1))
                        A(tb[:, 2 * c:2 * c + 2, :], ub[:, 2 * c:2 * c + 2, :], ACT.Square).then_inc(sem["usq"], 1)
                    if c >= 1:
                        act.wait_ge(sem["utu"], at(g, "utu", c))
                        A(tb[:, 2 * c - 2:2 * c, :], tb[:, 2 * c - 2:2 * c, :], ACT.Tanh, scale=0.7978845608028654).then_inc(sem["uth"], 1)

            def layer3(g, along):
                along("mlp_out")
                act.wait_ge(sem["ln_T"], at(g, "ln_T", 6))
                copy(flat(hT), R[0][:], "ln_out")
                along("x3_turn")
                act.wait_ge(sem["nm3"], at(g, "nm3", 1))
                for p in range(PAIRS):
                    for b2 in range(2):
                        r = slice(L * b2, L * b2 + L)
                        last = A(p3[r, p, L * b2:L * b2 + L], R[0][r, p * P + L * b2:p * P + L * b2 + L], ACT.Exp,
                                 bias=nm3[r, p:p + 1], scale=0.0625, accum_out=sm3[r, p:p + 1])
                last.then_inc(sem["e3"], 1)
                along("x3_scores")
                act.wait_ge(sem["pt3_p"], at(g, "pt3_p", 1))
                copy(flat(pT3), R[1][:, 0:PAIRS * P], "pt3")
                along("x3_turned")

            def group(g, along):
                steps.start(g)
                layer1(g, along)
                attention(g, 0, along)
                attention(g, 1, along)
                mlp(g, along)
                layer3(g, along)
                along("x3_out")
                steps.end()

            for k in range(PIECES):
                l0_piece(0, k)
            with act.Fori(0, NG - 1) as g:
                group(g, Along(l0_piece, g + 1))
            group(NG - 1, Along(None, None))

        @block.gpsimd
        def _(pool):
            GT = nc.gpsimd.tensor_tensor
            pool.memset(nhalf[:], -0.5)
            pool.memset(none[:], -1.0)
            pool.memset(wsh[:, :, :, 0:1], 0.0)
            pool.memset(p3[:], 0.0).then_inc(ready_pool, 1)
            pool.wait_ge(ready_pool, 1)

            pool_steps = Steps("pool")

            def l0_scale(g, n, h):
                u = RING_USES * n + 6 + h
                pool.wait_ge(sem[f"ring{u % 2}"], at(g, f"ring{u % 2}", u // 2 + 1))
                GT(rs0[:, h], rs0[:, h], none[:], ALU.pow).then_inc(pool_step, 1)
                pool.wait_ge(pool_step, pool_steps.next())
                GT(p0[:, h % 4], p0[:, h % 4], rs0[:, h].unsqueeze(2).to_broadcast([P, 2, C]), ALU.mult).then_inc(sem["l0_P"], 1)

            def l0_piece(g, k):
                if k == 0:
                    pool_steps.start(g)
                for what, n, i in PIECE_STEPS[k]:
                    if what == "norm" and n == 4:
                        pool.wait_ge(sem["l0_var"], at(g, "l0_var", 1))
                        GT(st0[:, :, 10], st0[:, :, 9], nhalf[:, 0:PAIRS], ALU.pow).then_inc(sem["l0_rstd"], 1)
                    elif what == "head" and i < H0:
                        l0_scale(g, n, i)
                if k == PIECES - 1:
                    pool_steps.end()

            def norm(g, k):
                pool.wait_ge(sem["ln_var"], at(g, "ln_var", k))
                GT(rstd[:], ve[:], nhalf[:, 0:PAIRS], ALU.pow).then_inc(sem["ln_rstd"], 1)

            def layer1(g, along):
                norm(g, 1)
                along("token_mix_in")
                xa = xs[:].rearrange("p t b l -> p (t b) l")[:, :, 1:L + 1]
                for f in range(5):
                    pool.wait_ge(sem["mix_tmp"], at(g, "mix_tmp", f + 1))
                    m = mix[:, f].rearrange("p t (b l) -> p (t b) l", l=L)
                    GT(m, m, xa, ALU.add).then_inc(sem["mix_x"], 1)
                    if f == 3:
                        along("token_mix")
                for t in range(CT):
                    for j in range(4):
                        along(f"spread{min(4 * t + j + 1, 7)}")
                        pool.wait_ge(sem["wkv_s"], at(g, "wkv_s", 8 * t + 2 * j + 2))
                        a2 = av[:, t, 2 * j:2 * j + 2].rearrange("p s b l -> p s (b l)")
                        GT(a2, a2, rT[:, t:t + 1, :].to_broadcast([P, 2, TOK]), ALU.mult).then_inc(sem["wkv_p"], 1)
                along("gn_out")
                norm(g, 2)

            def attention(g, a, along):
                at_point = ("self_", "cross_")[a]
                along(("channel_mix_in", "self_ctx_turn")[a])
                norm(g, 3 + a)
                along(at_point + "qkv")
                for r4 in range(4):
                    if r4 == 2:
                        along(at_point + "scores_a")
                    pool.wait_ge(sem["mskd"], at(g, "mskd", 4 * a + r4 + 1))
                    if a == 0:
                        GT(pb[:, r4], pb[:, r4], selfb[:].unsqueeze(1).to_broadcast([P, 8, L]), ALU.add).then_inc(sem["mbias"], 1)
                    else:
                        s = pb[:, r4].rearrange("p (r h) k -> p r h k", r=PAIRS)
                        GT(s, s, crossb[:].unsqueeze(2).to_broadcast([P, PAIRS, 4, L]), ALU.add).then_inc(sem["mbias"], 1)

            def mlp(g, along):
                along("cross_ctx_turn")
                norm(g, 5)
                along("mlp_turn")
                for c in range(4):
                    if c in (1, 3):
                        along(("mlp_in_a", "mlp_in")[c // 2])
                    pool.wait_ge(sem["ut"], at(g, "ut", c + 1))
                    s = slice(2 * c, 2 * c + 2)
                    GT(tb[:, s, :], tb[:, s, :], ub[:, s, :], ALU.mult).then_inc(sem["utu"], 1)

            def group(g, along):
                layer1(g, along)
                attention(g, 0, along)
                attention(g, 1, along)
                mlp(g, along)
                along("x3_out")

            for k in range(PIECES):
                l0_piece(0, k)
            with pool.Fori(0, NG - 1) as g:
                group(g, Along(l0_piece, g + 1))
            group(NG - 1, Along(None, None))

        @block.vector
        def _(dve):
            V = nc.vector
            for name, per in PER.items():
                dve.sem_inc(sem[name], per)
            dve.sem_inc(st_out, 16)
            dve.wait_ge(ld_const, 16 * N_CONST)
            V.memset(uv[:], 0.0)
            V.tensor_copy(bvb, cols[:, COLS["l0_bv"][0]:COLS["l0_bv"][0] + 4].unsqueeze(2).to_broadcast([P, 4, P]))
            V.memset(vbd[:], 0.0)
            V.tensor_scalar(selfb[:], selfm[:], 10000.0, -10000.0, ALU.mult, ALU.add).then_inc(ready, 1)
            dve.wait_ge(ready, 1)
            V.memset(vbd[0:L, :, :, 0, D2:KV], 1.0)
            V.memset(vbd[L:P, :, :, 1, D2:KV], 1.0)
            V.tensor_scalar(selfm[:], selfm[:], 0.25, None, ALU.mult)
            V.tensor_scalar(bq8[:], cols[:, COLS["l0_bq"][0]:COLS["l0_bq"][0] + 4], 0.125, None, ALU.mult).then_inc(ready, 1)
            dve.wait_ge(ready, 2)
            dve.wait_ge(ready_pool, 1)
            dve.wait_ge(fold_p, 1)
            for h in range(H0):
                s = slice(h * D0, (h + 1) * D0)
                for b2 in range(2):
                    V.tensor_copy(uv[L * b2:L * b2 + L, b2, s], R[h % 2][L * b2:L * b2 + L, s])
            dve.wait_ge(fold_p, 2)
            for h in range(H0):
                s = slice(h * D0, (h + 1) * D0)
                last = V.tensor_copy(bvo[:, s], R[2 + h % 2][:, s])
            last.then_inc(fold, 1)
            l0_steps = Steps("vec_l0")
            steps = Steps("vec")

            def flat(t):
                return t[:].rearrange("p a b -> p (a b)")

            def l0_norm(g, part):
                if part == 0:
                    for p in range(PAIRS):
                        dve.wait_ge(ld_pair[p], g * 32 + 32)
                        last = V.bn_stats(st0[:, p, 0:6], x_t[:, p, :])
                    last.then_inc(vec_l0_step, 1)
                    dve.wait_ge(vec_l0_step, l0_steps.next())
                    V.memset(st0[:, 0, 15:16], 0.0)
                    for p in range(PAIRS):
                        last = V.bn_aggr(st0[:, p, 6:8], st0[:, p, 0:6])
                    last.then_inc(sem["l0_stat"], 1)
                elif part == 2:
                    dve.wait_ge(sem["l0_mean"], at(g, "l0_mean", 1))
                    V.tensor_copy(st0[:, :, 11], yp[:, C:C + PAIRS])
                    V.tensor_tensor(st0[:, :, 8], st0[:, :, 6], yp[:, C:C + PAIRS], ALU.subtract).then_inc(vec_l0_step, 1)
                    dve.wait_ge(vec_l0_step, l0_steps.next())
                    V.tensor_tensor(st0[:, :, 9], st0[:, :, 8], st0[:, :, 8], ALU.mult).then_inc(vec_l0_step, 1)
                    dve.wait_ge(vec_l0_step, l0_steps.next())
                    V.tensor_tensor(st0[:, :, 7], st0[:, :, 7], st0[:, :, 9], ALU.add).then_inc(sem["l0_stat"], 1)
                elif part == 4:
                    dve.wait_ge(sem["l0_mean"], at(g, "l0_mean", 2))
                    V.tensor_scalar(st0[:, :, 9], yp[:, C + PAIRS:C + 2 * PAIRS], EPS, None, ALU.add).then_inc(sem["l0_var"], 1)
                elif part == 5:
                    dve.wait_ge(sem["l0_rstd"], at(g, "l0_rstd", 1))
                    V.tensor_scalar(st0[:, :, 10], st0[:, :, 10], col("l0_gamma"), None, ALU.mult).then_inc(vec_l0_step, 1)
                    dve.wait_ge(vec_l0_step, l0_steps.next())
                    for p in range(PAIRS):
                        last = V.tensor_scalar(xn[:, p, :], x_t[:, p, :], st0[:, p, 11:12], st0[:, p, 10:11], ALU.subtract, ALU.mult)
                    last.then_inc(vec_l0_step, 1)
                    dve.wait_ge(vec_l0_step, l0_steps.next())
                    V.tensor_scalar(flat(xn), flat(xn), col("l0_beta"), None, ALU.add).then_inc(sem["l0_xn"], 1)

            def l0_v(g, n):
                dve.wait_ge(sem["l0_AV"], at(g, "l0_AV", n * H0 // 2))
                for t in range(2):
                    dve.wait_ge(sem["l0_proj"], at(g, "l0_proj", 6 * n + 5 + t))
                    V.tensor_tensor(v0[:, t, :], ring[t][:], bvo[:], ALU.add).then_inc(sem[f"ring{t}"], 1)

            def l0_max(g, n, h):
                dve.wait_ge(sem["l0_S"], at(g, "l0_S", 8 * n + h + 1))
                V.tensor_reduce(nm0[:, h % 2, :], two(ring[h % 2][:]), AX, ALU.max, negate=True).then_inc(sem["l0_nm"], 1)

            def l0_pt(g, n, h):
                dve.wait_ge(sem["l0_T"], at(g, "l0_T", 8 * n + h + 1))
                dve.wait_ge(sem["l0_AV"], at(g, "l0_AV", (8 * n + h) // 2 - 1))
                V.tensor_copy(pt0[:, h % 4], two(ptp[:])).then_inc(sem["l0_pt"], 1)

            def l0_x1(g, p):
                dve.wait_ge(sem["l0_out"], at(g, "l0_out", 2 * p + 2))
                V.scalar_tensor_tensor(x1[:, p, :], yp[:, C:2 * C], col("l0_bo"), x_t[:, p, :], ALU.add, ALU.add).then_inc(sem["l0_x1"], 1)

            def l0_piece(g, k):
                if k == 0:
                    l0_steps.start(g)
                for what, n, i in PIECE_STEPS[k]:
                    if what == "norm":
                        l0_norm(g, n)
                    elif what == "project":
                        l0_v(g, n)
                    elif what == "output" and n % 2 == 1:
                        l0_x1(g, n // 2)
                    elif what == "head":
                        if i < H0:
                            l0_max(g, n, i)
                        if 2 <= i < H0 + 2:
                            l0_pt(g, n, i - 2)
                if k == PIECES - 1:
                    l0_steps.end()

            def norm(g, k):
                for p in range(PAIRS):
                    last = V.bn_stats(bst[:, p, :], xr[:, p, :])
                last.then_inc(vec_step, 1)
                dve.wait_ge(vec_step, steps.next())
                V.memset(st0[:, 0, 15:16], 0.0)
                for p in range(PAIRS):
                    last = V.bn_aggr(mv[:, p, :], bst[:, p, :])
                last.then_inc(vec_step, 1)
                dve.wait_ge(vec_step, steps.next())
                V.tensor_scalar(ve[:], mv[:, :, 1], EPS, None, ALU.add).then_inc(sem["ln_var"], 1)
                dve.wait_ge(sem["ln_rstd"], at(g, "ln_rstd", k))
                for p in range(PAIRS):
                    last = V.tensor_scalar(xh[:, p, :], xr[:, p, :], mv[:, p, 0:1], rstd[:, p:p + 1], ALU.subtract, ALU.mult)
                last.then_inc(sem["ln_xh"], 1)

            def shift(g, k, row_of_state):
                dve.wait_ge(sem["ctxT"], at(g, "ctxT", 1))
                V.tensor_copy(xs[:, :, :, 0], ctxT[:].rearrange("p t (b l) -> p t b l", l=L)[:, :, :, row_of_state]).then_inc(vec_step, 1)
                dve.wait_ge(vec_step, steps.next())
                dve.wait_ge(sem["ln_out"], at(g, "ln_out", k))
                xf = xs[:].rearrange("p t b l -> p (t b) l")
                V.tensor_tensor(sx[:].rearrange("p t (b l) -> p (t b) l", l=L), xf[:, :, 0:L], xf[:, :, 1:L + 1], ALU.subtract).then_inc(vec_step, 1)
                dve.wait_ge(vec_step, steps.next())

            def bl(ap):
                return ap.rearrange("p (b l) -> p b l", l=L)

            def lerp(dst, name):
                for t in range(CT):
                    last = V.scalar_tensor_tensor(bl(dst[:, t, :]), bl(sx[:, t, :]), col(name, t), xs[:, t, :, 1:L + 1], ALU.mult, ALU.add)
                return last

            def layer1(g, along):
                dve.wait_ge(sem["xo"], at(g, "xo", 0))
                dve.wait_ge(sem["l0_x1"], at(g, "l0_x1", PAIRS))
                V.tensor_copy(flat(xr), flat(x1)).then_inc(vec_step, 1)
                dve.wait_ge(vec_step, steps.next())
                norm(g, 1)
                along("ctx_turn")
                shift(g, 1, 1)
                lerp(xx, "maa_x").then_inc(sem["xxx"], 1)
                along("token_mix_in")
                for f, name in enumerate(("maa_w", "maa_k", "maa_v", "maa_r", "maa_g")):
                    dve.wait_ge(sem["mix_p"], at(g, "mix_p", f + 1))
                    for t in range(CT):
                        last = V.scalar_tensor_tensor(mix[:, f, t, :], R[(f + 1) % 4][:, t * TOK:(t + 1) * TOK], col(name, t), sx[:, t, :], ALU.add, ALU.mult)
                    last.then_inc(sem["mix_tmp"], 1)
                    if f == 3:
                        along("token_mix")
                along("values")
                dve.wait_ge(sem["rkv"], at(g, "rkv", 3))
                for t in range(CT):
                    last = V.scalar_tensor_tensor(yc[:, t, :], rT[:, t, :], col("faaaa", t), kT[:, t, :], ALU.mult, ALU.mult)
                last.then_inc(sem["ruk"], 1)
                dve.wait_ge(ld_s0, g * 64 + 64)
                for t in range(CT):
                    last = V.tensor_copy(av[:, t, :, :, 0], s0t[:, :, t, :].rearrange("p b s -> p s b"))
                last.then_inc(vec_step, 1)
                dve.wait_ge(vec_step, steps.next())

                along("receptance")
                dve.wait_ge(sem["ruk_p"], at(g, "ruk_p", 1))
                V.tensor_tensor(flat(ybon), R[0][:], flat(vT), ALU.mult).then_inc(sem["bonus"], 1)
                dve.wait_ge(sem["eg"], at(g, "eg", 1))
                V.tensor_scalar(flat(sg), flat(sg), 0.5, 0.5, ALU.mult, ALU.add).then_inc(vec_step, 1)
                dve.wait_ge(vec_step, steps.next())
                V.tensor_tensor(flat(sg), R[3][:], flat(sg), ALU.mult).then_inc(sem["silu"], 1)

                along("gate")
                
                def outer(t, j):
                    dve.wait_ge(sem["spread_p"], at(g, "spread_p", 4 * t + j + 1))
                    k = 4 * t + j
                    vb = R[1 + k % 2][:].rearrange("p (s b l) -> p s b l", s=2, l=L)[:, :, :, 0:L - 1]
                    kk = bl(kT[:, t, :]).unsqueeze(1).to_broadcast([P, 2, G, L])[:, :, :, 0:L - 1]
                    V.tensor_tensor(av[:, t, 2 * j:2 * j + 2, :, 1:L], vb, kk, ALU.mult).then_inc(sem["wkv_a"], 1)

                def scans(t, j):
                    dve.wait_ge(sem["wkv_a"], at(g, "wkv_a", 4 * t + j + 1))
                    for i in range(2):
                        s = av[:, t, 2 * j + i].rearrange("p b l -> p (b l)")
                        V.tensor_tensor_scan(s, wsh[:, t].rearrange("p b l -> p (b l)"), s, 0.0, ALU.mult, ALU.add).then_inc(sem["wkv_s"], 1)

                dve.wait_ge(sem["decw"], at(g, "decw", 1))
                outer(0, 0)
                outer(0, 1)
                along("spread1")
                for k in range(8):
                    scans(k // 4, k % 4)
                    if k + 2 < 8:
                        outer((k + 2) // 4, (k + 2) % 4)
                        along(f"spread{k + 2}")
                dve.wait_ge(sem["bonus"], at(g, "bonus", 1))
                for t in range(CT):
                    dve.wait_ge(sem["wkv_yp"], at(g, "wkv_yp", t + 1))
                    V.tensor_tensor(yc[:, t, :], R[3][:, t * TOK:(t + 1) * TOK], ybon[:, t, :], ALU.add).then_inc(sem["wkv_y"], 1)
                    along(f"gather{t}")
                dve.wait_ge(sem["gm_p"], at(g, "gm_p", 1))
                V.tensor_tensor(flat(yc), flat(yc), R[0][:], ALU.subtract).then_inc(sem["gd"], 1)
                along("gn_mean")
                dve.wait_ge(sem["gv_p"], at(g, "gv_p", 1))
                V.tensor_scalar(flat(gq), R[1][:], EPS, None, ALU.add).then_inc(sem["gve"], 1)
                along("gn_var")
                dve.wait_ge(sem["grs"], at(g, "grs", 1))
                V.reciprocal(flat(gq), flat(gq)).then_inc(vec_step, 1)
                dve.wait_ge(vec_step, steps.next())
                dve.wait_ge(sem["silu"], at(g, "silu", 1))
                for t in range(CT):
                    last = V.scalar_tensor_tensor(yc[:, t, :], yc[:, t, :], col("gn_w", t), gq[:, t, :], ALU.mult, ALU.mult)
                last.then_inc(vec_step, 1)
                dve.wait_ge(vec_step, steps.next())
                for t in range(CT):
                    last = V.scalar_tensor_tensor(yc[:, t, :], yc[:, t, :], col("gn_b", t), sg[:, t, :], ALU.add, ALU.mult)
                last.then_inc(sem["yg"], 1)
                along("gn_out")
                dve.wait_ge(sem["wo_p"], at(g, "wo_p", 1))
                V.tensor_tensor(flat(xr), R[2][:], flat(xr), ALU.add).then_inc(sem["x2"], 1)
                dve.wait_ge(sem["x2"], at(g, "x2", 1))
                norm(g, 2)
                along("wkv_out")
                shift(g, 2, 0)
                lerp(mix[:, 0], "fmaa_k")
                lerp(mix[:, 1], "fmaa_r").then_inc(sem["ffn_in"], 1)
                along("ln2_turn")
                dve.wait_ge(sem["fk_p"], at(g, "fk_p", 1))
                V.tensor_scalar(mix[:, 3].rearrange("p a b -> p (a b)"), R[0][:], 0.0, None, ALU.max).then_inc(sem["frelu"], 1)
                dve.wait_ge(sem["fe"], at(g, "fe", 1))
                V.tensor_scalar(flat(e1), flat(e1), 0.5, 0.5, ALU.mult, ALU.add).then_inc(vec_step, 1)
                dve.wait_ge(vec_step, steps.next())
                along("channel_mix_in")
                dve.wait_ge(sem["fv_p"], at(g, "fv_p", 1))
                V.tensor_tensor(flat(tmp), R[2][:], flat(e1), ALU.mult).then_inc(vec_step, 1)
                dve.wait_ge(vec_step, steps.next())
                V.tensor_tensor(flat(xr), flat(xr), flat(tmp), ALU.add).then_inc(sem["x3"], 1)
                dve.wait_ge(sem["x3"], at(g, "x3", 1))

            def attention(g, a, along):
                at_point = ("self_", "cross_")[a]
                norm(g, 3 + a)
                along(("channel_mix", "self_out")[a])
                along(at_point + "turn")
                dve.wait_ge(sem["qkv_p"], at(g, "qkv_p", 3 * a + 1))
                for t in range(CT):
                    for e, parity in enumerate(("even_head", "odd_head")):
                        last = V.tensor_scalar(kbd[:, t, e, :], R[1][:, t * TOK:(t + 1) * TOK], col(("sa_bk", "ca_bk")[a], t), col(parity),
                                               ALU.add, ALU.mult)
                last.then_inc(sem["k_bd"], 1)
                dve.wait_ge(sem["qkv_p"], at(g, "qkv_p", 3 * a + 2))
                dve.wait_ge(sem["v_bd"], at(g, "v_bd", a))
                V.tensor_tensor(vsb, two(R[2][:]), row(("sa_bv", "ca_bv")[a]).unsqueeze(1).to_broadcast([P, PAIRS, C]), ALU.add).then_inc(sem["v_sb"], 1)
                along(at_point + "qkv")
                if a == 1:
                    dve.wait_ge(ld_cmask, g * 32 + 32)
                    V.tensor_scalar(crossm[:], cmask[:], 0.25, None, ALU.mult)
                    V.tensor_scalar(crossb[:], cmask[:], 10000.0, -10000.0, ALU.mult, ALU.add).then_inc(sem["cmask"], 1)
                    dve.wait_ge(sem["cmask"], at(g, "cmask", 1))
                for r4 in range(4):
                    dve.wait_ge(sem["s_p"], at(g, "s_p", 4 * a + r4 + 1))
                    if a == 0:
                        last = V.tensor_tensor(pb[:, r4], R[r4][:].rearrange("p (h k) -> p h k", k=L),
                                               selfm[:].unsqueeze(1).to_broadcast([P, 8, L]), ALU.mult)
                    else:
                        last = V.tensor_tensor(pb[:, r4].rearrange("p (r h) k -> p r h k", r=PAIRS), R[r4][:].rearrange("p (r h k) -> p r h k", r=PAIRS, k=L),
                                               crossm[:].unsqueeze(2).to_broadcast([P, PAIRS, 4, L]), ALU.mult)
                    last.then_inc(sem["mskd"], 1)
                    if r4 == 1:
                        along(at_point + "scores_a")
                vh = vsb.rearrange("p r (h e d) -> p r h e d", e=2, d=D2)
                vw = vsw[:].rearrange("p r (h e d) -> p r h e d", e=2, d=D2)
                vo = vbd[:].rearrange("p (r b) h e d -> p r b h e d", b=2)
                V.tensor_copy(vo[0:L, :, 0, :, 0, 0:D2], vh[0:L, :, :, 0, :])
                V.tensor_copy(vo[L:P, :, 1, :, 1, 0:D2], vh[L:P, :, :, 1, :])
                dve.wait_ge(v_swap, g * 64 + 32 * (a + 1))
                V.tensor_copy(vo[0:L, :, 1, :, 0, 0:D2], vw[0:L, :, :, 0, :])
                V.tensor_copy(vo[L:P, :, 0, :, 1, 0:D2], vw[L:P, :, :, 1, :]).then_inc(sem["v_bd"], 1)
                for r4 in range(4):
                    dve.wait_ge(sem["mbias"], at(g, "mbias", 4 * a + r4 + 1))
                    V.tensor_reduce(mx[:, r4, :], pb[:, r4], AX, ALU.max).then_inc(vec_step, 1)
                    dve.wait_ge(vec_step, steps.next())
                    V.tensor_tensor(pb[:, r4], pb[:, r4], mx[:, r4, :].unsqueeze(2).to_broadcast([P, 8, L]), ALU.subtract).then_inc(sem["sub"], 1)
                    if r4 == 1:
                        along(at_point + "scores")
                along(at_point + "softmax")
                for r4 in (1, 3):
                    dve.wait_ge(sem["pt_p"], at(g, "pt_p", 4 * a + r4 + 1))
                    V.tensor_copy(ptb[:, r4].rearrange("p a b -> p (a b)"), R[r4][:]).then_inc(sem["pt_v"], 1)
                    along(at_point + ("turned_a" if r4 == 1 else "turned"))
                for p in range(PAIRS):
                    dve.wait_ge(sem["av_p"], at(g, "av_p", 2 * a + p + 1))
                    y = R[p][:, 0:H2 * KV].rearrange("p (h d) -> p h d", d=KV)
                    V.reciprocal(rc[:, p, :], y[:, :, D2]).then_inc(vec_step, 1)
                    dve.wait_ge(vec_step, steps.next())
                    V.tensor_tensor(cx[:, p, :].rearrange("p (h d) -> p h d", d=D2), y[:, :, 0:D2],
                                        rc[:, p, :].unsqueeze(2).to_broadcast([P, H2, D2]), ALU.mult).then_inc(sem["cx"], 1)
                along(at_point + "ctx_turn")
                dve.wait_ge(sem["ao_p"], at(g, "ao_p", a + 1))
                V.tensor_tensor(tmp[:], two(R[3][:]), row(("sa_bo", "ca_bo")[a]).unsqueeze(1).to_broadcast([P, PAIRS, C]), ALU.add).then_inc(vec_step, 1)
                dve.wait_ge(vec_step, steps.next())
                V.tensor_tensor(flat(xr), flat(xr), flat(tmp), ALU.add).then_inc(sem["ao"], 1)
                dve.wait_ge(sem["ao"], at(g, "ao", a + 1))

            def mlp(g, along):
                norm(g, 5)
                along("mlp_turn")
                for c in range(6):
                    if c < 4:
                        dve.wait_ge(sem["h1_p"], at(g, "h1_p", c + 1))
                        for i in range(2):
                            j = 2 * c + i
                            last = V.tensor_scalar(ub[:, j, :], R[c][:, i * TOK:(i + 1) * TOK], col("b1", j), None, ALU.add)
                        last.then_inc(sem["u"], 1)
                    if 1 <= c < 5:
                        dve.wait_ge(sem["usq"], at(g, "usq", c))
                        s = slice(2 * c - 2, 2 * c)
                        V.tensor_scalar(tb[:, s, :], tb[:, s, :], 0.044715, 1.0, ALU.mult, ALU.add).then_inc(sem["ut"], 1)
                    if c >= 2:
                        dve.wait_ge(sem["uth"], at(g, "uth", c - 1))
                        s = slice(2 * c - 4, 2 * c - 2)
                        V.scalar_tensor_tensor(tb[:, s, :], tb[:, s, :], 1.0, ub[:, s, :], ALU.add, ALU.mult).then_inc(sem["ug"], 1)
                    if c in (1, 3):
                        along(("mlp_in_a", "mlp_in")[c // 2])
                along("gelu")
                dve.wait_ge(sem["w2_p"], at(g, "w2_p", 1))
                for p in range(PAIRS):
                    last = V.scalar_tensor_tensor(tmp[:, p, :], R[p][:, 0:C], 0.5, row("b2"), ALU.mult, ALU.add)
                last.then_inc(vec_step, 1)
                dve.wait_ge(vec_step, steps.next())
                V.tensor_tensor(flat(xr), flat(xr), flat(tmp), ALU.add).then_inc(sem["x5"], 1)

            def layer3(g, along):
                along("mlp_out")
                dve.wait_ge(sem["x3kv_p"], at(g, "x3kv_p", 1))
                V.tensor_copy(kbd[:, 0].rearrange("p a b -> p (a b)"), R[2][:]).then_inc(sem["x3k"], 1)
                dve.wait_ge(sem["x3kv_p"], at(g, "x3kv_p", 2))
                V.tensor_copy(v3[:].rearrange("p a b -> p (a b)"), R[3][:]).then_inc(sem["x3v"], 1)
                along("x3_turn")
                dve.wait_ge(sem["s3_p"], at(g, "s3_p", 1))
                for b2 in range(2):
                    r = slice(L * b2, L * b2 + L)
                    last = V.tensor_reduce(nm3[r, :], R[0][r, 0:PAIRS * P].rearrange("p (r e k) -> p r e k", r=PAIRS, k=L)[:, :, b2, :], AX, ALU.max, negate=True)
                last.then_inc(vec_step, 1)
                dve.wait_ge(vec_step, steps.next())
                V.tensor_scalar(nm3[:], nm3[:], 0.0625, None, ALU.mult).then_inc(sem["nm3"], 1)
                dve.wait_ge(sem["e3"], at(g, "e3", 1))
                V.reciprocal(rc3[:], sm3[:]).then_inc(vec_step, 1)
                dve.wait_ge(vec_step, steps.next())
                for p in range(PAIRS):
                    last = V.tensor_scalar(p3[:, p, :], p3[:, p, :], rc3[:, p:p + 1], None, ALU.mult)
                last.then_inc(sem["pn3"], 1)
                along("x3_turned")
                dve.wait_ge(sem["d3_p"], at(g, "d3_p", 1))
                dve.wait_ge(st_out, (g + 1) * 16)
                for p in range(PAIRS):
                    last = V.scalar_tensor_tensor(xo[:, p, :], R[2][:, p * C:(p + 1) * C], col("alpha"), xr[:, p, :], ALU.mult, ALU.add)
                last.then_inc(sem["xo"], 1)

            def group(g, along):
                steps.start(g)
                layer1(g, along)
                attention(g, 0, along)
                attention(g, 1, along)
                mlp(g, along)
                layer3(g, along)
                along("x3_out")
                steps.end()

            for k in range(PIECES):
                l0_piece(0, k)
            dve.wait_ge(fold_p, 3)
            V.tensor_copy(w("x_k", 0), R[0][:, 0:C])
            V.tensor_copy(w("x_k", 1), R[0][:, C:2 * C])
            dve.wait_ge(fold_p, 4)
            V.tensor_copy(w("x_v", 0), R[1][:, 0:C])
            V.tensor_copy(w("x_v", 1), R[1][:, C:2 * C]).then_inc(fold, 1)
            with dve.Fori(0, NG - 1) as g:
                group(g, Along(l0_piece, g + 1))
            group(NG - 1, Along(None, None))


def value_order():
    import numpy as np
    return np.concatenate([t * P + np.arange(P).reshape(P // S1, S1).T.ravel() for t in range(CT)])


def constants():
    import numpy as np
    i = np.arange(P)
    eye = np.eye(P, dtype=np.float32)
    mean64 = ((i[:, None] // L) == (i[None, :] // L)).astype(np.float32) / L
    sum8 = ((i[:, None] // S1) == (i[None, :] // S1)).astype(np.float32)
    th = value_order()[:P]
    mean8 = sum8[th][:, th] / S1
    spread = np.stack([(sum8 * ((i[:, None] % S1) == t))[th] for t in range(S1)], 1).astype(np.float32)
    gather = np.stack([np.concatenate([(sum8[:, ::S1] if k == i2 else 0 * sum8[:, ::S1]) for k in range(2)], 1) for i2 in range(2)], 1)
    halves = (i[:, None] % L == np.arange(L)[None, :]).astype(np.float32)
    return dict(ident=eye, mean64=mean64, sum8=sum8[:, th], mean8=mean8, halves=halves,
                spread=spread.reshape(P, -1), gather=gather.reshape(P, -1))


def kernel(**inputs):
    import numpy as np
    import concourse.bacc as bacc
    from concourse import mybir as mb
    from concourse.bass_utils import run_bass_kernel_spmd as run

    a = {k: np.asarray(v) for k, v in inputs.items()}
    l0 = {k[9:]: v for k, v in a.items() if k.startswith("L0_xattn_")}
    l1 = {k[9:]: v for k, v in a.items() if k.startswith("L1_xattn_")}
    l2 = {k[9:]: v for k, v in a.items() if k.startswith("L2_xattn_")}
    l3 = {k[9:]: v for k, v in a.items() if k.startswith("L3_xattn_")}

    def column(v):
        return np.reshape(v, (-1, P)).T

    def twice(v):
        return np.concatenate([v, v], 0)

    half = np.arange(P) // D2 % 2
    col = dict(gn_w=l1["gn_w"][value_order()], gn_b=l1["gn_b"][value_order()], l0_gamma=twice(l0["gamma"]), l0_beta=twice(l0["beta"]), l0_bq=l0["bq"], l0_bk=l0["bkv"][:512], l0_bv=l0["bkv"][512:],
               l0_bo=twice(l0["bo"]), sa_s=l2["ln1_s"], sa_b=l2["ln1_b"], ca_s=l2["ln2_s"], ca_b=l2["ln2_b"],
               ml_s=l2["ln3_s"], ml_b=l2["ln3_b"], sa_bq=l2["b_qkv"][:C], sa_bk=l2["b_qkv"][C:2 * C],
               ca_bq=l2["b_q"], ca_bk=l2["b_kv"][:C], b1=l2["b1"], alpha=np.broadcast_to(l3["alpha"], (P,)),
               even_head=(half == 0).astype(np.float32), odd_head=(half == 1).astype(np.float32))
    cols = np.ascontiguousarray(np.concatenate([column(col[n] if n in col else l1[n]) for n in COLS], 1))
    row = dict(sa_bv=l2["b_qkv"][2 * C:], sa_bo=l2["b_ao"], ca_bv=l2["b_kv"][C:], ca_bo=l2["b_co"], b2=l2["b2"])
    rows = np.ascontiguousarray(np.concatenate([row[n] for n in ROWS])[None])

    def tiles(m):
        return np.reshape(np.transpose(np.reshape(m, (-1, P, m.shape[1])), (1, 0, 2)), (P, -1))

    def padded(m):
        return np.concatenate([m, np.zeros((P - m.shape[0], m.shape[1]), m.dtype)], 0)

    def either(m):
        z = np.zeros_like(m)
        return np.concatenate([np.concatenate([m, z], 0), np.concatenate([z, m], 0)], 1)

    w2 = np.reshape(l1["maa_w2"], (5 * DM, C))
    th = value_order()
    ordered = dict(l1, Wv=l1["Wv"][th], Wg=l1["Wg"][th], Wo=l1["Wo"][:, th])
    mats = dict(l0_q=either(l0["Wq"].T), l0_k=either(l0["Wkv"][:512].T), l0_v=tiles(l0["Wkv"][512:]), l0_o=tiles(l0["Wo"].T),
                maa_w1=tiles(l1["maa_w1"]), maa_w2=w2[:P], maa_w2g=padded(w2[P:]), dec_w1=tiles(l1["decay_w1"]), dec_w2=padded(l1["decay_w2"]),
                **{n: tiles(ordered[n].T) for n in ("Wk", "Wv", "Wr", "Wg", "Wo", "fWk", "fWr", "fWv")},
                sa_q=tiles(l2["w_qkv"][:, :C]), sa_k=tiles(l2["w_qkv"][:, C:2 * C]), sa_v=tiles(l2["w_qkv"][:, 2 * C:]), sa_o=tiles(l2["w_ao"]),
                ca_q=tiles(l2["w_q"]), ca_k=tiles(l2["w_kv"][:, :C]), ca_v=tiles(l2["w_kv"][:, C:]), ca_o=tiles(l2["w_co"]),
                w1=tiles(l2["w1"]), w2=tiles(l2["w2"]),
                x_q=tiles(l3["w_q"]), x_k=tiles(l3["w_k"]), x_v=tiles(l3["w_v"]), x_o=tiles(l3["w_o"].T), **constants())
    wts = np.ascontiguousarray(np.concatenate([mats[n] for n in WTS], 1))

    nc = bacc.Bacc("TRN2", target_bir_lowering=False, num_devices=1)
    arrays, args = {}, []
    for name, v in (("x", a["x"]), ("ctx", a["ctx_2048"]), ("mask_self", a["mask_1x1xSxS2_fc1"]), ("mask_cross", a["mask_Bx1xSxS2_ff1"]),
                    ("cols", cols), ("rows", rows), ("wts", wts)):
        v = np.ascontiguousarray(v)
        arrays[f"in_{name}_dram"] = v
        args.append(nc.dram_tensor(f"in_{name}_dram", v.shape, mb.dt.from_np(v.dtype), kind="ExternalInput").ap())
    args.append(nc.dram_tensor("out_0_dram", (B, L, C), mb.dt.float32, kind="ExternalOutput").ap())
    program(nc, *args)
    r = run(nc, [arrays], core_ids=[0])
    return r.results[0]["out_0_dram"]
```
